# Optimizing a Trainium2 kernel written in Bass

```python
import numpy as np
import jax
import jax.numpy as jnp

def _softmax(x, axis=-1):
    return jax.nn.softmax(x, axis=axis)

def _gelu(x):
    return jax.nn.gelu(x, approximate=True)

def _silu(x):
    return jax.nn.silu(x)

def _sigmoid(x):
    return jax.nn.sigmoid(x)

def _layernorm(x, axis=-1, eps=1e-05):
    m = jnp.mean(x, axis=axis, keepdims=True)
    v = jnp.var(x, axis=axis, keepdims=True)
    return (x - m) / jnp.sqrt(v + eps)

def _scatter_add(tgt, idx, src, axis=0):
    return tgt.at[idx].add(src)

def _segment_sum(src, seg, n):
    return jax.ops.segment_sum(src, seg, n)
kernel_name = 'mk_vit_tower_cls_d2_tok_img1024_r4_6c044e'

def setup_inputs(seed: int=0):
    np.random.seed(seed)
    _w = jnp.asarray

    def _rec_inputs():
        import jax
        import jax.numpy as jnp
        _rk = jax.random.key(seed)
        x = -0.000392918 + 0.999932 * jax.random.normal(jax.random.fold_in(_rk, 1), (8, 256, 256, 1), jnp.float32)
        cls_tok = 0.02 * jax.random.normal(jax.random.fold_in(_rk, 5), (1, 1, 256), jnp.float32)
        return (x, cls_tok)
    x, cls_tok = _rec_inputs()

    def _L0_tok_setup():
        import jax, jax.numpy as jnp
        import numpy as np
        INV_SQRT2 = 0.7071067811865476
        LEVEL = 3

        def _split(x, axis):
            ax = axis % x.ndim
            sl0 = [slice(None)] * x.ndim
            sl0[ax] = slice(0, None, 2)
            sl1 = [slice(None)] * x.ndim
            sl1[ax] = slice(1, None, 2)
            x0, x1 = (x[tuple(sl0)], x[tuple(sl1)])
            return ((x0 + x1) * INV_SQRT2, (x0 - x1) * INV_SQRT2)

        def _merge(lo, hi, axis):
            ax = axis % lo.ndim
            e = (lo + hi) * INV_SQRT2
            o = (lo - hi) * INV_SQRT2
            s = jnp.stack([e, o], axis=ax + 1)
            shape = list(lo.shape)
            shape[ax] *= 2
            return s.reshape(shape)

        def _dwt2(x):
            lo, hi = _split(x, -1)
            a, h = _split(lo, -2)
            v, d = _split(hi, -2)
            return (a, h, v, d)

        def _idwt2(a, h, v, d):
            lo = _merge(a, h, -2)
            hi = _merge(v, d, -2)
            return _merge(lo, hi, -1)
        key = jax.random.key(seed)
        ks = jax.random.split(key, 8)
        B, H, W = (16, 256, 256)
        x = jax.random.normal(ks[0], (B, H, W, 1), dtype=jnp.float32)
        na = H // 8 * (W // 8)
        n2 = H // 4 * (W // 4)
        n1 = H // 2 * (W // 2)
        scale = 0.02
        Wa = jax.random.normal(ks[1], (na, 1), dtype=jnp.float32) * scale
        ba = jnp.zeros((1,), jnp.float32)
        Wd1 = jax.random.normal(ks[2], (3 * na, 3), dtype=jnp.float32) * scale
        bd1 = jnp.zeros((3,), jnp.float32)
        Wd2 = jax.random.normal(ks[3], (3 * n2, 3), dtype=jnp.float32) * scale
        bd2 = jnp.zeros((3,), jnp.float32)
        Wd3 = jax.random.normal(ks[4], (3 * n1, 3), dtype=jnp.float32) * scale
        bd3 = jnp.zeros((3,), jnp.float32)
        return {'x': x, 'Wa': Wa, 'ba': ba, 'Wd1': Wd1, 'bd1': bd1, 'Wd2': Wd2, 'bd2': bd2, 'Wd3': Wd3, 'bd3': bd3}
    _L0_tok_all = _L0_tok_setup()
    _L0_tok_in = {k: v for k, v in _L0_tok_all.items() if k in ('Wa', 'ba', 'Wd1', 'bd1', 'Wd2', 'bd2', 'Wd3', 'bd3')}
    del _L0_tok_all

    def _L0_attn_setup():
        import jax, jax.numpy as jnp
        import numpy as np
        import math
        H = 256
        S = 16
        K = 4
        INNER = 2 * H
        BATCH, L = (2, 1024)

        def _linrec_combine(c1, c2):
            a1, b1 = c1
            a2, b2 = c2
            return (a1 * a2, a2 * b1 + b2)
        key = jax.random.key(seed)
        ks = jax.random.split(key, 8)
        x = jax.random.normal(ks[0], (BATCH, L, H), dtype=jnp.float32)
        W_in = jax.random.normal(ks[1], (2 * INNER, H), dtype=jnp.float32) * 0.02
        conv_w = jax.random.normal(ks[2], (INNER, 1, K), dtype=jnp.float32) * 0.1
        conv_b = jnp.zeros((INNER,), dtype=jnp.float32)
        W_x = jax.random.normal(ks[3], (2 * S + INNER, INNER), dtype=jnp.float32) * 0.02
        W_dt = jax.random.normal(ks[4], (INNER, INNER), dtype=jnp.float32) * 0.02
        u = jax.random.uniform(ks[5], (INNER,), dtype=jnp.float32)
        b_dt = jnp.exp(u * (math.log(0.1) - math.log(0.001)) + math.log(0.001))
        A_log = jnp.log(jnp.broadcast_to(jnp.arange(1, S + 1, dtype=jnp.float32), (INNER, S)))
        D = jnp.ones((INNER,), dtype=jnp.float32)
        W_out = jax.random.normal(ks[6], (H, INNER), dtype=jnp.float32) * 0.02
        return {'x': x, 'W_in': W_in, 'conv_w': conv_w, 'conv_b': conv_b, 'W_x': W_x, 'W_dt': W_dt, 'b_dt': b_dt, 'A_log': A_log, 'D': D, 'W_out': W_out}
    _L0_attn_all = _L0_attn_setup()
    _L0_attn_in = {k: v for k, v in _L0_attn_all.items() if k in ('W_in', 'conv_w', 'conv_b', 'W_x', 'W_dt', 'b_dt', 'A_log', 'D', 'W_out')}
    del _L0_attn_all

    def _L0_ffn_setup():
        import jax, jax.numpy as jnp
        import numpy as np
        B, S, M, E, DFF = (4, 512, 256, 8, 1024)
        CAPACITY_FACTOR = 1.25

        def _top1_gate(tokens, wg, capacity):
            gates = jax.nn.softmax(tokens @ wg)
            expert_idx = jnp.argmax(gates, axis=-1)
            mask1 = jax.nn.one_hot(expert_idx, gates.shape[-1], dtype=gates.dtype)
            pos = jnp.sum(jnp.cumsum(mask1, axis=0) * mask1, axis=-1).astype(jnp.int32) - 1
            keep = (pos < capacity).astype(gates.dtype)
            mask1c = mask1 * keep[:, None]
            gates1 = jnp.sum(gates * mask1c, axis=-1)
            loc_oh = jax.nn.one_hot(pos, capacity, dtype=gates.dtype)
            combine = gates1[:, None, None] * mask1c[:, :, None] * loc_oh[:, None, :]
            dispatch = (combine > 0).astype(tokens.dtype)
            return (combine, dispatch)
        key = jax.random.key(seed)
        k = jax.random.split(key, 5)
        x = jax.random.normal(k[0], (B, S, M), dtype=jnp.float32)
        wg = jax.random.normal(k[1], (M, E), dtype=jnp.float32) * 0.02
        w1 = jax.random.normal(k[2], (E, M, DFF), dtype=jnp.float32) * 0.02
        b1 = jnp.zeros((E, DFF), dtype=jnp.float32)
        w2 = jax.random.normal(k[3], (E, DFF, M), dtype=jnp.float32) * 0.02
        b2 = jnp.zeros((E, M), dtype=jnp.float32)
        return {'x': x, 'wg': wg, 'w1': w1, 'b1': b1, 'w2': w2, 'b2': b2}
    _L0_ffn_all = _L0_ffn_setup()
    _L0_ffn_in = {k: v for k, v in _L0_ffn_all.items() if k in ('wg', 'w1', 'b1', 'w2', 'b2')}
    del _L0_ffn_all

    def _L1_attn_setup():
        import jax, jax.numpy as jnp
        import numpy as np
        import math
        HEAD_SIZE = 128

        def rotate_every_two(x):
            x1 = x[..., ::2]
            x2 = x[..., 1::2]
            return jnp.stack((-x2, x1), axis=-1).reshape(x.shape)

        def rope_table(seq_len, dtype=jnp.float32):
            pos = jnp.arange(seq_len, dtype=jnp.float32)
            inv = 10000.0 ** (jnp.arange(0, HEAD_SIZE, 2, dtype=jnp.float32) / HEAD_SIZE)
            radians = pos[:, None] / inv
            sincos = jnp.stack((jnp.sin(radians), jnp.cos(radians)), axis=-1).reshape(seq_len, -1)
            t = jnp.repeat(sincos, 2, axis=-1)
            return t.astype(dtype)
        key = jax.random.key(seed)
        ks = jax.random.split(key, 7)
        B, S, H = (2, 1024, 256)
        sd = 1.0 / math.sqrt(H)
        return {'hidden_states': jax.random.normal(ks[0], (B, S, H), dtype=jnp.float32), 'Wq': jax.random.normal(ks[1], (H, H), dtype=jnp.float32) * sd, 'bq': jax.random.normal(ks[2], (H,), dtype=jnp.float32) * sd, 'Wk': jax.random.normal(ks[3], (H, H), dtype=jnp.float32) * sd, 'bk': jax.random.normal(ks[4], (H,), dtype=jnp.float32) * sd, 'Wv': jax.random.normal(ks[5], (H, H), dtype=jnp.float32) * sd, 'bv': jax.random.normal(ks[6], (H,), dtype=jnp.float32) * sd}
    _L1_attn_all = _L1_attn_setup()
    _L1_attn_in = {k: v for k, v in _L1_attn_all.items() if k in ('Wq', 'bq', 'Wk', 'bk', 'Wv', 'bv')}
    del _L1_attn_all

    def _L1_ffn_setup():
        import jax, jax.numpy as jnp
        import numpy as np
        B, S, H = (1, 512, 256)
        E = 16
        I = 192
        TOPK = 4
        G = 4
        TOPK_G = 2
        SCALE = 2.5
        N_SHARED = 1

        def _route(x, gate_w, gate_bias):
            n = x.shape[0]
            logits = jnp.einsum('nh,eh->ne', x.astype(jnp.float32), gate_w)
            scores = jax.nn.sigmoid(logits)
            sb = scores + gate_bias
            gs = sb.reshape(n, G, E // G)
            group_scores = jnp.sum(jax.lax.top_k(gs, 2)[0], axis=-1)
            _, gidx = jax.lax.top_k(group_scores, TOPK_G)
            gmask = jnp.sum(jax.nn.one_hot(gidx, G, dtype=sb.dtype), axis=1)
            emask = jnp.repeat(gmask, E // G, axis=-1)
            masked = jnp.where(emask > 0, sb, -jnp.inf)
            _, tidx = jax.lax.top_k(masked, TOPK)
            w = jnp.take_along_axis(scores, tidx, axis=1)
            w = w / (jnp.sum(w, axis=-1, keepdims=True) + 1e-20)
            return (tidx, w * SCALE)
        key = jax.random.key(seed)
        ks = jax.random.split(key, 9)

        def rn(k, shape, scale=0.02):
            return jax.random.normal(k, shape, dtype=jnp.float32) * scale
        return dict(hidden_states=jax.random.normal(ks[0], (B, S, H), dtype=jnp.float32), gate_w=rn(ks[1], (E, H)), gate_bias=jax.random.normal(ks[2], (E,), dtype=jnp.float32) * 0.1, w1=rn(ks[3], (E, I, H)), w2=rn(ks[4], (E, H, I)), w3=rn(ks[5], (E, I, H)), ws1=rn(ks[6], (I * N_SHARED, H)), ws2=rn(ks[7], (H, I * N_SHARED)), ws3=rn(ks[8], (I * N_SHARED, H)))
    _L1_ffn_all = _L1_ffn_setup()
    _L1_ffn_in = {k: v for k, v in _L1_ffn_all.items() if k in ('gate_w', 'gate_bias', 'w1', 'w2', 'w3', 'ws1', 'ws2', 'ws3')}
    del _L1_ffn_all
    return {'x': x, 'cls_tok': cls_tok, 'L0_tok_Wa': _L0_tok_in['Wa'], 'L0_tok_ba': _L0_tok_in['ba'], 'L0_tok_Wd1': _L0_tok_in['Wd1'], 'L0_tok_bd1': _L0_tok_in['bd1'], 'L0_tok_Wd2': _L0_tok_in['Wd2'], 'L0_tok_bd2': _L0_tok_in['bd2'], 'L0_tok_Wd3': _L0_tok_in['Wd3'], 'L0_tok_bd3': _L0_tok_in['bd3'], 'L0_attn_W_in': _L0_attn_in['W_in'], 'L0_attn_conv_w': _L0_attn_in['conv_w'], 'L0_attn_conv_b': _L0_attn_in['conv_b'], 'L0_attn_W_x': _L0_attn_in['W_x'], 'L0_attn_W_dt': _L0_attn_in['W_dt'], 'L0_attn_b_dt': _L0_attn_in['b_dt'], 'L0_attn_A_log': _L0_attn_in['A_log'], 'L0_attn_D': _L0_attn_in['D'], 'L0_attn_W_out': _L0_attn_in['W_out'], 'L0_ffn_wg': _L0_ffn_in['wg'], 'L0_ffn_w1': _L0_ffn_in['w1'], 'L0_ffn_b1': _L0_ffn_in['b1'], 'L0_ffn_w2': _L0_ffn_in['w2'], 'L0_ffn_b2': _L0_ffn_in['b2'], 'L1_attn_Wq': _L1_attn_in['Wq'], 'L1_attn_bq': _L1_attn_in['bq'], 'L1_attn_Wk': _L1_attn_in['Wk'], 'L1_attn_bk': _L1_attn_in['bk'], 'L1_attn_Wv': _L1_attn_in['Wv'], 'L1_attn_bv': _L1_attn_in['bv'], 'L1_ffn_gate_w': _L1_ffn_in['gate_w'], 'L1_ffn_gate_bias': _L1_ffn_in['gate_bias'], 'L1_ffn_w1': _L1_ffn_in['w1'], 'L1_ffn_w2': _L1_ffn_in['w2'], 'L1_ffn_w3': _L1_ffn_in['w3'], 'L1_ffn_ws1': _L1_ffn_in['ws1'], 'L1_ffn_ws2': _L1_ffn_in['ws2'], 'L1_ffn_ws3': _L1_ffn_in['ws3']}

def reference(x, cls_tok, L0_tok_Wa, L0_tok_ba, L0_tok_Wd1, L0_tok_bd1, L0_tok_Wd2, L0_tok_bd2, L0_tok_Wd3, L0_tok_bd3, L0_attn_W_in, L0_attn_conv_w, L0_attn_conv_b, L0_attn_W_x, L0_attn_W_dt, L0_attn_b_dt, L0_attn_A_log, L0_attn_D, L0_attn_W_out, L0_ffn_wg, L0_ffn_w1, L0_ffn_b1, L0_ffn_w2, L0_ffn_b2, L1_attn_Wq, L1_attn_bq, L1_attn_Wk, L1_attn_bk, L1_attn_Wv, L1_attn_bv, L1_ffn_gate_w, L1_ffn_gate_bias, L1_ffn_w1, L1_ffn_w2, L1_ffn_w3, L1_ffn_ws1, L1_ffn_ws2, L1_ffn_ws3):
    import jax
    import jax.numpy as jnp

    def _L0_tok_ref(x, Wa, ba, Wd1, bd1, Wd2, bd2, Wd3, bd3):
        import jax, jax.numpy as jnp
        import numpy as np
        INV_SQRT2 = 0.7071067811865476
        LEVEL = 3

        def _split(x, axis):
            ax = axis % x.ndim
            sl0 = [slice(None)] * x.ndim
            sl0[ax] = slice(0, None, 2)
            sl1 = [slice(None)] * x.ndim
            sl1[ax] = slice(1, None, 2)
            x0, x1 = (x[tuple(sl0)], x[tuple(sl1)])
            return ((x0 + x1) * INV_SQRT2, (x0 - x1) * INV_SQRT2)

        def _merge(lo, hi, axis):
            ax = axis % lo.ndim
            e = (lo + hi) * INV_SQRT2
            o = (lo - hi) * INV_SQRT2
            s = jnp.stack([e, o], axis=ax + 1)
            shape = list(lo.shape)
            shape[ax] *= 2
            return s.reshape(shape)

        def _dwt2(x):
            lo, hi = _split(x, -1)
            a, h = _split(lo, -2)
            v, d = _split(hi, -2)
            return (a, h, v, d)

        def _idwt2(a, h, v, d):
            lo = _merge(a, h, -2)
            hi = _merge(v, d, -2)
            return _merge(lo, hi, -1)
        img = x[..., 0]
        B = img.shape[0]
        details = []
        cur = img
        for _ in range(LEVEL):
            cur, h, v, d = _dwt2(cur)
            details.append((h, v, d))
        aw = jax.nn.sigmoid(cur.reshape(B, -1) @ Wa + ba)
        rec = cur * aw[:, :, None]
        det_params = [(Wd1, bd1), (Wd2, bd2), (Wd3, bd3)]
        for (h, v, d), (Wd, bd) in zip(reversed(details), det_params):
            flat = jnp.stack([h, v, d], axis=1).reshape(B, -1)
            w = jax.nn.softmax(flat @ Wd + bd, axis=-1)
            rec = _idwt2(rec, h * w[:, 0, None, None], v * w[:, 1, None, None], d * w[:, 2, None, None])
        return rec

    def _L0_attn_ref(x, W_in, conv_w, conv_b, W_x, W_dt, b_dt, A_log, D, W_out):
        import jax, jax.numpy as jnp
        import numpy as np
        import math
        H = 256
        S = 16
        K = 4
        INNER = 2 * H
        BATCH, L = (2, 1024)

        def _linrec_combine(c1, c2):
            a1, b1 = c1
            a2, b2 = c2
            return (a1 * a2, a2 * b1 + b2)
        xz = jnp.einsum('blh,ih->bli', x, W_in)
        x_proj, z = jnp.split(xz, 2, axis=-1)
        xc = jnp.transpose(x_proj, (0, 2, 1))
        xc = jax.lax.conv_general_dilated(xc, conv_w, window_strides=(1,), padding=[(K - 1, 0)], dimension_numbers=('NCH', 'OIH', 'NCH'), feature_group_count=INNER)
        xc = xc + conv_b[None, :, None]
        x_conv = jax.nn.silu(jnp.transpose(xc, (0, 2, 1)))
        x_ssm = jnp.einsum('bli,oi->blo', x_conv, W_x)
        Bm = x_ssm[..., :S]
        Cm = x_ssm[..., S:2 * S]
        dt_in = x_ssm[..., 2 * S:]
        dt = jax.nn.softplus(jnp.einsum('bli,oi->blo', dt_in, W_dt) + b_dt)
        alpha = jax.nn.sigmoid(dt * 0.1)
        B_gate = jax.nn.sigmoid(jnp.mean(Bm, axis=-1, keepdims=True))
        gated = (1.0 - alpha) * B_gate * x_conv
        alpha_c = jnp.clip(alpha, 0.01, 0.99)
        _, h = jax.lax.associative_scan(_linrec_combine, (alpha_c, gated), axis=1)
        C_gate = jax.nn.sigmoid(jnp.mean(Cm, axis=-1, keepdims=True))
        y = h * C_gate + D * x_conv
        y = y * jax.nn.silu(z)
        out = jnp.einsum('bli,hi->blh', y, W_out)
        return out

    def _L0_ffn_ref(x, wg, w1, b1, w2, b2):
        import jax, jax.numpy as jnp
        import numpy as np
        B, S, M, E, DFF = (4, 512, 256, 8, 1024)
        CAPACITY_FACTOR = 1.25

        def _top1_gate(tokens, wg, capacity):
            gates = jax.nn.softmax(tokens @ wg)
            expert_idx = jnp.argmax(gates, axis=-1)
            mask1 = jax.nn.one_hot(expert_idx, gates.shape[-1], dtype=gates.dtype)
            pos = jnp.sum(jnp.cumsum(mask1, axis=0) * mask1, axis=-1).astype(jnp.int32) - 1
            keep = (pos < capacity).astype(gates.dtype)
            mask1c = mask1 * keep[:, None]
            gates1 = jnp.sum(gates * mask1c, axis=-1)
            loc_oh = jax.nn.one_hot(pos, capacity, dtype=gates.dtype)
            combine = gates1[:, None, None] * mask1c[:, :, None] * loc_oh[:, None, :]
            dispatch = (combine > 0).astype(tokens.dtype)
            return (combine, dispatch)
        d_model = x.shape[-1]
        tokens = x.reshape(-1, d_model)
        T = tokens.shape[0]
        num_experts = wg.shape[1]
        capacity = int(CAPACITY_FACTOR * T / num_experts)
        combine, dispatch = _top1_gate(tokens, wg, capacity)
        dispatched = jnp.einsum('sec,sm->ecm', dispatch, tokens)
        h = jax.nn.relu(jnp.einsum('ecm,emf->ecf', dispatched, w1) + b1[:, None, :])
        expert_out = jnp.einsum('ecf,efm->ecm', h, w2) + b2[:, None, :]
        combined = jnp.einsum('sec,ecm->sm', combine, expert_out)
        return combined.reshape(x.shape)

    def _L1_attn_ref(hidden_states, Wq, bq, Wk, bk, Wv, bv):
        import jax, jax.numpy as jnp
        import numpy as np
        import math
        HEAD_SIZE = 128

        def rotate_every_two(x):
            x1 = x[..., ::2]
            x2 = x[..., 1::2]
            return jnp.stack((-x2, x1), axis=-1).reshape(x.shape)

        def rope_table(seq_len, dtype=jnp.float32):
            pos = jnp.arange(seq_len, dtype=jnp.float32)
            inv = 10000.0 ** (jnp.arange(0, HEAD_SIZE, 2, dtype=jnp.float32) / HEAD_SIZE)
            radians = pos[:, None] / inv
            sincos = jnp.stack((jnp.sin(radians), jnp.cos(radians)), axis=-1).reshape(seq_len, -1)
            t = jnp.repeat(sincos, 2, axis=-1)
            return t.astype(dtype)
        B, S, H = hidden_states.shape
        t = rope_table(S, hidden_states.dtype)
        q = hidden_states @ Wq.T + bq
        k = hidden_states @ Wk.T + bk
        v = hidden_states @ Wv.T + bv
        q = q * t + rotate_every_two(q) * t
        k = k * t + rotate_every_two(k) * t
        scale = math.sqrt(HEAD_SIZE)
        scores = jnp.einsum('bsh,bth->bst', q, k) / scale
        probs = jax.nn.softmax(scores, axis=-1)
        out = jnp.einsum('bst,bth->bsh', probs, v)
        return out

    def _L1_ffn_ref(hidden_states, gate_w, gate_bias, w1, w2, w3, ws1, ws2, ws3):
        import jax, jax.numpy as jnp
        import numpy as np
        B, S, H = (1, 512, 256)
        E = 16
        I = 192
        TOPK = 4
        G = 4
        TOPK_G = 2
        SCALE = 2.5
        N_SHARED = 1

        def _route(x, gate_w, gate_bias):
            n = x.shape[0]
            logits = jnp.einsum('nh,eh->ne', x.astype(jnp.float32), gate_w)
            scores = jax.nn.sigmoid(logits)
            sb = scores + gate_bias
            gs = sb.reshape(n, G, E // G)
            group_scores = jnp.sum(jax.lax.top_k(gs, 2)[0], axis=-1)
            _, gidx = jax.lax.top_k(group_scores, TOPK_G)
            gmask = jnp.sum(jax.nn.one_hot(gidx, G, dtype=sb.dtype), axis=1)
            emask = jnp.repeat(gmask, E // G, axis=-1)
            masked = jnp.where(emask > 0, sb, -jnp.inf)
            _, tidx = jax.lax.top_k(masked, TOPK)
            w = jnp.take_along_axis(scores, tidx, axis=1)
            w = w / (jnp.sum(w, axis=-1, keepdims=True) + 1e-20)
            return (tidx, w * SCALE)
        b, s, h = hidden_states.shape
        x = hidden_states.reshape(-1, h)
        tidx, tw = _route(x, gate_w, gate_bias)
        n = x.shape[0]
        combine = jnp.zeros((n, E), x.dtype).at[jnp.arange(n)[:, None], tidx].add(tw)
        g = jnp.einsum('nh,eih->nei', x, w1)
        u = jnp.einsum('nh,eih->nei', x, w3)
        hact = jax.nn.silu(g) * u * combine[:, :, None]
        y = jnp.einsum('nei,ehi->nh', hact, w2)
        shared = jnp.einsum('ni,hi->nh', jax.nn.silu(x @ ws1.T) * (x @ ws3.T), ws2)
        return (y + shared).reshape(b, s, h)
    h = _L0_tok_ref(x, L0_tok_Wa, L0_tok_ba, L0_tok_Wd1, L0_tok_bd1, L0_tok_Wd2, L0_tok_bd2, L0_tok_Wd3, L0_tok_bd3)
    h = jnp.concatenate([jnp.broadcast_to(cls_tok, (h.shape[0], 1, h.shape[2])), h], axis=1)
    h = h + _L0_attn_ref(_layernorm(h, axis=-1), L0_attn_W_in, L0_attn_conv_w, L0_attn_conv_b, L0_attn_W_x, L0_attn_W_dt, L0_attn_b_dt, L0_attn_A_log, L0_attn_D, L0_attn_W_out)
    h = h + _L0_ffn_ref(_layernorm(h, axis=-1), L0_ffn_wg, L0_ffn_w1, L0_ffn_b1, L0_ffn_w2, L0_ffn_b2)
    h = h + _L1_attn_ref(_layernorm(h, axis=-1), L1_attn_Wq, L1_attn_bq, L1_attn_Wk, L1_attn_bk, L1_attn_Wv, L1_attn_bv)
    h = h + _L1_ffn_ref(_layernorm(h, axis=-1), L1_ffn_gate_w, L1_ffn_gate_bias, L1_ffn_w1, L1_ffn_w2, L1_ffn_w3, L1_ffn_ws1, L1_ffn_ws2, L1_ffn_ws3)
    return h

_drawn_inputs = setup_inputs


def setup_inputs(seed=0):
    import zlib

    import numpy as np

    out = dict(_drawn_inputs(seed))
    spreads = {'L0_tok_bd1': (0.0, 0.364),
     'L0_tok_bd2': (0.0, 0.443),
     'L0_tok_bd3': (0.0, 0.488),
     'L0_attn_conv_b': (0.0, 0.378),
     'L0_attn_D': (1.0, 0.6),
     'L0_ffn_b1': (0.0, 0.302),
     'L0_ffn_b2': (0.0, 0.1)}
    factors = {'L0_attn_W_in': 2.743,
     'L0_attn_conv_w': 4.834,
     'L0_attn_W_x': 8.0,
     'L0_attn_W_dt': 36.916,
     'L0_attn_b_dt': 64.0,
     'L1_attn_bk': 2.961}
    for name, (base, spread) in spreads.items():
        noise = np.random.default_rng([zlib.crc32(name.encode()), seed]).standard_normal(out[name].shape)
        drawn = base * np.exp(spread * noise) if base else spread * noise
        out[name] = jnp.asarray(drawn.astype(out[name].dtype))
    for name, factor in factors.items():
        out[name] = (out[name] * factor).astype(out[name].dtype)
    return out
```

```python
from contextlib import ExitStack, contextmanager

import numpy as np

import concourse.bass as bass
from concourse import mybir

F32 = mybir.dt.float32
U32 = mybir.dt.uint32
ALU = mybir.AluOpType
ACT = mybir.ActivationFunctionType
AX = mybir.AxisListType
ds = bass.ds

P = 128
IMAGES, SIDE, HID = 8, 256, 256
LEN = SIDE + 1
TOKENS = IMAGES * LEN
HALVES = HID // P
TILES = 3
ROWS = (P, P, 1)
EPS = 1e-5
INNER, STATE, TAPS = 512, 16, 4
CH = INNER // P
EXP0, DFF = 8, 1024
CAP = int(1.25 * TOKENS / EXP0)
CAPP = CAP // 3
EXP1, DFE, TOPK, GROUPS = 16, 192, 4, 4
DK = DFE // 2
HEAD = 128
NT1 = (TOKENS * TOPK + EXP1 * (P - 1)) // P
FAR = 1.0e6
LOW = 1.0e30
T1 = 2 * IMAGES + 1
XR, IDX, LAG = 8, 16, 7
TAB = 4


class Signals:

    def __init__(self, sem):
        self.sem, self.base, self.k = sem, 0, 0

    def on(self, ins):
        ins.then_inc(self.sem, 1)
        self.k += 1
        return self.base + self.k

    def now(self):
        return self.base + self.k

    @contextmanager
    def loop(self, trip, trips, per):
        start = self.base + self.k
        self.base, self.k = start + trip * per, 0
        yield
        assert self.k == per, (self.k, per)
        self.base, self.k = start + trips * per, 0


def staged(eng, first, last, body, signals=()):
    trips = (last - first + 1) // 2
    with ExitStack() as ctx:
        p = ctx.enter_context(eng.Fori(0, trips))
        for s, per in signals:
            ctx.enter_context(s.loop(p, trips, per))
        body(2 * p + first, first % 2)
        body(2 * p + (first + 1), (first + 1) % 2)


def after(eng, sem, value):
    if not isinstance(value, int) or value > 0:
        eng.wait_ge(sem, value)


def constants():
    k = np.arange(P)
    ident = np.eye(P, dtype=np.float32)
    before = (k[:, None] < k[None, :]).astype(np.float32)
    same_image = (k[:, None] // 32 == k[None, :] // 32).astype(np.float32)
    ones = np.ones((P, P), np.float32)
    mats = np.stack([ident, before, same_image, ones], 1)
    pos = np.arange(LEN, dtype=np.float32)
    inv = np.float32(10000.0) ** (np.arange(0, HEAD, 2, dtype=np.float32) / np.float32(HEAD))
    radians = (pos[:, None] / inv).astype(np.float32)
    sincos = np.stack((np.sin(radians), np.cos(radians)), -1).reshape(LEN, -1)
    rope = np.repeat(sincos, 2, axis=-1).astype(np.float32)
    rope = np.ascontiguousarray(rope.T.reshape(HALVES, P, LEN).transpose(1, 0, 2))
    valid = np.ones((P, IMAGES, TILES), np.float32)
    valid[1:, :, 2] = 0
    gate_scale = np.array([1 / 64.] + [1 / 64.] * 3 + [1 / 16.] * 3 + [1 / 4.] * 3, np.float32)
    e0 = np.arange(EXP0, dtype=np.float32)
    e1 = np.arange(EXP1, dtype=np.float32)
    row = np.concatenate([gate_scale, EXP0 - e0, e0 * CAP, EXP1 - e1])
    row = np.broadcast_to(row, (P, row.size))
    token = np.zeros((P, T1))
    for i in range(IMAGES):
        for q in range(2):
            token[:, 2 * i + q] = i * LEN + q * P + k
    token[:IMAGES, T1 - 1] = k[:IMAGES] * LEN + 2 * P
    valid1 = np.ones((P, T1))
    valid1[IMAGES:, T1 - 1] = 0
    bcast = lambda r: np.broadcast_to(np.asarray(r).reshape(-1), (P, np.asarray(r).size))
    g = np.arange(GROUPS)
    misc = np.concatenate([row, valid.reshape(P, -1), np.full((P, 1), EPS), token, valid1,
                           bcast(g[:, None] > g[None, :]), bcast(np.arange(T1) * P), bcast(np.arange(NT1))], 1)
    records = np.zeros((NT1 * P, TAB), np.float32)
    records[:, 1] = FAR
    return {"records": records, "mats": mats, "rope": rope, "misc": np.ascontiguousarray(misc.astype(np.float32))}


PER_MIX, PER_MIX_ACT = 76, 24
PER_ATT, PER_ATT_ACT = 62, 12
M_SCALE, M_FIRST0, M_BASE0, M_FIRST1, M_VALID, M_EPS = 0, 10, 18, 26, 42, 66
M_TOKEN = 67
M_VALID1 = M_TOKEN + T1
M_LOWER = M_VALID1 + T1
M_STEPS = M_LOWER + GROUPS * GROUPS
M_TILE = M_STEPS + T1
M_END = M_TILE + NT1


def build(nc, d, phases=9):
    ctx = ExitStack()
    with ctx:
        def sb(name, shape, dt=F32):
            return ctx.enter_context(nc.sbuf_tensor(name, shape, dt))

        def sem(name):
            return ctx.enter_context(nc.semaphore(name))

        def dram(name, shape, dt=F32):
            return nc.dram_tensor(name, shape, dt, kind="Internal").ap()

        h0_rows = dram("h0_rows", (TOKENS, HID))
        slots0 = dram("slots0", (EXP0 * CAP, HID))
        outs0 = dram("outs0", (EXP0 * CAP, HID))
        n4_rows = dram("n4_rows", (TOKENS, HID))
        table = dram("table", (NT1 * P, TAB))
        outs1 = dram("outs1", (TOPK * TOKENS, HID))

        mats = sb("mats", [P, 4, P])
        ident, before, same_image, ones = (mats[:, k, :] for k in range(4))
        misc = sb("misc_c", [P, M_END])
        big, mid, mix, spare = sb("big", [P, 20480]), sb("mid", [P, 4112]), sb("mix", [P, 10240]), sb("spare", [P, 6144])

        def arena(mem):
            at = [0]

            def part(n, **dims):
                at[0] += n
                assert at[0] <= mem.shape[1], at[0]
                p = mem[:, at[0] - n:at[0]]
                return p.rearrange("p (a b) -> p a b", **dims) if dims else p

            return part

        part = arena(big)

        img = part(2 * 2048).rearrange("p (g r c) -> p g r c", g=2, r=8)
        w_l1 = part(4608).rearrange("p (f j) -> p f j", j=3)
        w_l2 = part(1152).rearrange("p (f j) -> p f j", j=3)
        w_l3 = part(288).rearrange("p (f j) -> p f j", j=3)
        w_a = part(32)
        gbias = part(10)
        sumc = part(1024)
        difc = part(1024)
        A1, A2, A3 = part(512), part(128), part(32)
        B1, B2, B3 = part(1536), part(384), part(96)
        R2, R1 = part(128), part(512)
        A3g = part(32)
        vw = part(512)
        dot_out = part(1536)
        partial = part(20).rearrange("p (g n) -> p g n", g=2)
        gl = part(80).rearrange("p (k n) -> p k n", n=10)
        rec = img
        lnstat = sb("lnstat", [P, 8, 8])
        lnst = sb("lnst", [P, 8, 6])
        normed = part(2048).rearrange("p (r c) -> p r c", r=8)
        cls = part(512)

        nT0 = arena(mid)(HALVES * TOKENS, a=HALVES)
        part = arena(mix)
        w_in = part(HALVES * 2 * INNER, a=HALVES)
        w_dt = part(CH * INNER, a=CH)
        w_xdt = part(CH * INNER, a=CH)
        w_fold = part(CH * INNER, a=CH)
        w_bcr = part(2 * CH * P).rearrange("p (b k m) -> p b k m", b=2, k=CH)
        w_out = part(CH * HID, a=CH)
        w_bc = sb("w_bc", [P, CH, 2 * STATE])
        w_bcs = sb("w_bcs", [P, CH, 2])
        chan = sb("chan", [P, CH, 8])
        part = arena(big)
        conv, xb, soft, dts, al, om, gat, hs = (part(CH * LEN, a=CH) for _ in range(8))
        xconv, zs, es, ys = ([part(CH * LEN, a=CH) for _ in range(2)] for _ in range(4))
        bct = [part(2 * LEN, a=2) for _ in range(2)]
        outT = sb("outT", [P, HALVES, LEN])
        n2T = sb("n2T", [P, HALVES, LEN])
        part = arena(spare)
        rows = part(IMAGES * TILES * HID).rearrange("p (i q c) -> p i q c", i=IMAGES, q=TILES)

        part = arena(mix)
        part(2048)
        w1e, w2e = zip(*[(part(HALVES * DFF, a=HALVES), part(DFF // P * HID, a=DFF // P)) for _ in range(2)])
        part = arena(big)
        b2_rows = part(EXP0 * HID, a=EXP0)
        slot_rows = [part(3 * HID, a=3) for _ in range(2)]
        slotT = [part(HALVES * CAP, a=HALVES) for _ in range(2)]
        hidden = [part(DFF // P * CAP, a=DFF // P) for _ in range(2)]
        expert_rows = [part(3 * HID, a=3) for _ in range(2)]
        r_exp, r_hot, r_cum, r_tmp = (part(IMAGES * TILES * EXP0, a=IMAGES * TILES) for _ in range(4))
        r_one = part(8 * IMAGES * TILES, a=8)
        part = arena(mix)
        w_qkr, w_qk = part(HALVES * 2 * HID, a=HALVES), part(HALVES * 2 * HID, a=HALVES)
        w_v, rope = part(HALVES * HID, a=HALVES), part(HALVES * LEN, a=HALVES)
        bv_rows, qk_bias = part(HID), part(12)
        wg1, ws13, ws2 = part(HALVES * EXP1, a=HALVES), part(HALVES * 2 * DFE, a=HALVES), part(2 * HID, a=2)
        qkT = part(2 * HALVES * LEN, a=2 * HALVES)
        probs, probsT = part(TILES * LEN, a=TILES), part(TILES * LEN, a=TILES)
        soft_c = part(24)
        gated, silu_g = part(TILES * DFE, a=TILES), part(TILES * DFE, a=TILES)
        gatedT = part(2 * LEN, a=2)
        part = arena(mid)
        n3T, n4T = part(HALVES * LEN, a=HALVES), part(HALVES * LEN, a=HALVES)
        vals = [part(TILES * HID, a=TILES) for _ in range(2)]
        turn_src4 = part(TILES * HID, a=TILES)
        logit1 = sb("logit1", [P, T1, EXP1])
        n4T_last = sb("n4T_last", [P, HALVES, IMAGES])
        bias1 = sb("bias1", [P, EXP1])
        part = arena(spare)
        fetched = [part(TILES * HID, a=TILES) for _ in range(2)]
        part = arena(big)
        w13 = part(EXP1 * HALVES * 2 * DFE).rearrange("p (e h n) -> p e h n", e=EXP1, h=HALVES)
        w2s = part(EXP1 * 2 * HID).rearrange("p (e k n) -> p e k n", e=EXP1, k=2)
        part = arena(mix)
        score, biased, left, r1_tmp, sel, place, cumA, cumB = (part(T1 * EXP1, a=T1) for _ in range(8))
        hots = part(TOPK * T1 * EXP1, a=TOPK)
        hots2 = part(TOPK * T1 * EXP1, a=TOPK)
        one_k = part(6 * TOPK * T1, a=6)
        g_all = part(10 * T1 * GROUPS, a=10)
        g_pair = part(2 * T1 * GROUPS * GROUPS, a=2)
        steps_c = part(EXP1 * T1, a=EXP1)
        per_exp = part(6 * EXP1, a=6)
        xg = [part(HID) for _ in range(XR)]
        part = arena(spare)
        tile_cmp = part(NT1 * EXP1, a=NT1)
        record = part(TOPK * T1 * TAB).rearrange("p (k t w) -> p k t w", k=TOPK, t=T1)
        records = part(NT1 * TAB, a=NT1)
        part = arena(mid)
        xT1, gT1 = [part(HALVES * P, a=HALVES) for _ in range(2)], [part(2 * P, a=2) for _ in range(2)]
        sg1, gu1 = [part(DFE) for _ in range(2)], [part(DFE) for _ in range(2)]
        y1 = [part(HID) for _ in range(4)]
        part = arena(mix)
        ysum = [part(TOPK * TILES * HID).rearrange("p (k q c) -> p k q c", k=TOPK, q=TILES) for _ in range(2)]
        slot1 = sb("slot1", [P, TOPK, T1], U32)
        tile_exp = sb("tile_exp", [1, NT1], U32)
        rec_idx = sb("rec_idx", [P, NT1, 2], U32)
        idx_now = [sb(f"idx_now{k}", [P, 2], U32) for k in range(IDX)]
        idx_weight = sb("idx_weight", [P, NT1])
        b1_cols = sb("b1_cols", [P, EXP0, DFF // P])
        scratch_dve, scratch_pool = sb("scratch_dve", [1, 1]), sb("scratch_pool", [1, 3])
        gl7 = sb("gl7", [P, 1])
        gl8 = sb("gl8", [P, 1])
        gate0 = sb("gate0", [P, IMAGES * TILES])
        slot_to = sb("slot_to", [P, IMAGES * TILES], U32)
        slot_from = sb("slot_from", [P, IMAGES * TILES], U32)
        turn_src = sb("turn_src", [P, TILES, HID])
        wg0 = sb("wg0", [P, HALVES, EXP0])
        logit0 = sb("logit0", [P, IMAGES, TILES, EXP0])
        h_all = sb("h_all", [P, IMAGES, TILES, HID])

        bank = [ctx.enter_context(nc.psum_tensor(f"bank{k}", [P, 512], F32)) for k in range(8)]

        ld_const, ld_img, ld_wav, ld_mix = sem("ld_const"), [sem("ld_img0"), sem("ld_img1")], sem("ld_wav"), sem("ld_mix")
        dve_done, act_done, pool_done = sem("dve_done"), sem("act_done"), sem("pool_done")
        dots_ready, sums_ready, logit_ready, exp_ready = sem("dots_ready"), sem("sums_ready"), sem("logit_ready"), sem("exp_ready")
        vgated, vin = sem("vgated"), sem("vin")
        var_ready, rstd_ready = sem("var_ready"), sem("rstd_ready")
        rec_ready, rows_stored = sem("rec_ready"), sem("rows_stored")
        normed_ready, turned, turned_out = sem("normed_ready"), sem("turned"), sem("turned_out")
        fold_done, fold_out, bc_summed, bc_ready = sem("fold_done"), sem("fold_out"), sem("bc_summed"), sem("bc_ready")
        stored = sem("stored")
        x_ready, z_ready, tap_done, conv_done, xconv_ready, zs_done = (sem(n) for n in (
            "x_ready", "z_ready", "tap_done", "conv_done", "xconv_ready", "zs_done"))
        y_ready, out_ready, outT_done, tok_ready, res_done = (sem(n) for n in (
            "y_ready", "out_ready", "outT_done", "tok_ready", "res_done"))
        bcsum_ready, bct_done, dt_ready, xb_done, soft_ready, dt_done, e_done = (sem(n) for n in (
            "bcsum_ready", "bct_done", "dt_ready", "xb_done", "soft_ready", "dt_done", "e_done"))
        n2_ready, n2_turned, n2T_done, log_ready, log_saved = (sem(n) for n in (
            "n2_ready", "n2_turned", "n2T_done", "log_ready", "log_saved"))
        (ld_att, fetched_in, h2_done, n3_ready, n3_turned, n3T_done, qk_ready, qk_done, v_ready, v_done, s_ready, m_ready, p_ready, pt_ready, pt_done, o_ready, oT_done, tokens_ready, h3_done, n4_ready, n4_turned, n4T_done, n4_stored, lg1_ready, lg1_saved, gu_ready, sg_done, hs_done, ht_ready, ht_done, mm2_ready, acc_done, w_qk_ready) = (sem(n) for n in (
            "a_ld_att", "a_fetched_in", "a_h2_done", "a_n3_ready", "a_n3_turned", "a_n3T_done", "a_qk_ready", "a_qk_done", "a_v_ready", "a_v_done", "a_s_ready", "a_m_ready", "a_p_ready", "a_pt_ready", "a_pt_done", "a_o_ready", "a_oT_done", "a_tokens_ready", "a_h3_done", "a_n4_ready", "a_n4_turned", "a_n4T_done", "a_n4_stored", "a_lg1_ready", "a_lg1_saved", "a_gu_ready", "a_sg_done", "a_hs_done", "a_ht_ready", "a_ht_done", "a_mm2_ready", "a_acc_done", "a_w_qk_ready"))
        (ld_w1, table_set, last_lg, sg_shift, sg_exp, ranks_in, rank_ready, cnt_ready, slots1_ready, table_sent, tab_loaded, idx_ready, idx_copied, x_turned, xT_done, gu1_ready, sg1_done, g1_done, g1_turned, gT_done, y_ready2, y_done, last_stored) = (sem(n) for n in (
            "b_ld_w1", "b_table_set", "b_last_lg", "b_sg_shift", "b_sg_exp", "b_ranks_in", "b_rank_ready", "b_cnt_ready", "b_slots1_ready", "b_table_sent", "b_tab_loaded", "b_idx_ready", "b_idx_copied", "b_x_turned", "b_xT_done", "b_gu1_ready", "b_sg1_done", "b_g1_done", "b_g1_turned", "b_gT_done", "b_y_ready2", "b_y_done", "b_last_stored"))
        y_done2, last_cols = sem("y_done2"), sem("last_cols")
        xg_in, y_sent, ys_in = [sem(f"xg_in{k}") for k in range(XR)], [sem(f"y_sent{k}") for k in range(4)], [sem(f"ys_in{k}") for k in range(2)]
        fetched_in = [sem("fetched_in0"), sem("fetched_in1")]
        h0_loaded, zeroed = sem("h0_loaded"), sem("zeroed")
        zero_ready, slots_zeroed, rows_kept = sem("zero_ready"), sem("slots_zeroed"), sem("rows_kept")
        shift_ready, exps_ready, hot_ready, pos_ready, slots_ready, sent = (sem(n) for n in (
            "shift_ready", "exps_ready", "hot_ready", "pos_ready", "slots_ready", "sent"))
        ld_b, w_loaded, xs_loaded = sem("ld_b"), [sem("w_loaded0"), sem("w_loaded1")], [sem("xs_loaded0"), sem("xs_loaded1")]
        xt_ready, xt_done, hid_ready, hid_done, eo_ready, eo_done = (sem(n) for n in (
            "xt_ready", "xt_done", "hid_ready", "hid_done", "eo_ready", "eo_done"))
        eo_stored = [sem("eo_stored0"), sem("eo_stored1")]

        block = ctx.enter_context(nc.Block())

        @block.sync
        def _(sp):
            sp.dma_start(img[:, 0], d["x"][0:4].rearrange("b (r j) c -> (b r) j c", j=8)).then_inc(ld_img[0], 16)
            sp.dma_start(mats[:], d["mats"]).then_inc(ld_const, 16)
            sp.dma_start(misc[:], d["misc"]).then_inc(ld_const, 16)
            for b in range(4):
                q = slice(32 * b, 32 * b + 32)
                sp.dma_start(w_l1[q].rearrange("p (s f) j -> p s (f j)", s=3),
                             d["Wd3"].rearrange("(s p f) j -> p s (f j)", s=3, p=32)).then_inc(ld_wav, 16)
                sp.dma_start(w_l2[q].rearrange("p (s f) j -> p s (f j)", s=3),
                             d["Wd2"].rearrange("(s p f) j -> p s (f j)", s=3, p=32)).then_inc(ld_wav, 16)
                sp.dma_start(w_l3[q].rearrange("p (s f) j -> p s (f j)", s=3),
                             d["Wd1"].rearrange("(s p f) j -> p s (f j)", s=3, p=32)).then_inc(ld_wav, 16)
                sp.dma_start(w_a[q], d["Wa"].rearrange("(p f) j -> p (f j)", p=32)).then_inc(ld_wav, 16)
            sp.dma_start(gbias, d["gbias"].partition_broadcast(P)).then_inc(ld_wav, 16)
            sp.dma_start(cls[0:1, 0:HID], d["cls_tok"]).then_inc(ld_wav, 16)
            sp.dma_start(img[:, 1], d["x"][4:8].rearrange("b (r j) c -> (b r) j c", j=8)).then_inc(ld_img[1], 16)
            for t, n in ((w_xdt, "w_xdt"), (w_dt, "w_dt"), (w_bc, "w_bc"), (w_in, "w_in"), (chan, "chan"), (w_out, "w_out"), (wg0, "wg0")):
                sp.dma_start(t[:], d[n]).then_inc(ld_mix, 16)
            for b in range(IMAGES):
                sp.dma_start(h0_rows[b * LEN:b * LEN + 1, :], d["cls_tok"]).then_inc(rows_stored, 16)
            for g in range(2):
                sp.wait_ge(rec_ready, g + 1)
                for b in range(4):
                    first = (4 * g + b) * LEN + 1
                    sp.dma_start(h0_rows[first:first + SIDE, :].rearrange("(r j) c -> r j c", j=8),
                                 rec[32 * b:32 * b + 32, g]).then_inc(rows_stored, 16)
            sp.wait_ge(rows_stored, 16 * 16)
            sp.dma_start(table, d["records"]).then_inc(table_set, 16)
            sp.wait_ge(zero_ready, 1)
            sp.dma_start(slots0.rearrange("(p r) c -> p (r c)", p=CAPP),
                         rows[0:CAPP].rearrange("p i q c -> p (i q c)")).then_inc(slots_zeroed, 16)
            sp.wait_ge(zeroed, 1)
            by_image = h0_rows.rearrange("(i t) c -> t i c", t=LEN)
            for q in range(2):
                sp.dma_start(h_all[:, :, q], by_image[q * P:(q + 1) * P]).then_inc(h0_loaded, 16)
            sp.dma_start(h_all[0:1, :, 2], by_image[2 * P:LEN]).then_inc(h0_loaded, 16)
            def load_weights(e, par):
                sp.dma_start(w1e[par].rearrange("p a b -> p (a b)"),
                             d["w1"][ds(e, 1)].rearrange("e p n -> (e p) n")).then_inc(w_loaded[par], 16)
                sp.dma_start(w2e[par].rearrange("p a b -> p (a b)"),
                             d["w2"][ds(e, 1)].rearrange("e p n -> (e p) n")).then_inc(w_loaded[par], 16)

            def load_slots(e, par):
                sp.dma_start(slot_rows[par][0:CAPP],
                             slots0[ds(e * CAP, CAP)].rearrange("(q p) c -> p q c", p=CAPP)).then_inc(xs_loaded[par], 16)

            def store_expert(e, par):
                sp.wait_ge(eo_done, e + 1)
                sp.dma_start(outs0[ds(e * CAP, CAP)].rearrange("(q p) c -> p q c", p=CAPP),
                             expert_rows[par][0:CAPP]).then_inc(eo_stored[par], 16)

            def expert(e, par):
                store_expert(e, par)
                load_weights(e + 2, par)
                load_slots(e + 2, par)

            sp.wait_ge(fold_done, CH)
            sp.wait_ge(bc_ready, 1)
            load_weights(0, 0)
            sp.wait_ge(log_saved, IMAGES)
            load_weights(1, 1)
            sp.dma_start(b2_rows.rearrange("p a b -> p (a b)"), d["b2"].partition_broadcast(P)).then_inc(ld_b, 16)
            sp.dma_start(b1_cols[:], d["b1"]).then_inc(ld_b, 16)
            sp.wait_ge(sent, 16 * IMAGES * TILES)
            load_slots(0, 0)
            load_slots(1, 1)
            staged(sp, 0, EXP0 - 3, expert)
            store_expert(EXP0 - 2, 0)
            store_expert(EXP0 - 1, 1)
            for par in range(2):
                sp.wait_ge(eo_stored[par], 16 * EXP0 // 2)
            if phases == 3:
                sp.dma_start(d["out"][0:EXP0 * CAP, :], outs0).then_inc(stored, 16)
                sp.dma_start(d["out"][2568:2568+128, 0:24], slot_from[:].bitcast(F32)).then_inc(stored, 16)
                sp.dma_start(d["out"][2568:2568+128, 24:48], gate0[:]).then_inc(stored, 16)
                sp.wait_ge(stored, 48)

            sp.wait_ge(eo_ready, EXP0)
            for t, n in ((w_qkr, "w_qk"), (w_v, "w_v"), (rope, "rope"), (wg1, "wg1"), (ws13, "ws13")):
                sp.dma_start(t, d[n]).then_inc(ld_att, 16)
            sp.dma_start(ws2[0:DK], d["ws2"]).then_inc(ld_att, 16)
            sp.dma_start(qk_bias, d["qk_bias"]).then_inc(ld_att, 16)
            sp.dma_start(bv_rows, d["bv"].partition_broadcast(P)).then_inc(ld_att, 16)
            sp.dma_start(bias1[:], d["gate_bias"].partition_broadcast(P)).then_inc(ld_w1, 16)
            sp.dma_start(w13.rearrange("p e h n -> p (e h n)"), d["w13"]).then_inc(ld_w1, 16)
            sp.dma_start(w2s[0:DK].rearrange("p e k n -> p (e k n)"), d["w2s"]).then_inc(ld_w1, 16)

            def store_norm(i, par):
                sp.wait_ge(n4_ready, i + 1)
                sp.dma_start(n4_rows[ds(i * LEN, 2 * P)].rearrange("(q p) c -> p q c", p=P),
                             turn_src4[:, 0:2]).then_inc(n4_stored, 16)
                sp.dma_start(n4_rows[ds(i * LEN + 2 * P, 1)], turn_src4[0:1, 2]).then_inc(n4_stored, 16)

            staged(sp, 0, IMAGES - 1, store_norm)
            sp.wait_ge(n4_stored, 32 * IMAGES)
            if phases == 4:
                sp.wait_ge(acc_done, IMAGES)
                sp.dma_start(d["out"][:, 0:6144], h_all[:].rearrange("p i q c -> p (i q c)")).then_inc(stored, 16)
                sp.dma_start(d["out"][:, 6144:6528], logit1.rearrange("p q e -> p (q e)")).then_inc(stored, 16)
                sp.wait_ge(stored, 32)

            sp.wait_ge(table_sent, 16 * TOPK * T1)
            sp.dma_start(records, table.rearrange("(t p) w -> p t w", p=P)).then_inc(tab_loaded, 16)
            for k in range(4):
                sp.wait_ge(y_sent[k], 16 * NT1 // 4)
            y_rows = outs1.rearrange("(k i t) c -> i t k c", k=TOPK, t=LEN)
            o_rows = d["out"].rearrange("(i t) c -> i t c", t=LEN)

            def load_sum(i, par):
                for q in range(2):
                    sp.dma_start(ysum[par][:, :, q], y_rows[ds(i, 1), q * P:(q + 1) * P].rearrange(
                        "i t k c -> (i t) k c")).then_inc(ys_in[par], 16)
                sp.dma_start(ysum[par][0:1, :, 2], y_rows[ds(i, 1), 2 * P:LEN].rearrange(
                    "i t k c -> (i t) k c")).then_inc(ys_in[par], 16)

            def store_out(i):
                sp.wait_ge(y_done2, i + 1)
                sp.dma_start(o_rows[ds(i, 1), 0:2 * P].rearrange("i (q p) c -> p (i q) c", p=P),
                             h_all[:, ds(i, 1), 0:2].rearrange("p i q c -> p (i q) c")).then_inc(stored, 16)
                sp.dma_start(o_rows[ds(i, 1), 2 * P:LEN].rearrange("i t c -> (i t) c"),
                             h_all[0:1, ds(i, 1), 2].rearrange("p i c -> p (i c)")).then_inc(stored, 16)

            def finish(i, par):
                store_out(i)
                load_sum(i + 2, par)

            load_sum(0, 0)
            load_sum(1, 1)
            staged(sp, 0, IMAGES - 3, finish)
            store_out(IMAGES - 2)
            store_out(IMAGES - 1)
            sp.wait_ge(stored, 32 * IMAGES)

        @block.vector
        def _(dve):
            v = Signals(dve_done)
            lns = Signals(var_ready)

            def run(ins):
                v.on(ins)

            def chain():
                dve.wait_ge(dve_done, v.now())

            def tt(o, a, b, op):
                run(nc.vector.tensor_tensor(o, a, b, op))

            def haar(cur, R, C, bands, A):
                pairs = cur.rearrange("p r (c t) -> p r c t", t=2)
                s = sumc[:, 0:R * C // 2].rearrange("p (r c) -> p r c", r=R)
                f = difc[:, 0:R * C // 2].rearrange("p (r c) -> p r c", r=R)
                tt(s, pairs[:, :, :, 0], pairs[:, :, :, 1], ALU.add)
                tt(f, pairs[:, :, :, 0], pairs[:, :, :, 1], ALU.subtract)
                chain()
                s2 = s.rearrange("p (r t) c -> p t r c", t=2)
                f2 = f.rearrange("p (r t) c -> p t r c", t=2)
                bv = bands.rearrange("p (s r c) -> p s r c", s=3, r=R // 2)
                Av = A.rearrange("p (r c) -> p r c", r=R // 2)
                tt(Av, s2[:, 0], s2[:, 1], ALU.add)
                tt(bv[:, 0], s2[:, 0], s2[:, 1], ALU.subtract)
                tt(bv[:, 1], f2[:, 0], f2[:, 1], ALU.add)
                tt(bv[:, 2], f2[:, 0], f2[:, 1], ALU.subtract)
                chain()
                return Av

            def ihaar(cur, R, C, bands, lev, out):
                bv = bands.rearrange("p (s r c) -> p s r c", s=3, r=R)
                g = lambda k, s: gl[:, 4 + (s < 0), 1 + 3 * lev + k:2 + 3 * lev + k]
                lo = sumc[:, 0:2 * R * C].rearrange("p (r t c) -> p t r c", t=2, c=C)
                hi = difc[:, 0:2 * R * C].rearrange("p (r t c) -> p t r c", t=2, c=C)
                vv = vw[:, 0:R * C].rearrange("p (r c) -> p r c", r=R)
                run(nc.vector.tensor_scalar(vv, bv[:, 1], g(1, 1), None, ALU.mult))
                run(nc.vector.scalar_tensor_tensor(lo[:, 0], bv[:, 0], g(0, 1), cur, ALU.mult, ALU.add))
                run(nc.vector.scalar_tensor_tensor(lo[:, 1], bv[:, 0], g(0, -1), cur, ALU.mult, ALU.add))
                chain()
                run(nc.vector.scalar_tensor_tensor(hi[:, 0], bv[:, 2], g(2, 1), vv, ALU.mult, ALU.add))
                run(nc.vector.scalar_tensor_tensor(hi[:, 1], bv[:, 2], g(2, -1), vv, ALU.mult, ALU.add))
                chain()
                lo = sumc[:, 0:2 * R * C].rearrange("p (r c) -> p r c", c=C)
                hi = difc[:, 0:2 * R * C].rearrange("p (r c) -> p r c", c=C)
                pairs = out.rearrange("p r (c t) -> p r c t", t=2)
                tt(pairs[:, :, :, 0], lo, hi, ALU.add)
                tt(pairs[:, :, :, 1], lo, hi, ALU.subtract)
                chain()

            def settle():
                nc.vector.memset(scratch_dve[:], 0.0)

            def layernorm(dst, src, n, rows=P, ends=None):
                st = lnst[0:rows]
                ag = lnstat[0:rows]
                settle()
                for k in range(n):
                    run(nc.vector.bn_stats(st[:, k, :], src[:, k, :]))
                chain()
                settle()
                for k in range(n):
                    last = nc.vector.bn_aggr(ag[:, k, 0:2], st[:, k, :])
                    if k < n - 1:
                        run(last)
                last.then_inc(var_ready, 1)
                lns.k += 1
                dve.wait_ge(rstd_ready, lns.now())
                y, t = ag[:, 0:n, 2:3], ag[:, 0:n, 4:5]
                run(nc.vector.scalar_tensor_tensor(t, ag[:, 0:n, 1:2], EPS, y, ALU.add, ALU.mult))
                chain()
                run(nc.vector.scalar_tensor_tensor(t, t, -0.5, y, ALU.mult, ALU.mult))
                chain()
                run(nc.vector.scalar_tensor_tensor(y, t, 1.5, y, ALU.add, ALU.mult))
                chain()
                for k in range(n):
                    ins = nc.vector.tensor_scalar(dst[:, k, :], src[:, k, :], ag[:, k, 0:1], ag[:, k, 2:3],
                                                  ALU.subtract, ALU.mult)
                    if k == n - 1 and ends is not None:
                        ins.then_inc(ends, 1)
                    else:
                        run(ins)

            dve.wait_ge(ld_const, 32)
            dve.wait_ge(ld_wav, 18 * 16)
            layernorm(cls[0:1, HID:2 * HID].rearrange("p (k c) -> p k c", k=1),
                      cls[0:1, 0:HID].rearrange("p (k c) -> p k c", k=1), 1, 1)
            chain()
            nc.vector.engine_nop().then_inc(normed_ready, 1) if 0 else nc.vector.tensor_copy(gl[0:1, 7, 0:1], cls[0:1, 0:1]).then_inc(normed_ready, 1)
            for g in range(2):
                dve.wait_ge(ld_img[g], 16)
                a1 = haar(img[:, g], 8, 256, B1, A1)
                a2 = haar(a1, 4, 128, B2, A2)
                haar(a2, 2, 64, B3, A3)
                pt = partial[:, g]
                last = None
                for col, (b, w, n, s) in enumerate(
                        [(A3, w_a, 32, 1 / 8)] + [(B3, w_l3[:, :, j], 96, 1 / 8) for j in range(3)]
                        + [(B2, w_l2[:, :, j], 384, 1 / 4) for j in range(3)]
                        + [(B1, w_l1[:, :, j], 1536, 1 / 2) for j in range(3)]):
                    last = nc.vector.tensor_tensor_reduce(dot_out[:, 0:n], b, w, s, 0.0, ALU.mult, ALU.add,
                                                          pt[:, col:col + 1])
                    if col < 9:
                        run(last)
                        chain()
                last.then_inc(dots_ready, 1)
                dve.wait_ge(sums_ready, g + 1)
                lg, ex = gl[:, 0], gl[:, 1]
                tt(lg, bank[0][:, 0:10], gbias, ALU.add)
                chain()
                l9 = lg[:, 1:10].rearrange("p (l k) -> p l k", k=3)
                run(nc.vector.tensor_reduce(gl[:, 2, 0:3], l9, AX.X, ALU.max))
                chain()
                tt(l9, l9, gl[:, 2, 0:3].unsqueeze(2).broadcast_to([P, 3, 3]), ALU.subtract)
                nc.vector.tensor_scalar(lg[:, 0:1], lg[:, 0:1], -1.0, None, ALU.mult).then_inc(logit_ready, 1)
                dve.wait_ge(exp_ready, g + 1)
                e9 = ex[:, 1:10].rearrange("p (l k) -> p l k", k=3)
                run(nc.vector.tensor_reduce(gl[:, 3, 0:3], e9, AX.X, ALU.add))
                run(nc.vector.tensor_scalar(gl[:, 3, 3:4], ex[:, 0:1], 1.0, None, ALU.add))
                chain()
                run(nc.vector.reciprocal(gl[:, 3, 4:8], gl[:, 3, 0:4]))
                run(nc.vector.memset(ex[:, 0:1], 1.0))
                chain()
                tt(gl[:, 4, 1:10].rearrange("p (l k) -> p l k", k=3), e9,
                   gl[:, 3, 4:7].unsqueeze(2).broadcast_to([P, 3, 3]), ALU.mult)
                run(nc.vector.tensor_copy(gl[:, 4, 0:1], gl[:, 3, 7:8]))
                chain()
                tt(gl[:, 4], gl[:, 4], misc[:, M_SCALE:M_SCALE + 10], ALU.mult)
                chain()
                run(nc.vector.tensor_scalar(gl[:, 5], gl[:, 4], -1.0, None, ALU.mult))
                run(nc.vector.tensor_scalar(A3g, A3, gl[:, 4, 0:1], None, ALU.mult))
                chain()
                ihaar(A3g.rearrange("p (r c) -> p r c", r=1), 1, 32, B3, 0, R2.rearrange("p (r c) -> p r c", r=2))
                ihaar(R2.rearrange("p (r c) -> p r c", r=2), 2, 64, B2, 1, R1.rearrange("p (r c) -> p r c", r=4))
                ihaar(R1.rearrange("p (r c) -> p r c", r=4), 4, 128, B1, 2, rec[:, g])
                nc.vector.tensor_copy(gl[:, 7, 0:1], rec[:, g, 7, 255:256]).then_inc(rec_ready, 1)
                if g == 1:
                    dve.wait_ge(turned, 1 + 4)
                layernorm(normed, rec[:, g], 8)
                chain()
                nc.vector.tensor_copy(gl[:, 7, 1:2], normed[:, 7, 255:256]).then_inc(normed_ready, 1)
            dve.wait_ge(ld_mix, 7 * 16)
            run(nc.vector.tensor_reduce(w_bcs[:], w_bc[:].rearrange("p k (b s) -> p k b s", s=STATE), AX.X, ALU.add))
            chain()
            for b in range(2):
                run(nc.vector.tensor_copy(w_bcr[:, b], w_bcs[:, :, b:b + 1].broadcast_to([P, CH, P])))
            chain()
            nc.vector.tensor_copy(gl[:, 7, 2:3], w_bcr[:, 1, 0, 0:1]).then_inc(bc_ready, 1)
            if phases == 1:
                return

            def recurrence_in(n, par):
                for k in (2, 1, 0):
                    off = TAPS - 1 - k
                    for c in range(CH):
                        if k == 2:
                            dve.wait_ge(tap_done, 4 * n + (c + 1))
                        ins = nc.vector.scalar_tensor_tensor(conv[:, c, off:LEN], bank[c][:, 0:LEN - off],
                                                             chan[:, c, k:k + 1], conv[:, c, off:LEN], ALU.mult, ALU.add)
                        if k == 0 and c == CH - 1:
                            ins.then_inc(conv_done, 1)
                        else:
                            run(ins)
                    if k:
                        chain()

            def step_size(n, par):
                dve.wait_ge(soft_ready, n + 1)
                nc.vector.scalar_tensor_tensor(dts, xb, 0.0, soft, ALU.max, ALU.add).then_inc(dt_done, 1)
                run(nc.vector.tensor_scalar(bct[par], bct[par], 0.5, 0.5, ALU.mult, ALU.add))

            def recurrence(i, par):
                gate = lambda b: bct[par][:, b:b + 1, :].broadcast_to([P, CH, LEN])
                dve.wait_ge(e_done, i + 1)
                chain()
                tt(gat, xconv[par], gate(0), ALU.mult)
                run(nc.vector.tensor_scalar(al, es[par], 0.5, 0.5, ALU.mult, ALU.add))
                run(nc.vector.tensor_scalar(om, es[par], -0.5, 0.5, ALU.mult, ALU.add))
                chain()
                run(nc.vector.tensor_scalar(al, al, 0.01, 0.99, ALU.max, ALU.min))
                tt(gat, gat, om, ALU.mult)
                chain()
                for c in range(CH):
                    run(nc.vector.tensor_tensor_scan(hs[:, c], al[:, c], gat[:, c], 0.0, ALU.mult, ALU.add))
                chain()
                tt(hs, hs, gate(1), ALU.mult)
                chain()
                for c in range(CH):
                    run(nc.vector.scalar_tensor_tensor(hs[:, c], xconv[par][:, c], chan[:, c, 6:7], hs[:, c],
                                                       ALU.mult, ALU.add))
                chain()
                after(dve, out_ready, 2 * i - 2)
                nc.vector.tensor_tensor(ys[par], hs, zs[par], ALU.mult).then_inc(y_ready, 1)

            def residual_norm(i, ready, done, ln_done):
                dve.wait_ge(ready, i + 1)
                pair = bank[2][:, :].rearrange("p (q c) -> p q c", q=2)
                h2 = h_all[:, ds(i, 1), 0:2].rearrange("p i q c -> p (i q) c")
                h3 = h_all[0:1, ds(i, 1), 2].rearrange("p i c -> p (i c)")
                tt(h2, h2, pair, ALU.add)
                nc.vector.tensor_tensor(h3, h3, bank[3][0:1, 0:HID], ALU.add).then_inc(done, 1)
                dve.wait_ge(done, i + 1)
                src = h_all[:, ds(i, 1)].rearrange("p i q c -> p (i q) c")
                after(dve, rows_kept, i)
                after(dve, n2_turned, i)
                layernorm(turn_src, src, TILES, ends=ln_done)

            def save_logits(i):
                dve.wait_ge(log_ready, i + 1)
                lg = bank[3][:, 300:300 + TILES * EXP0].rearrange("p (q e) -> p q e", q=TILES)
                run(nc.vector.tensor_copy(logit0[:, ds(i, 1), 0:2].rearrange("p i q e -> p (i q) e"), lg[:, 0:2]))
                nc.vector.tensor_copy(logit0[0:1, ds(i, 1), 2].rearrange("p i e -> p (i e)"), lg[0:1, 2]).then_inc(log_saved, 1)

            dve.wait_ge(h0_loaded, 48)

            def stage(n, par, a=True, b=True, c=True):
                if a:
                    recurrence_in(n, par)
                if b:
                    recurrence(n - 1, 1 - par)
                if c:
                    residual_norm(n - 2, tok_ready, res_done, n2_ready)
                if a:
                    step_size(n, par)
                if c:
                    save_logits(n - 2)

            stage(0, 0, b=False, c=False)
            stage(1, 1, c=False)
            stage(2, 0)
            staged(dve, 3, 6, stage, ((v, PER_MIX), (lns, 2)))
            stage(7, 1)
            stage(IMAGES, 0, a=False)
            stage(IMAGES + 1, 1, a=False, b=False)

            T0 = IMAGES * TILES
            wide = lambda a: a.unsqueeze(2).broadcast_to([P, T0, EXP0])
            row_of = lambda off, n: misc[:, off:off + n].unsqueeze(1).broadcast_to([P, T0, n])
            lg = logit0[:].rearrange("p i q e -> p (i q) e")
            valid = misc[:, M_VALID:M_VALID + T0]
            mx, sm, posv, basev, keep, dest = (r_one[:, k] for k in range(6))
            chain()
            dve.wait_ge(log_saved, IMAGES)
            run(nc.vector.tensor_reduce(mx, lg, AX.X, ALU.max))
            chain()
            nc.vector.tensor_tensor(r_exp, lg, wide(mx), ALU.subtract).then_inc(shift_ready, 1)
            tt(r_hot, lg, wide(mx), ALU.is_equal)
            chain()
            tt(r_hot, r_hot, row_of(M_FIRST0, EXP0), ALU.mult)
            chain()
            run(nc.vector.tensor_reduce(mx, r_hot, AX.X, ALU.max))
            chain()
            tt(r_hot, r_hot, wide(mx), ALU.is_equal)
            chain()
            tt(r_hot, r_hot, wide(valid), ALU.mult)
            chain()

            def earlier_tiles(hot, a, b, n):
                run(nc.vector.memset(a[:, 0:1], 0.0))
                run(nc.vector.tensor_copy(a[:, 1:n], hot[:, 0:n - 1]))
                chain()
                step = 1
                while step < n:
                    tt(b[:, step:n], a[:, step:n], a[:, 0:n - step], ALU.add)
                    run(nc.vector.tensor_copy(b[:, 0:step], a[:, 0:step]))
                    chain()
                    a, b, step = b, a, 2 * step
                return a

            cum = earlier_tiles(r_hot, r_cum, r_tmp, T0)
            assert cum is r_tmp
            nc.vector.tensor_copy(gl7[:], r_hot[:, 0, 0:1]).then_inc(hot_ready, 1)
            dve.wait_ge(exps_ready, 1)
            run(nc.vector.tensor_reduce(sm, r_exp, AX.X, ALU.add))
            tt(r_cum, r_hot, row_of(M_BASE0, EXP0), ALU.mult)
            chain()
            run(nc.vector.reciprocal(sm, sm))
            run(nc.vector.tensor_reduce(basev, r_cum, AX.X, ALU.add))
            dve.wait_ge(pos_ready, 1)
            chain()
            tt(r_cum, r_hot, bank[0][:, 0:T0 * EXP0].rearrange("p (t e) -> p t e", e=EXP0), ALU.mult)
            chain()
            run(nc.vector.tensor_reduce(posv, r_cum, AX.X, ALU.add))
            chain()
            run(nc.vector.tensor_scalar(keep, posv, float(CAP), None, ALU.is_lt))
            tt(dest, posv, basev, ALU.add)
            chain()
            tt(keep, keep, valid, ALU.mult)
            chain()
            tt(gate0[:], sm, keep, ALU.mult)
            tt(posv, dest, keep, ALU.mult)
            run(nc.vector.scalar_tensor_tensor(dest, dest, -FAR, keep, ALU.add, ALU.mult))
            chain()
            run(nc.vector.tensor_copy(slot_from[:], posv))
            nc.vector.tensor_scalar(slot_to[:], dest, FAR, None, ALU.add).then_inc(slots_ready, 1)

            def slots_out(e, par):
                dve.wait_ge(xt_ready, e + 1)
                run(nc.vector.tensor_copy(slotT[par][:, 0], bank[0][:, 0:CAP]))
                nc.vector.tensor_copy(slotT[par][:, 1], bank[1][:, 0:CAP]).then_inc(xt_done, 1)

            def expert(e, par, more=True):
                if more:
                    slots_out(e + 1, 1 - par)
                dve.wait_ge(eo_ready, e + 1)
                after(dve, eo_stored[par], 8 * (e - par))
                b2 = b2_rows[0:CAPP, ds(e, 1), :]
                run(nc.vector.tensor_tensor(expert_rows[par][0:CAPP, 0:2],
                                            bank[6][0:CAPP, :].rearrange("p (q c) -> p q c", q=2),
                                            b2.broadcast_to([CAPP, 2, HID]), ALU.add))
                nc.vector.tensor_tensor(expert_rows[par][0:CAPP, 2:3], bank[7][0:CAPP, 0:HID].unsqueeze(1), b2,
                                        ALU.add).then_inc(eo_done, 1)

            dve.wait_ge(ld_b, 32)
            slots_out(0, 0)
            expert(0, 0)
            expert(1, 1)
            staged(dve, 2, 5, expert, ((v, 4),))
            expert(6, 0)
            expert(7, 1, more=False)

            dve.wait_ge(ld_att, 16 * 8)
            raw, fold = (w.rearrange("p h (o t) -> p (h o) t", t=2) for w in (w_qkr, w_qk))
            tt(fold[:, :, 0], raw[:, :, 0], raw[:, :, 1], ALU.subtract)
            tt(fold[:, :, 1], raw[:, :, 0], raw[:, :, 1], ALU.add)
            run(nc.vector.scalar_tensor_tensor(qk_bias[:, 0:4], qk_bias[:, 4:8], qk_bias[:, 8:9], qk_bias[:, 0:4],
                                               ALU.mult, ALU.add))
            chain()
            run(nc.vector.memset(logit1[:], 0.0))
            nc.vector.tensor_copy(gl7[:], w_qk[:, 1, 511:512]).then_inc(w_qk_ready, 1)

            def combine(i, par):
                dve.wait_ge(fetched_in[par], 24 * (i + (2 - par)))
                for q in range(TILES):
                    k = ROWS[q]
                    h = h_all[0:k, ds(i, 1), q].rearrange("p i c -> p (i c)")
                    g = gate0[0:k, ds(i * TILES + q, 1)]
                    ins = nc.vector.scalar_tensor_tensor(h, fetched[par][0:k, q], g, h, ALU.mult, ALU.add)
                    run(ins) if q < TILES - 1 else ins.then_inc(h2_done, 1)
                after(dve, h2_done, i + 1)
                after(dve, n3_turned, i)
                layernorm(turn_src, h_all[:, ds(i, 1)].rearrange("p i q c -> p (i q) c"), TILES, ends=n3_ready)

            def maxima(i, par):
                for q in range(TILES):
                    k = ROWS[q]
                    dve.wait_ge(s_ready, 3 * i + (q + 1))
                    if q == 0:
                        after(dve, p_ready, 3 * i)
                    run(nc.vector.tensor_reduce(soft_c[0:k, q:q + 1], bank[2 + q][0:k, 0:LEN], AX.X, ALU.max))
                chain()
                for q in range(TILES):
                    k = ROWS[q]
                    nc.vector.tensor_scalar(soft_c[0:k, 3 + q:4 + q], soft_c[0:k, q:q + 1], -float(HEAD) ** -0.5, None,
                                            ALU.mult).then_inc(m_ready, 1)

            def rotate(n, par):
                after(dve, s_ready, 3 * n)
                for g in range(4):
                    dve.wait_ge(qk_ready, 4 * n + (g + 1))
                    nc.vector.scalar_tensor_tensor(qkT[:, g], bank[g % 2][:, 0:LEN], qk_bias[:, g:g + 1],
                                                   rope[:, g % 2], ALU.add, ALU.mult).then_inc(qk_done, 1)

            def shared_gate(j, par):
                dve.wait_ge(lg1_ready, j + 1)
                lg = bank[7][:, 300:300 + 2 * EXP1].rearrange("p (q e) -> p q e", q=2)
                nc.vector.tensor_copy(logit1[:, ds(j * 2, 2)], lg[:, 0:2]).then_inc(lg1_saved, 1)
                after(dve, ht_ready, 2 * j)
                for q in range(TILES):
                    k = ROWS[q]
                    dve.wait_ge(sg_done, 3 * j + (q + 1))
                    nc.vector.tensor_tensor(gated[0:k, q], silu_g[0:k, q], bank[6 + q % 2][0:k, DFE:2 * DFE],
                                            ALU.mult).then_inc(hs_done, 1)

            def values(n, par):
                dve.wait_ge(v_ready, n + 1)
                after(dve, o_ready, 2 * n - 2)
                run(nc.vector.tensor_tensor(vals[par][:, 0:2], bank[0][:, :].rearrange("p (q c) -> p q c", q=2),
                                            bv_rows.unsqueeze(1).broadcast_to([P, 2, HID]), ALU.add))
                nc.vector.tensor_tensor(vals[par][0:1, 2], bank[1][0:1, 0:HID], bv_rows[0:1], ALU.add).then_inc(v_done, 1)

            def shared_out(j, par):
                dve.wait_ge(mm2_ready, j + 1)
                h2 = h_all[:, ds(j, 1), 0:2].rearrange("p i q c -> p (i q) c")
                h3 = h_all[0:1, ds(j, 1), 2].rearrange("p i c -> p (i c)")
                run(nc.vector.tensor_tensor(h2, h2, bank[6][:, :].rearrange("p (q c) -> p q c", q=2), ALU.add))
                nc.vector.tensor_tensor(h3, h3, bank[7][0:1, 0:HID], ALU.add).then_inc(acc_done, 1)

            def attended(i, par):
                dve.wait_ge(tokens_ready, i + 1)
                dve.wait_ge(p_ready, 3 * i + 3)
                run(nc.vector.reciprocal(soft_c[:, 9:11], soft_c[:, 6:8]))
                run(nc.vector.reciprocal(soft_c[0:1, 11:12], soft_c[0:1, 8:9]))
                chain()
                for q in range(TILES):
                    k = ROWS[q]
                    h = h_all[0:k, ds(i, 1), q].rearrange("p i c -> p (i c)")
                    o = bank[2][0:k, q * HID:(q + 1) * HID] if q < 2 else bank[3][0:1, 0:HID]
                    ins = nc.vector.scalar_tensor_tensor(h, o, soft_c[0:k, 9 + q:10 + q], h, ALU.mult, ALU.add)
                    run(ins) if q < TILES - 1 else ins.then_inc(h3_done, 1)
                after(dve, h3_done, i + 1)
                after(dve, n4_turned, i)
                after(dve, n4_stored, 32 * i)
                layernorm(turn_src4, h_all[:, ds(i, 1)].rearrange("p i q c -> p (i q) c"), TILES, ends=n4_ready)

            def stage(n, par, a=True, b=True, c=True, ahead=True):
                if b:
                    maxima(n - 1, 1 - par)
                if a:
                    rotate(n, par)
                if c:
                    shared_gate(n - 2, par)
                if a:
                    values(n, par)
                if c:
                    shared_out(n - 2, par)
                if b:
                    attended(n - 1, 1 - par)
                if ahead:
                    combine(n + 1, 1 - par)

            combine(0, 0)
            stage(0, 0, b=False, c=False)
            stage(1, 1, c=False)
            stage(2, 0)
            staged(dve, 3, 6, stage, ((v, PER_ATT), (lns, 4)))
            stage(7, 1, ahead=False)
            stage(8, 0, a=False, ahead=False)
            stage(9, 1, a=False, b=False, ahead=False)

            dve.wait_ge(ld_w1, 48)
            dve.wait_ge(last_lg, 1)
            run(nc.vector.tensor_copy(logit1[0:IMAGES, T1 - 1], bank[0][0:IMAGES, 0:EXP1]))
            chain()
            nc.vector.tensor_scalar(score, logit1[:], -1.0, None, ALU.mult).then_inc(sg_shift, 1)
            dve.wait_ge(sg_exp, 1)
            run(nc.vector.tensor_scalar(score, score, 1.0, None, ALU.add))
            chain()
            run(nc.vector.reciprocal(score, score))
            chain()
            tt(biased, score, bias1[:].unsqueeze(1).broadcast_to([P, T1, EXP1]), ALU.add)
            chain()
            quad = biased.rearrange("p t (g k) -> p (t g) k", g=GROUPS)
            hi1, lo1, hi2, lo2, top, mid_, low, gsum, gkeep, gpen = (g_all[:, k] for k in range(10))
            tt(hi1, quad[:, :, 0], quad[:, :, 1], ALU.max)
            tt(lo1, quad[:, :, 0], quad[:, :, 1], ALU.min)
            tt(hi2, quad[:, :, 2], quad[:, :, 3], ALU.max)
            tt(lo2, quad[:, :, 2], quad[:, :, 3], ALU.min)
            chain()
            tt(top, hi1, hi2, ALU.max)
            tt(mid_, hi1, hi2, ALU.min)
            tt(low, lo1, lo2, ALU.max)
            chain()
            tt(mid_, mid_, low, ALU.max)
            chain()
            tt(gsum, top, mid_, ALU.add)
            chain()
            gs = gsum.rearrange("p (t g) -> p t g", g=GROUPS)
            other = gs.unsqueeze(2).broadcast_to([P, T1, GROUPS, GROUPS])
            own = gs.unsqueeze(3).broadcast_to([P, T1, GROUPS, GROUPS])
            cmp = g_pair[:, 0].rearrange("p (t g k) -> p t g k", t=T1, g=GROUPS)
            same = g_pair[:, 1].rearrange("p (t g k) -> p t g k", t=T1, g=GROUPS)
            tt(cmp, other, own, ALU.is_gt)
            tt(same, other, own, ALU.is_equal)
            chain()
            tt(g_pair[:, 1].rearrange("p (t n) -> p t n", t=T1), g_pair[:, 1].rearrange("p (t n) -> p t n", t=T1),
               misc[:, M_LOWER:M_LOWER + GROUPS * GROUPS].unsqueeze(1).broadcast_to([P, T1, GROUPS * GROUPS]), ALU.mult)
            chain()
            tt(g_pair[:, 0], g_pair[:, 0], g_pair[:, 1], ALU.add)
            chain()
            run(nc.vector.tensor_reduce(gkeep, g_pair[:, 0].rearrange("p (n k) -> p n k", k=GROUPS), AX.X, ALU.add))
            chain()
            run(nc.vector.tensor_scalar(gkeep, gkeep, 2.0, None, ALU.is_lt))
            chain()
            run(nc.vector.tensor_scalar(gpen, gkeep, LOW, LOW, ALU.mult, ALU.subtract))
            four = lambda a: a.unsqueeze(2).broadcast_to([P, T1 * GROUPS, GROUPS])
            leftq = left.rearrange("p t (g k) -> p (t g) k", g=GROUPS)
            tt(leftq, quad, four(gkeep), ALU.mult)
            chain()
            tt(leftq, leftq, four(gpen), ALU.add)
            chain()
            exps = lambda a: a.unsqueeze(2).broadcast_to([P, T1, EXP1])
            best = one_k[:, 0, 0:T1]
            for k in range(TOPK):
                hot = hots[:, k].rearrange("p (t e) -> p t e", e=EXP1)
                run(nc.vector.tensor_reduce(best, left, AX.X, ALU.max))
                chain()
                tt(r1_tmp, left, exps(best), ALU.is_equal)
                chain()
                tt(r1_tmp, r1_tmp, misc[:, M_FIRST1:M_FIRST1 + EXP1].unsqueeze(1).broadcast_to([P, T1, EXP1]), ALU.mult)
                chain()
                run(nc.vector.tensor_reduce(best, r1_tmp, AX.X, ALU.max))
                chain()
                tt(hot, r1_tmp, exps(best), ALU.is_equal)
                chain()
                run(nc.vector.scalar_tensor_tensor(left, hot, -4.0 * LOW, left, ALU.mult, ALU.add))
                if k == 0:
                    run(nc.vector.tensor_copy(sel, hot))
                else:
                    tt(sel, sel, hot, ALU.add)
                chain()
            tt(sel, sel, exps(misc[:, M_VALID1:M_VALID1 + T1]), ALU.mult)
            chain()
            cum = earlier_tiles(sel, cumA, cumB, T1)
            assert cum is cumB
            tt(per_exp[:, 0], cum[:, T1 - 1], sel[:, T1 - 1], ALU.add)
            chain()
            nc.vector.tensor_copy(gl7[:], per_exp[:, 0, 0:1]).then_inc(ranks_in, 1)
            flat = lambda a: a.rearrange("p t e -> p (t e)")
            tt(hots2, hots, flat(score).unsqueeze(1).broadcast_to([P, TOPK, T1 * EXP1]), ALU.mult)
            chain()
            wk = one_k[:, 1].rearrange("p (k t) -> p k t", k=TOPK)
            run(nc.vector.tensor_reduce(one_k[:, 1], hots2.rearrange("p k (t e) -> p (k t) e", e=EXP1), AX.X, ALU.add))
            chain()
            total = one_k[:, 0, 0:T1]
            tt(total, wk[:, 0], wk[:, 1], ALU.add)
            chain()
            tt(total, total, wk[:, 2], ALU.add)
            chain()
            tt(total, total, wk[:, 3], ALU.add)
            chain()
            run(nc.vector.tensor_scalar(total, total, 1e-20, None, ALU.add))
            chain()
            run(nc.vector.reciprocal(total, total))
            chain()
            tt(wk, wk, total.unsqueeze(1).broadcast_to([P, TOPK, T1]), ALU.mult)
            chain()
            run(nc.vector.tensor_scalar(record[:, :, :, 2], wk, 2.5, None, ALU.mult))
            for k in range(TOPK):
                run(nc.vector.tensor_copy(record[:, k, :, 0], misc[:, M_TOKEN:M_TOKEN + T1]))
                run(nc.vector.tensor_scalar(record[:, k, :, 1], misc[:, M_TOKEN:M_TOKEN + T1], float(k * TOKENS), None, ALU.add))
            run(nc.vector.memset(record[:, :, :, 3], 0.0))
            dve.wait_ge(cnt_ready, 1)
            cnt, tiles_of, first, other_, ends = (per_exp[:, k] for k in range(1, 6))
            run(nc.vector.tensor_copy(cnt, bank[1][:, 0:EXP1]))
            chain()
            tt(steps_c, cnt.unsqueeze(2).broadcast_to([P, EXP1, T1]),
               misc[:, M_STEPS:M_STEPS + T1].unsqueeze(1).broadcast_to([P, EXP1, T1]), ALU.is_gt)
            chain()
            run(nc.vector.tensor_reduce(tiles_of, steps_c, AX.X, ALU.add))
            chain()
            one = lambda a: a.unsqueeze(2)
            earlier_tiles(one(tiles_of), one(first), one(other_), EXP1)
            start = first
            tt(ends, start, tiles_of, ALU.add)
            run(nc.vector.tensor_scalar(cnt, start, float(P), None, ALU.mult))
            chain()
            dve.wait_ge(rank_ready, 1)
            tt(place, bank[0][:, 0:T1 * EXP1].rearrange("p (t e) -> p t e", e=EXP1),
               cnt.unsqueeze(1).broadcast_to([P, T1, EXP1]), ALU.add)
            chain()
            tt(hots2, hots, flat(place).unsqueeze(1).broadcast_to([P, TOPK, T1 * EXP1]), ALU.mult)
            chain()
            run(nc.vector.tensor_reduce(one_k[:, 2], hots2.rearrange("p k (t e) -> p (k t) e", e=EXP1), AX.X, ALU.add))
            chain()
            nc.vector.tensor_copy(slot1[:].rearrange("p k t -> p (k t)"), one_k[:, 2]).then_inc(slots1_ready, 1)
            tt(tile_cmp[0:1], ends[0:1].unsqueeze(1).broadcast_to([1, NT1, EXP1]),
               misc[0:1, M_TILE:M_TILE + NT1].unsqueeze(2).broadcast_to([1, NT1, EXP1]), ALU.is_le)
            chain()
            run(nc.vector.tensor_reduce(idx_weight[0:1], tile_cmp[0:1], AX.X, ALU.add))
            chain()
            run(nc.vector.tensor_scalar(tile_exp[:], idx_weight[0:1], float(EXP1 - 1), None, ALU.min))
            chain()
            dve.wait_ge(tab_loaded, 16)
            run(nc.vector.tensor_copy(idx_weight[:], records[:, :, 2]))
            nc.vector.tensor_copy(rec_idx[:], records[:, :, 0:2]).then_inc(idx_ready, 1)
            chain()

            def gate(j, par):
                dve.wait_ge(sg1_done, j + 1)
                after(dve, g1_turned, j - 1)
                nc.vector.tensor_tensor(gu1[par], sg1[par], bank[2 + par][:, DFE:2 * DFE], ALU.mult).then_inc(g1_done, 1)

            def weigh(j, r):
                dve.wait_ge(y_ready2, j + 1)
                after(dve, y_sent[r], 4 * (j - r))
                nc.vector.tensor_scalar(y1[r], bank[6 + r % 2][:, 0:HID], idx_weight[:, ds(j, 1)], None,
                                        ALU.mult).then_inc(y_done, 1)

            for j in range(4):
                gate(j, j % 2)
                if j >= 2:
                    weigh(j - 2, j - 2)
            gate(4, 0)
            weigh(2, 2)
            gate(5, 1)
            weigh(3, 3)
            with dve.Fori(0, (NT1 - 8) // 4) as p:
                for r in range(4):
                    gate(4 * p + (6 + r), r % 2)
                    weigh(4 * p + (4 + r), r)
            gate(NT1 - 2, 0)
            weigh(NT1 - 4, 0)
            gate(NT1 - 1, 1)
            weigh(NT1 - 3, 1)
            weigh(NT1 - 2, 2)
            weigh(NT1 - 1, 3)

            def sum_up(i, par):
                dve.wait_ge(ys_in[par], 24 * (i + (2 - par)))
                h2 = h_all[:, ds(i, 1), 0:2].rearrange("p i q c -> p (i q c)")
                h3 = h_all[0:1, ds(i, 1), 2].rearrange("p i c -> p (i c)")
                y = ysum[par]
                two = lambda k: y[:, k, 0:2].rearrange("p q c -> p (q c)")
                for a, b, to in ((0, 1, 0), (2, 3, 2), (0, 2, 0)):
                    tt(two(to), two(a), two(b), ALU.add)
                    tt(y[0:1, to, 2], y[0:1, a, 2], y[0:1, b, 2], ALU.add)
                    if (a, b) != (0, 1):
                        chain()
                tt(h2, h2, two(0), ALU.add)
                nc.vector.tensor_tensor(h3, h3, y[0:1, 0, 2], ALU.add).then_inc(y_done2, 1)

            staged(dve, 0, IMAGES - 1, sum_up, ((v, 14),))

        @block.gpsimd
        def _(pool):
            def settle(j, col):
                if not isinstance(j, int):
                    nc.gpsimd.tensor_tensor(scratch_pool[0:1, col:col + 1], scratch_pool[0:1, 2:3],
                                            scratch_pool[0:1, 2:3], ALU.add)

            nc.gpsimd.memset(scratch_pool[:], 0.0).then_inc(pool_done, 1)
            pool.wait_ge(pool_done, 1)
            nc.gpsimd.memset(rows, 0.0).then_inc(zero_ready, 1)
            nc.gpsimd.memset(logit0[:], 0.0)
            nc.gpsimd.memset(h_all[:, :, 2], 0.0).then_inc(zeroed, 1)

            pool.wait_ge(slots_zeroed, 16)

            def keep_rows(i, par):
                pool.wait_ge(n2_ready, i + 1)
                nc.gpsimd.tensor_copy(rows[:, ds(i, 1)].rearrange("p i q c -> p (i q c)"),
                                      turn_src[:].rearrange("p q c -> p (q c)")).then_inc(rows_kept, 1)

            staged(pool, 0, IMAGES - 1, keep_rows)
            pool.wait_ge(rows_kept, IMAGES)

            pool.wait_ge(slots_ready, 1)
            for t in range(IMAGES * TILES):
                nc.gpsimd.indirect_dma_start(slots0, bass.IndirectOffsetOnAxis(ap=slot_to[:, t:t + 1], axis=0),
                                             rows[:, t // TILES, t % TILES], None, bounds_check=EXP0 * CAP - 1,
                                             oob_is_err=False).then_inc(sent, 16)
            for par in range(2):
                pool.wait_ge(eo_stored[par], 16 * EXP0 // 2)
            pool.wait_ge(sent, 16 * IMAGES * TILES)
            for i in range(IMAGES):
                after(pool, h2_done, i - 1)
                for q in range(TILES):
                    k = max(2, ROWS[q])
                    t = i * TILES + q
                    nc.gpsimd.indirect_dma_start(fetched[i % 2][0:k, q], None, outs0,
                                                 bass.IndirectOffsetOnAxis(ap=slot_from[0:k, t:t + 1], axis=0))\
                        .then_inc(fetched_in[i % 2], 16)

            pool.wait_ge(slots1_ready, 1)
            pool.wait_ge(table_set, 16)
            for t in range(T1):
                k_rows = P if t < T1 - 1 else IMAGES
                for k in range(TOPK):
                    nc.gpsimd.indirect_dma_start(table, bass.IndirectOffsetOnAxis(ap=slot1[0:k_rows, k, t:t + 1], axis=0),
                                                 record[0:k_rows, k, t], None).then_inc(table_sent, 16)
            pool.wait_ge(idx_ready, 1)
            pool.wait_ge(n4_stored, 32 * IMAGES)

            def fetch(j, r):
                after(pool, x_turned, j - (XR - 1))
                after(pool, y_sent[r % 4], 4 * (j - r % 4) - 4 * IDX + 16)
                nc.gpsimd.tensor_copy(idx_now[r][:], rec_idx[:, ds(j, 1)].rearrange("p j w -> p (j w)")).then_inc(idx_copied, 1)
                pool.wait_ge(idx_copied, j + 1)
                settle(j, 0)
                nc.gpsimd.indirect_dma_start(xg[r % XR], None, n4_rows, bass.IndirectOffsetOnAxis(ap=idx_now[r][:, 0:1], axis=0))\
                    .then_inc(xg_in[r % XR], 16)

            def send(j, r):
                pool.wait_ge(y_done, j + 1)
                settle(j, 1)
                nc.gpsimd.indirect_dma_start(outs1, bass.IndirectOffsetOnAxis(ap=idx_now[r][:, 1:2], axis=0), y1[r % 4], None,
                                             bounds_check=TOPK * TOKENS - 1, oob_is_err=False).then_inc(y_sent[r % 4], 16)

            for j in range(IDX):
                if j >= LAG:
                    send(j - LAG, j - LAG)
                fetch(j, j)
            with pool.Fori(1, NT1 // IDX) as p:
                for r in range(IDX):
                    send(IDX * p + (r - LAG), (r - LAG) % IDX)
                    fetch(IDX * p + r, r)
            for j in range(NT1 - LAG, NT1):
                send(j, j % IDX)

        @block.scalar
        def _(act):
            s = Signals(act_done)
            lns = Signals(rstd_ready)

            def inverse_std(rows, n):
                lns.k += 1
                act.wait_ge(var_ready, lns.now())
                s.on(nc.scalar.activation(lnstat[0:rows, 0:n, 3:4], lnstat[0:rows, 0:n, 1:2], ACT.Ln,
                                          bias=misc[0:rows, M_EPS:M_EPS + 1]))
                act.wait_ge(act_done, s.now())
                nc.scalar.activation(lnstat[0:rows, 0:n, 2:3], lnstat[0:rows, 0:n, 3:4], ACT.Exp,
                                     scale=-0.5).then_inc(rstd_ready, 1)

            act.wait_ge(ld_const, 32)
            inverse_std(1, 1)
            act.wait_ge(turned, 1)
            for h in range(HALVES):
                ins = nc.scalar.activation(nT0[:, h, :].rearrange("p (i t) -> p i t", t=LEN)[:, :, 0],
                                           bank[1][:, h:h + 1].broadcast_to([P, IMAGES]), ACT.Copy)
                ins.then_inc(turned_out, 1)
            for g in range(2):
                act.wait_ge(logit_ready, g + 1)
                nc.scalar.activation(gl[:, 1], gl[:, 0], ACT.Exp).then_inc(exp_ready, 1)
                inverse_std(P, 8)
                for n in range(4):
                    h, jj = n // 2, 4 * (n % 2)
                    act.wait_ge(turned, 1 + 4 * g + n + 1)
                    dst = nT0[:, h, :].rearrange("p (i t) -> p i t", t=LEN)[:, 4 * g:4 * g + 4, 1:LEN]
                    dst = dst.rearrange("p i (r j) -> p j i r", j=8)[:, jj:jj + 4]
                    nc.scalar.activation(dst, bank[4 + n % 4][:, :].rearrange("p (j i r) -> p j i r", j=4, i=4),
                                         ACT.Copy).then_inc(turned_out, 1)
            for c in range(CH):
                act.wait_ge(fold_done, c + 1)
                nc.scalar.activation(w_fold[:, c], bank[2 + c % 2][:, :], ACT.Copy).then_inc(fold_out, 1)
            if phases == 1:
                return
            act.wait_ge(ld_mix, 7 * 16)
            act.wait_ge(rows_stored, 16 * 16)
            act.wait_ge(bc_ready, 1)

            def project(n, par):
                for c in range(CH):
                    act.wait_ge(x_ready, 4 * n + (c + 1))
                    nc.scalar.activation(conv[:, c], bank[c][:, 0:LEN], ACT.Identity, bias=chan[:, c, 4:5],
                                         scale=chan[:, c, 3:4]).then_inc(tap_done, 1)
                after(act, y_ready, n - 1)
                for c in range(CH):
                    act.wait_ge(z_ready, 4 * n + (c + 1))
                    ins = nc.scalar.activation(zs[par][:, c], bank[4 + c][:, 0:LEN], ACT.Silu)
                    s.on(ins) if c < CH - 1 else ins.then_inc(zs_done, 1)
                act.wait_ge(conv_done, n + 1)
                nc.scalar.activation(xconv[par], conv, ACT.Silu).then_inc(xconv_ready, 1)

            def out_rows(i):
                for h in range(HALVES):
                    act.wait_ge(out_ready, 2 * i + (h + 1))
                    if h == 0 and (not isinstance(i, int) or i >= 1):
                        act.wait_ge(tok_ready, i)
                    ins = nc.scalar.activation(outT[:, h], bank[h][:, 0:LEN], ACT.Copy)
                    s.on(ins) if h == 0 else ins.then_inc(outT_done, 1)

            def steps(n, par):
                act.wait_ge(bcsum_ready, n + 1)
                for b in range(2):
                    ins = nc.scalar.activation(bct[par][:, b], bank[4 + b][:, 0:LEN], ACT.Tanh, scale=0.5 / STATE)
                    s.on(ins) if b == 0 else ins.then_inc(bct_done, 1)
                act.wait_ge(dt_ready, n + 1)
                after(act, dt_done, n)
                for c in range(CH):
                    ins = nc.scalar.activation(xb[:, c], bank[(6 + c) % 8][:, 0:LEN], ACT.Identity, bias=chan[:, c, 5:6])
                    s.on(ins) if c < CH - 1 else ins.then_inc(xb_done, 1)
                act.wait_ge(xb_done, n + 1)
                s.on(nc.scalar.activation(soft, xb, ACT.Abs))
                act.wait_ge(act_done, s.now())
                s.on(nc.scalar.activation(soft, soft, ACT.Exp, scale=-1.0))
                act.wait_ge(act_done, s.now())
                nc.scalar.activation(soft, soft, ACT.Ln, bias=1.0).then_inc(soft_ready, 1)

            def decay(n, par):
                act.wait_ge(dt_done, n + 1)
                after(act, y_ready, n)
                nc.scalar.activation(es[par], dts, ACT.Tanh, scale=0.05).then_inc(e_done, 1)

            def norm_out(i, turned_sem, done, dst):
                act.wait_ge(turned_sem, i + 1)
                s.on(nc.scalar.activation(dst[:, :, 0:2 * P].rearrange("p h (q t) -> p q h t", q=2),
                                          bank[2][:, :].rearrange("p (q h t) -> p q h t", q=2, h=2), ACT.Copy))
                nc.scalar.activation(dst[:, :, 2 * P:LEN], bank[3][:, 256:258].unsqueeze(2), ACT.Copy).then_inc(done, 1)

            def stage(n, par, a=True, b=True, c=True):
                if a:
                    project(n, par)
                if c:
                    out_rows(n - 2)
                if a:
                    steps(n, par)
                if c:
                    inverse_std(P, TILES)
                if a:
                    decay(n, par)
                if c:
                    norm_out(n - 2, n2_turned, n2T_done, n2T)

            stage(0, 0, b=False, c=False)
            stage(1, 1, c=False)
            stage(2, 0)
            staged(act, 3, 6, stage, ((s, PER_MIX_ACT), (lns, 2)))
            stage(7, 1)
            stage(IMAGES, 0, a=False)
            stage(IMAGES + 1, 1, a=False, b=False)

            act.wait_ge(shift_ready, 1)
            nc.scalar.activation(r_exp, r_exp, ACT.Exp).then_inc(exps_ready, 1)
            act.wait_ge(ld_b, 32)

            def expert(e, par):
                for m in range(DFF // P):
                    act.wait_ge(hid_ready, 8 * e + (m + 1))
                    nc.scalar.activation(hidden[par][:, m], bank[2 + m % 4][:, 0:CAP], ACT.Relu,
                                         bias=b1_cols[:, ds(e, 1), m]).then_inc(hid_done, 1)

            staged(act, 0, EXP0 - 1, expert)

            def turned_rows(i, ready, done, dst, b):
                act.wait_ge(ready, i + 1)
                s.on(nc.scalar.activation(dst[:, :, 0:2 * P].rearrange("p h (q t) -> p q h t", q=2),
                                          bank[b][:, :].rearrange("p (q h t) -> p q h t", q=2, h=2), ACT.Copy))
                nc.scalar.activation(dst[:, :, 2 * P:LEN], bank[b + 1][:, 256:258].unsqueeze(2), ACT.Copy).then_inc(done, 1)

            def exponents(i, par):
                after(act, pt_ready, 3 * i)
                after(act, h3_done, i)
                for q in range(TILES):
                    k = ROWS[q]
                    act.wait_ge(m_ready, 3 * i + (q + 1))
                    nc.scalar.activation(probs[0:k, q], bank[2 + q][0:k, 0:LEN], ACT.Exp, bias=soft_c[0:k, 3 + q:4 + q],
                                         scale=float(HEAD) ** -0.5, accum_out=soft_c[0:k, 6 + q:7 + q]).then_inc(p_ready, 1)

            def probs_out(i, par):
                after(act, o_ready, 2 * i)
                for q in range(TILES):
                    k = ROWS[q]
                    act.wait_ge(pt_ready, 3 * i + (q + 1))
                    nc.scalar.activation(probsT[0:k, q], bank[(5, 2, 3)[q]][0:k, 0:LEN], ACT.Copy).then_inc(pt_done, 1)

            def shared_silu(j, par):
                after(act, hs_done, 3 * j)
                for q in range(TILES):
                    k = ROWS[q]
                    act.wait_ge(gu_ready, 3 * j + (q + 1))
                    nc.scalar.activation(silu_g[0:k, q], bank[6 + q % 2][0:k, 0:DFE], ACT.Silu).then_inc(sg_done, 1)

            def gated_out(j, par):
                after(act, mm2_ready, j)
                for k in range(2):
                    act.wait_ge(ht_ready, 2 * j + (k + 1))
                    nc.scalar.activation(gatedT[0:DK, k], bank[7 - k][0:DK, 0:LEN], ACT.Copy).then_inc(ht_done, 1)

            def attended(i, par):
                after(act, tokens_ready, i)
                for h in range(HALVES):
                    act.wait_ge(o_ready, 2 * i + (h + 1))
                    ins = nc.scalar.activation(outT[:, h], bank[4 + h][:, 0:LEN], ACT.Copy)
                    s.on(ins) if h == 0 else ins.then_inc(oT_done, 1)

            def stage(n, par, a=True, b=True, c=True, ahead=True):
                if a:
                    after(act, qk_ready, 4 * n)
                    after(act, v_ready, n)
                    turned_rows(n, n3_turned, n3T_done, n3T, 0)
                if b:
                    exponents(n - 1, 1 - par)
                if c:
                    after(act, gu_ready, 3 * (n - 2))
                    turned_rows(n - 2, n4_turned, n4T_done, n4T, 6)
                    act.wait_ge(n4T_done, n - 1)
                    s.on(nc.scalar.activation(n4T_last[:, :, ds(n - 2, 1)], n4T[:, :, 2 * P:LEN], ACT.Copy))
                if c:
                    shared_silu(n - 2, par)
                if b:
                    probs_out(n - 1, 1 - par)
                if c:
                    gated_out(n - 2, par)
                if b:
                    attended(n - 1, 1 - par)
                    inverse_std(P, TILES)
                if ahead:
                    inverse_std(P, TILES)

            inverse_std(P, TILES)
            stage(0, 0, b=False, c=False)
            stage(1, 1, c=False)
            stage(2, 0)
            staged(act, 3, 6, stage, ((s, PER_ATT_ACT), (lns, 4)))
            stage(7, 1, ahead=False)
            stage(8, 0, a=False, ahead=False)
            stage(9, 1, a=False, b=False, ahead=False)

            nc.scalar.activation(gl8[:], n4T_last[:, 0, 0:1], ACT.Copy).then_inc(last_cols, 1)
            act.wait_ge(sg_shift, 1)
            nc.scalar.activation(score, score, ACT.Exp).then_inc(sg_exp, 1)

            def x_out(j, par):
                act.wait_ge(x_turned, j + 1)
                nc.scalar.activation(xT1[par], bank[par][:, 0:2 * P].rearrange("p (h t) -> p h t", h=HALVES),
                                     ACT.Copy).then_inc(xT_done, 1)

            def silu(j, par):
                act.wait_ge(gu1_ready, j + 1)
                after(act, g1_done, j - 1)
                nc.scalar.activation(sg1[par], bank[2 + par][:, 0:DFE], ACT.Silu).then_inc(sg1_done, 1)

            def gated1_out(j, par):
                act.wait_ge(g1_turned, j + 1)
                nc.scalar.activation(gT1[par][0:DK], bank[4 + par][0:DK, 0:2 * P].rearrange("p (k t) -> p k t", k=2),
                                     ACT.Copy).then_inc(gT_done, 1)

            def tile(j, par, ahead=True, now=True, late=True):
                if ahead:
                    x_out(j + 1, 1 - par)
                if now:
                    silu(j, par)
                if late:
                    gated1_out(j - 1, 1 - par)

            x_out(0, 0)
            tile(0, 0, late=False)
            tile(1, 1)
            tile(2, 0)
            staged(act, 3, NT1 - 2, tile)
            tile(NT1 - 1, 1, ahead=False)
            tile(NT1, 0, ahead=False, now=False)

        @block.tensor
        def _(pe):
            pe.wait_ge(ld_const, 32)
            pe.wait_ge(normed_ready, 1)
            for h in range(HALVES):
                mm = nc.tensor.transpose(bank[1][:, h:h + 1], cls[0:1, HID + h * P:HID + (h + 1) * P], ident[0:1, 0:1])
            mm.then_inc(turned, 1)
            for g in range(2):
                pe.wait_ge(dots_ready, g + 1)
                nc.tensor.matmul(bank[0][:, 0:10], same_image, partial[:, g], start=True, stop=True).then_inc(sums_ready, 1)
                pe.wait_ge(normed_ready, 1 + g + 1)
                for n in range(4):
                    h, jj = n // 2, 4 * (n % 2)
                    if g:
                        pe.wait_ge(turned_out, 2 + n + 1)
                    for j in range(4):
                        mm = nc.tensor.transpose(bank[4 + n][:, j * P:(j + 1) * P], normed[:, jj + j, h * P:(h + 1) * P], ident)
                    mm.then_inc(turned, 1)
            pe.wait_ge(ld_mix, 7 * 16)
            for c in range(CH):
                if c >= 2:
                    pe.wait_ge(fold_out, c - 1)
                for k in range(CH):
                    mm = nc.tensor.matmul(bank[2 + c % 2][:, :], w_xdt[:, k, c * P:(c + 1) * P], w_dt[:, k],
                                          start=(k == 0), stop=(k == CH - 1))
                mm.then_inc(fold_done, 1)
            if phases == 1:
                return
            pe.wait_ge(fold_out, CH)
            pe.wait_ge(turned_out, 10)
            pe.wait_ge(bc_ready, 1)

            def dense(out, weights, moving, last=None):
                for k in range(len(weights)):
                    mm = nc.tensor.matmul(out, weights[k], moving[k], start=(k == 0), stop=(k == len(weights) - 1))
                return mm

            def project(n, par):
                x = [nT0[:, h, ds(n * LEN, LEN)] for h in range(HALVES)]
                after(pe, xb_done, n)
                after(pe, log_saved, n - 2)
                for c in range(CH):
                    dense(bank[c][:, 0:LEN], [w_in[:, h, c * P:(c + 1) * P] for h in range(HALVES)], x).then_inc(x_ready, 1)
                after(pe, bct_done, n)
                for c in range(CH):
                    dense(bank[4 + c][:, 0:LEN], [w_in[:, h, (CH + c) * P:(CH + c + 1) * P] for h in range(HALVES)],
                          x).then_inc(z_ready, 1)

            def out_rows(i, par, conv_count):
                pe.wait_ge(conv_done, conv_count)
                pe.wait_ge(y_ready, i + 1)
                for h in range(HALVES):
                    dense(bank[h][:, 0:LEN], [w_out[:, c, h * P:(h + 1) * P] for c in range(CH)],
                          [ys[par][:, c] for c in range(CH)]).then_inc(out_ready, 1)
                pe.wait_ge(outT_done, i + 1)
                after(pe, log_saved, i)
                turn_rows(outT, tok_ready)

            def turn_rows(src, done):
                for q in range(TILES):
                    for h in range(HALVES):
                        o = bank[2][:, q * HID + h * P:q * HID + (h + 1) * P] if q < 2 else bank[3][0:1, h * P:(h + 1) * P]
                        mm = nc.tensor.transpose(o, src[:, h, q * P:q * P + ROWS[q]], ident)
                mm.then_inc(done, 1)

            def turn_norm(i, ready, done):
                pe.wait_ge(ready, i + 1)
                for q in range(TILES):
                    for h in range(HALVES):
                        k = ROWS[q]
                        o = bank[2][:, (q * 2 + h) * P:(q * 2 + h + 1) * P] if q < 2 else bank[3][:, 256 + h:257 + h]
                        src = turn_src[0:k, q, h * P:(h + 1) * P]
                        mm = nc.tensor.transpose(o, src, ident[0:k, 0:k])
                mm.then_inc(done, 1)

            def steps(n, par):
                pe.wait_ge(xconv_ready, n + 1)
                pe.wait_ge(zs_done, n + 1)
                x = [xconv[par][:, c] for c in range(CH)]
                for b in range(2):
                    mm = dense(bank[4 + b][:, 0:LEN], [w_bcr[:, b, c] for c in range(CH)], x)
                mm.then_inc(bcsum_ready, 1)
                after(pe, outT_done, n - 1)
                for c in range(CH):
                    mm = dense(bank[(6 + c) % 8][:, 0:LEN], [w_fold[:, k, c * P:(c + 1) * P] for k in range(CH)], x)
                mm.then_inc(dt_ready, 1)

            def logits(i, done, wg, nT, n_exp, out):
                pe.wait_ge(done, i + 1)
                for q in range(TILES):
                    k = ROWS[q]
                    mm = dense(bank[3][0:k, 300 + q * n_exp:300 + (q + 1) * n_exp],
                               [nT[:, h, q * P:q * P + k] for h in range(HALVES)], [wg[:, h] for h in range(HALVES)])
                mm.then_inc(out, 1)

            def stage(n, par, a=True, b=True, c=True):
                if a:
                    project(n, par)
                if c:
                    out_rows(n - 2, par, n + 1 if a else IMAGES)
                if a:
                    steps(n, par)
                if c:
                    turn_norm(n - 2, n2_ready, n2_turned)
                    logits(n - 2, n2T_done, wg0, n2T, EXP0, log_ready)

            stage(0, 0, b=False, c=False)
            stage(1, 1, c=False)
            stage(2, 0)
            staged(pe, 3, 6, stage)
            stage(7, 1)
            stage(IMAGES, 0, a=False)
            stage(IMAGES + 1, 1, a=False, b=False)

            pe.wait_ge(hot_ready, 1)
            flat = lambda a: a.rearrange("p t e -> p (t e)")
            dense(bank[0][:, 0:IMAGES * TILES * EXP0], [before, ones], [flat(r_hot), flat(r_tmp)]).then_inc(pos_ready, 1)

            def turn_slots(e, par):
                pe.wait_ge(xs_loaded[par], 8 * (e + (2 - par)))
                after(pe, xt_done, e)
                for h in range(HALVES):
                    for q in range(3):
                        mm = nc.tensor.transpose(bank[h][:, q * CAPP:(q + 1) * CAPP],
                                                 slot_rows[par][0:CAPP, q, h * P:(h + 1) * P], ident[0:CAPP, 0:CAPP])
                mm.then_inc(xt_ready, 1)

            def expert(e, par, more=True):
                pe.wait_ge(w_loaded[par], 16 * (e + (2 - par)))
                pe.wait_ge(xt_done, e + 1)
                x = [slotT[par][:, h] for h in range(HALVES)]
                for m in range(DFF // P):
                    after(pe, hid_done, 8 * e + (m - 3))
                    dense(bank[2 + m % 4][:, 0:CAP], [w1e[par][:, h, m * P:(m + 1) * P] for h in range(HALVES)],
                          x).then_inc(hid_ready, 1)
                if more:
                    turn_slots(e + 1, 1 - par)
                pe.wait_ge(hid_done, 8 * e + 8)
                after(pe, eo_done, e)
                for q in range(3):
                    o = bank[6][0:CAPP, q * HID:(q + 1) * HID] if q < 2 else bank[7][0:CAPP, 0:HID]
                    mm = dense(o, [hidden[par][:, m, q * CAPP:(q + 1) * CAPP] for m in range(DFF // P)],
                               [w2e[par][:, m] for m in range(DFF // P)])
                mm.then_inc(eo_ready, 1)

            pe.wait_ge(slots_ready, 1)
            turn_slots(0, 0)
            expert(0, 0)
            staged(pe, 1, 6, expert)
            expert(7, 1, more=False)

            def turn_rows_in(i, src, ready, done, b):
                pe.wait_ge(ready, i + 1)
                for q in range(TILES):
                    for h in range(HALVES):
                        k = ROWS[q]
                        o = bank[b][:, (q * 2 + h) * P:(q * 2 + h + 1) * P] if q < 2 else bank[b + 1][:, 256 + h:257 + h]
                        mm = nc.tensor.transpose(o, src[0:k, q, h * P:(h + 1) * P], ident[0:k, 0:k])
                mm.then_inc(done, 1)

            def tile_of(x, q):
                return x[:, q * P:q * P + ROWS[q]]

            def stage(n, par, a=True, b=True, c=True, ahead=True):
                i, j = n - 1, n - 2
                if a:
                    after(pe, v_done, n)
                    turn_rows_in(n, turn_src, n3_ready, n3_turned, 0)
                if b:
                    pe.wait_ge(qk_done, 4 * i + 4)
                    after(pe, h3_done, i)
                    after(pe, oT_done, i)
                    for q in range(TILES):
                        dense(bank[2 + q][0:ROWS[q], 0:LEN], [tile_of(qkT[:, h], q) for h in range(HALVES)],
                              [qkT[:, HALVES + h] for h in range(HALVES)]).then_inc(s_ready, 1)
                if c:
                    after(pe, acc_done, j)
                    turn_rows_in(j, turn_src4, n4_ready, n4_turned, 6)
                if a:
                    pe.wait_ge(n3T_done, n + 1)
                    for g in range(4):
                        if g >= 2:
                            pe.wait_ge(qk_done, 4 * n + (g - 1))
                        dense(bank[g % 2][:, 0:LEN], [w_qk[:, h, g * P:(g + 1) * P] for h in range(HALVES)],
                              [n3T[:, h] for h in range(HALVES)]).then_inc(qk_ready, 1)
                if c:
                    pe.wait_ge(n4T_done, j + 1)
                    for q in range(2):
                        k = ROWS[q]
                        mm = dense(bank[7][0:k, 300 + q * EXP1:300 + (q + 1) * EXP1],
                                   [tile_of(n4T[:, h], q) for h in range(HALVES)], [wg1[:, h] for h in range(HALVES)])
                    mm.then_inc(lg1_ready, 1)
                    for q in range(TILES):
                        k = ROWS[q]
                        if q == 1:
                            pe.wait_ge(lg1_saved, j + 1)
                        if q == 2:
                            pe.wait_ge(hs_done, 3 * j + 1)
                        dense(bank[6 + q % 2][0:k, 0:2 * DFE], [tile_of(n4T[:, h], q) for h in range(HALVES)],
                              [ws13[:, h] for h in range(HALVES)]).then_inc(gu_ready, 1)
                if b:
                    pe.wait_ge(p_ready, 3 * i + 3)
                    for kt in range(TILES):
                        for q in range(TILES):
                            mm = nc.tensor.transpose(bank[(5, 2, 3)[kt]][0:ROWS[kt], q * P:q * P + ROWS[q]],
                                                     tile_of(probs[0:ROWS[q], q], kt), ident[0:ROWS[q], 0:ROWS[q]])
                        mm.then_inc(pt_ready, 1)
                if a:
                    pe.wait_ge(qk_done, 4 * n + 4)
                    for q in range(TILES):
                        k = ROWS[q]
                        mm = dense(bank[0][:, q * HID:(q + 1) * HID] if q < 2 else bank[1][0:1, 0:HID],
                                   [tile_of(n3T[:, h], q) for h in range(HALVES)], [w_v[:, h] for h in range(HALVES)])
                    mm.then_inc(v_ready, 1)
                if c:
                    pe.wait_ge(hs_done, 3 * j + 3)
                    for k in range(2):
                        for q in range(TILES):
                            mm = nc.tensor.transpose(bank[7 - k][0:DK, q * P:q * P + ROWS[q]],
                                                     gated[0:ROWS[q], q, k * DK:(k + 1) * DK], ident[0:ROWS[q], 0:ROWS[q]])
                        mm.then_inc(ht_ready, 1)
                if b:
                    pe.wait_ge(pt_done, 3 * i + 3)
                    pe.wait_ge(v_done, i + 1)
                    for h in range(HALVES):
                        dense(bank[4 + h][:, 0:LEN],
                              [vals[1 - par][0:ROWS[kt], kt, h * P:(h + 1) * P] for kt in range(TILES)],
                              [probsT[0:ROWS[kt], kt] for kt in range(TILES)]).then_inc(o_ready, 1)
                if c:
                    pe.wait_ge(ht_done, 2 * j + 2)
                    for q in range(TILES):
                        mm = dense(bank[6][:, q * HID:(q + 1) * HID] if q < 2 else bank[7][0:1, 0:HID],
                                   [tile_of(gatedT[0:DK, k], q) for k in range(2)], [ws2[0:DK, k] for k in range(2)])
                    mm.then_inc(mm2_ready, 1)
                if b:
                    pe.wait_ge(oT_done, i + 1)
                    turn_rows(outT, tokens_ready)

            pe.wait_ge(w_qk_ready, 1)
            stage(0, 0, b=False, c=False)
            stage(1, 1, c=False)
            stage(2, 0)
            staged(pe, 3, 6, stage)
            stage(7, 1)
            stage(8, 0, a=False)
            stage(9, 1, a=False, b=False)

            pe.wait_ge(last_cols, 1)
            dense(bank[0][0:IMAGES, 0:EXP1], [n4T_last[:, h] for h in range(HALVES)],
                  [wg1[:, h] for h in range(HALVES)]).then_inc(last_lg, 1)
            pe.wait_ge(ranks_in, 1)
            dense(bank[1][:, 0:EXP1], [ones], [per_exp[:, 0]]).then_inc(cnt_ready, 1)
            dense(bank[0][:, 0:T1 * EXP1], [before, ones], [flat(sel), flat(cumB)]).then_inc(rank_ready, 1)

            def turn_x(j, par, r):
                pe.wait_ge(xg_in[r], 16 // XR * (j + (XR - r)))
                after(pe, xT_done, j - 1)
                for h in range(HALVES):
                    mm = nc.tensor.transpose(bank[par][:, h * P:(h + 1) * P], xg[r][:, h * P:(h + 1) * P], ident)
                mm.then_inc(x_turned, 1)

            def expert_of(j):
                return pe.value_load(tile_exp[0:1, ds(j, 1)], min_val=0, max_val=EXP1 - 1)

            def gate_up(j, par):
                e = expert_of(j)
                pe.wait_ge(xT_done, j + 1)
                after(pe, g1_done, j - 1)
                dense(bank[2 + par][:, 0:2 * DFE], [xT1[par][:, h] for h in range(HALVES)],
                      [w13[:, ds(e, 1), h].rearrange("p e n -> p (e n)") for h in range(HALVES)]).then_inc(gu1_ready, 1)

            def turn_gated(j, par):
                pe.wait_ge(g1_done, j + 1)
                after(pe, gT_done, j - 1)
                for k in range(2):
                    mm = nc.tensor.transpose(bank[4 + par][0:DK, k * P:(k + 1) * P], gu1[par][:, k * DK:(k + 1) * DK], ident)
                mm.then_inc(g1_turned, 1)

            def down(j, par):
                e = expert_of(j)
                pe.wait_ge(gT_done, j + 1)
                after(pe, y_done, j - 1)
                dense(bank[6 + par][:, 0:HID], [gT1[par][0:DK, k] for k in range(2)],
                      [w2s[0:DK, ds(e, 1), k].rearrange("p e n -> p (e n)") for k in range(2)]).then_inc(y_ready2, 1)

            def tile(j, r, ahead=True, now=True, late=True, last=True):
                par = r % 2
                if ahead:
                    turn_x(j + 1, 1 - par, (r + 1) % XR)
                if now:
                    gate_up(j, par)
                if late:
                    turn_gated(j - 1, 1 - par)
                if last:
                    down(j - 2, par)

            pe.wait_ge(idx_ready, 1)
            turn_x(0, 0, 0)
            tile(0, 0, late=False, last=False)
            tile(1, 1, last=False)
            for j in range(2, XR):
                tile(j, j)
            with pe.Fori(1, NT1 // XR - 1) as p:
                for r in range(XR):
                    tile(XR * p + r, r)
            for j in range(NT1 - XR, NT1 - 1):
                tile(j, j % XR)
            tile(NT1 - 1, XR - 1, ahead=False)
            tile(NT1, 0, ahead=False, now=False)
            tile(NT1 + 1, 1, ahead=False, now=False, late=False)
    return nc


def rows_on_partitions(w):
    k, n = w.shape
    return w.reshape(k // P, P, n).transpose(1, 0, 2)


def lay_out(a):
    o = dict(constants())
    o["x"] = a["x"].reshape(IMAGES, SIDE, SIDE)
    o["cls_tok"] = a["cls_tok"].reshape(1, HID)
    for n in ("Wa", "Wd1", "Wd2", "Wd3"):
        o[n] = a["L0_tok_" + n]
    o["gbias"] = np.concatenate([a["L0_tok_" + n] for n in ("ba", "bd1", "bd2", "bd3")])
    wx = a["L0_attn_W_x"]
    o["w_in"] = rows_on_partitions(a["L0_attn_W_in"].T)
    o["w_dt"] = rows_on_partitions(a["L0_attn_W_dt"].T)
    o["w_xdt"] = rows_on_partitions(wx[2 * STATE:])
    o["w_bc"] = rows_on_partitions(wx[:2 * STATE].T)
    o["w_out"] = rows_on_partitions(a["L0_attn_W_out"].T)
    chan = np.concatenate([a["L0_attn_conv_w"][:, 0, :], a["L0_attn_conv_b"][:, None], a["L0_attn_b_dt"][:, None],
                           a["L0_attn_D"][:, None], a["L0_attn_D"][:, None]], 1)
    o["chan"] = rows_on_partitions(chan)
    o["w1"] = a["L0_ffn_w1"].reshape(EXP0, HALVES, P, DFF).transpose(0, 2, 1, 3).reshape(EXP0, P, -1)
    o["w2"] = a["L0_ffn_w2"].reshape(EXP0, DFF // P, P, HID).transpose(0, 2, 1, 3).reshape(EXP0, P, -1)
    o["b1"] = a["L0_ffn_b1"].reshape(EXP0, DFF // P, P).transpose(2, 0, 1)
    o["b2"] = a["L0_ffn_b2"].reshape(-1)
    wq, wk, bq, bk = (a["L1_attn_" + n] for n in ("Wq", "Wk", "bq", "bk"))
    o["w_qk"] = rows_on_partitions(np.concatenate([wq.T, wk.T], 1))
    bias = np.concatenate([bq, bk]).reshape(4, P)
    pair = bias.reshape(4, P // 2, 2)[:, :, ::-1].reshape(4, P)
    sign = np.broadcast_to(np.tile(np.array([-1, 1], np.float32), P // 2), (4, P))
    o["qk_bias"] = np.concatenate([bias, pair, sign]).T
    o["w_v"] = rows_on_partitions(a["L1_attn_Wv"].T)
    o["bv"] = a["L1_attn_bv"]
    o["wg1"] = rows_on_partitions(a["L1_ffn_gate_w"].T)
    o["ws13"] = rows_on_partitions(np.concatenate([a["L1_ffn_ws1"].T, a["L1_ffn_ws3"].T], 1))
    o["ws2"] = a["L1_ffn_ws2"].T.reshape(2, DK, HID).transpose(1, 0, 2)
    o["gate_bias"] = a["L1_ffn_gate_bias"]
    w13 = np.concatenate([a["L1_ffn_w1"], a["L1_ffn_w3"]], 1)
    o["w13"] = w13.transpose(2, 0, 1).reshape(HALVES, P, EXP1, 2 * DFE).transpose(1, 2, 0, 3).reshape(P, -1)
    w2 = a["L1_ffn_w2"].transpose(2, 0, 1).reshape(2, DK, EXP1, HID)
    o["w2s"] = w2.transpose(1, 2, 0, 3).reshape(DK, -1)
    o["wg0"] = rows_on_partitions(a["L0_ffn_wg"])
    return {k: np.ascontiguousarray(v) for k, v in o.items()}


def kernel(**inputs):
    import concourse.bacc as bacc
    from concourse.bass_utils import run_bass_kernel_spmd

    nc = bacc.Bacc("TRN2", target_bir_lowering=False, num_devices=1)
    arrays = {f"in_{n}": v for n, v in lay_out({n: np.asarray(v) for n, v in inputs.items()}).items()}
    d = {n[3:]: nc.dram_tensor(n, v.shape, mybir.dt.from_np(v.dtype), kind="ExternalInput").ap()
         for n, v in arrays.items()}
    d["out"] = nc.dram_tensor("out", (TOKENS, HID), F32, kind="ExternalOutput").ap()
    build(nc, d)
    r = run_bass_kernel_spmd(nc, [arrays], core_ids=[0])
    return r.results[0]["out"].reshape(IMAGES, LEN, HID)
```

```python
from contextlib import ExitStack, contextmanager

import numpy as np

import concourse.bass as bass
from concourse import mybir

F32 = mybir.dt.float32
U32 = mybir.dt.uint32
ALU = mybir.AluOpType
ACT = mybir.ActivationFunctionType
AX = mybir.AxisListType
ds = bass.ds

P = 128
IMAGES, SIDE, HID = 8, 256, 256
LEN = SIDE + 1
TOKENS = IMAGES * LEN
HALVES = HID // P
TILES = 3
ROWS = (P, P, 1)
EPS = 1e-5
INNER, STATE, TAPS = 512, 16, 4
CH = INNER // P
EXP0, DFF = 8, 1024
CAP = int(1.25 * TOKENS / EXP0)
CAPP = CAP // 3
EXP1, DFE, TOPK, GROUPS = 16, 192, 4, 4
DK = DFE // 2
HEAD = 128
NT1 = (TOKENS * TOPK + EXP1 * (P - 1)) // P
FAR = 1.0e6
LOW = 1.0e30
T1 = 2 * IMAGES + 1
XR, IDX, LAG = 8, 16, 7
DT_ORDER = (2, 3, 0, 1)
ROUND = 1.5 * 2.0 ** 23


class Signals:

    def __init__(self, sem):
        self.sem, self.base, self.k = sem, 0, 0

    def on(self, ins):
        ins.then_inc(self.sem, 1)
        self.k += 1
        return self.base + self.k

    def now(self):
        return self.base + self.k

    @contextmanager
    def loop(self, trip, trips, per):
        start = self.base + self.k
        self.base, self.k = start + trip * per, 0
        yield
        assert self.k == per, (self.k, per)
        self.base, self.k = start + trips * per, 0


def staged(eng, first, last, body, signals=()):
    trips = (last - first + 1) // 2
    with ExitStack() as ctx:
        p = ctx.enter_context(eng.Fori(0, trips))
        for s, per in signals:
            ctx.enter_context(s.loop(p, trips, per))
        body(2 * p + first, first % 2)
        body(2 * p + (first + 1), (first + 1) % 2)


def fours(eng, body, signals=()):
    assert T1 % 4 == 1
    with ExitStack() as ctx:
        p = ctx.enter_context(eng.Fori(1, T1 // 4))
        for s, per in signals:
            ctx.enter_context(s.loop(p - 1, T1 // 4 - 1, per))
        for r in range(4):
            body(4 * p + r, r)


def after(eng, sem, value):
    if not isinstance(value, int) or value > 0:
        eng.wait_ge(sem, value)


def constants():
    k = np.arange(P)
    ident = np.eye(P, dtype=np.float32)
    before = (k[:, None] < k[None, :]).astype(np.float32)
    same_image = (k[:, None] // 32 == k[None, :] // 32).astype(np.float32)
    ones = np.ones((P, P), np.float32)
    mats = np.stack([ident, before, same_image, ones], 1)
    pos = np.arange(LEN, dtype=np.float32)
    inv = np.float32(10000.0) ** (np.arange(0, HEAD, 2, dtype=np.float32) / np.float32(HEAD))
    radians = (pos[:, None] / inv).astype(np.float32)
    sincos = np.stack((np.sin(radians), np.cos(radians)), -1).reshape(LEN, -1)
    rope = np.repeat(sincos, 2, axis=-1).astype(np.float32)
    rope = np.ascontiguousarray(rope.T.reshape(HALVES, P, LEN).transpose(1, 0, 2))
    valid = np.ones((P, IMAGES, TILES), np.float32)
    valid[1:, :, 2] = 0
    gate_scale = np.array([1 / 64.] + [1 / 64.] * 3 + [1 / 16.] * 3 + [1 / 4.] * 3, np.float32)
    e0 = np.arange(EXP0, dtype=np.float32)
    e1 = np.arange(EXP1, dtype=np.float32)
    row = np.concatenate([gate_scale, EXP0 - e0, e0 * CAP, EXP1 - e1])
    row = np.broadcast_to(row, (P, row.size))
    token = np.zeros((P, T1))
    for i in range(IMAGES):
        for q in range(2):
            token[:, 2 * i + q] = i * LEN + q * P + k
    token[:IMAGES, T1 - 1] = k[:IMAGES] * LEN + 2 * P
    valid1 = np.ones((P, T1))
    valid1[IMAGES:, T1 - 1] = 0
    bcast = lambda r: np.broadcast_to(np.asarray(r).reshape(-1), (P, np.asarray(r).size))
    g = np.arange(GROUPS)
    misc = np.concatenate([row, valid.reshape(P, -1), np.full((P, 1), 0.5), token, valid1,
                           bcast([EPS, -0.5, 1.5]),
                           bcast(g[:, None] > g[None, :]), bcast(np.arange(T1) * P), bcast(np.arange(NT1)), bcast(k)], 1)
    return {"mats": mats, "rope": rope, "misc": np.ascontiguousarray(misc.astype(np.float32))}


PER_MIX, PER_MIX_ACT = 68, 16
PER_ATT, PER_ATT_ACT = 50, 8
PER_STD, PER_STD4 = 28, 58
M_SCALE, M_FIRST0, M_BASE0, M_FIRST1, M_VALID, M_HALF = 0, 10, 18, 26, 42, 66
M_TOKEN = 67
M_VALID1 = M_TOKEN + T1
M_NEWTON = M_VALID1 + T1
M_LOWER = M_NEWTON + 3
M_STEPS = M_LOWER + GROUPS * GROUPS
M_TILE = M_STEPS + T1
M_LANE = M_TILE + NT1
M_END = M_LANE + P


def build(nc, d, phases=9):
    ctx = ExitStack()
    with ctx:
        def sb(name, shape, dt=F32):
            return ctx.enter_context(nc.sbuf_tensor(name, shape, dt))

        def sem(name):
            return ctx.enter_context(nc.semaphore(name))

        def dram(name, shape, dt=F32):
            return nc.dram_tensor(name, shape, dt, kind="Internal").ap()

        h0_rows = dram("h0_rows", (TOKENS, HID))
        slots0 = dram("slots0", (EXP0 * CAP, HID))
        outs0 = dram("outs0", (EXP0 * CAP, HID))
        n4_rows = dram("n4_rows", (TOKENS, HID))
        last_weights = dram("last_weights", (IMAGES, TOPK))
        outs1 = dram("outs1", (TOPK * TOKENS, HID))

        mats = sb("mats", [P, 4, P])
        ident, before, same_image, ones = (mats[:, k, :] for k in range(4))
        misc = sb("misc_c", [P, M_END])
        big, mid, mix, spare = sb("big", [P, 20480]), sb("mid", [P, 4112]), sb("mix", [P, 10240]), sb("spare", [P, 6144])

        def arena(mem):
            at = [0]

            def part(n, **dims):
                at[0] += n
                assert at[0] <= mem.shape[1], at[0]
                p = mem[:, at[0] - n:at[0]]
                return p.rearrange("p (a b) -> p a b", **dims) if dims else p

            return part

        part = arena(big)

        img = part(2 * 2048).rearrange("p (g r c) -> p g r c", g=2, r=8)
        w_l1 = part(4608).rearrange("p (f j) -> p f j", j=3)
        w_l2 = part(1152).rearrange("p (f j) -> p f j", j=3)
        w_l3 = part(288).rearrange("p (f j) -> p f j", j=3)
        w_a = part(32)
        gbias = part(10)
        sumc = part(1024)
        difc = part(1024)
        A1, A2, A3 = part(512), part(128), part(32)
        B1, B2, B3 = part(1536), part(384), part(96)
        R2, R1 = part(128), part(512)
        A3g = part(32)
        vw = part(512)
        dot_out = part(1536)
        partial = part(20).rearrange("p (g n) -> p g n", g=2)
        gl = part(80).rearrange("p (k n) -> p k n", n=10)
        rec = img
        lnstat = sb("lnstat", [P, 8, 8])
        lnst = sb("lnst", [P, 8, 6])
        normed = part(2048).rearrange("p (r c) -> p r c", r=8)
        cls = part(512)

        nT0 = arena(mid)(HALVES * TOKENS, a=HALVES)
        part = arena(mix)
        w_in = part(HALVES * 2 * INNER, a=HALVES)
        w_dt = part(CH * INNER, a=CH)
        w_xdt = part(CH * INNER, a=CH)
        w_fold = part(CH * INNER, a=CH)
        w_bcr = part(2 * CH * P).rearrange("p (b k m) -> p b k m", b=2, k=CH)
        w_out = part(CH * HID, a=CH)
        w_bc = sb("w_bc", [P, CH, 2 * STATE])
        w_bcs = sb("w_bcs", [P, CH, 2])
        chan = sb("chan", [P, CH, 8])
        part = arena(big)
        conv, xb, soft, dts, al, om, gat, hs = (part(CH * LEN, a=CH) for _ in range(8))
        xconv, zs, es, ys = ([part(CH * LEN, a=CH) for _ in range(2)] for _ in range(4))
        bct = [part(2 * LEN, a=2) for _ in range(2)]
        outT = sb("outT", [P, HALVES, LEN])
        n2T = sb("n2T", [P, HALVES, LEN])
        part = arena(spare)
        rows = part(IMAGES * TILES * HID).rearrange("p (i q c) -> p i q c", i=IMAGES, q=TILES)

        part = arena(mix)
        part(2048)
        w1e, w2e = zip(*[(part(HALVES * DFF, a=HALVES), part(DFF // P * HID, a=DFF // P)) for _ in range(2)])
        part = arena(big)
        b2_rows = part(EXP0 * HID, a=EXP0)
        slot_rows = [part(3 * HID, a=3) for _ in range(2)]
        slotT = [part(HALVES * CAP, a=HALVES) for _ in range(2)]
        hidden = [part(DFF // P * CAP, a=DFF // P) for _ in range(2)]
        expert_rows = [part(3 * HID, a=3) for _ in range(2)]
        r_exp, r_hot, r_cum, r_tmp = (part(IMAGES * TILES * EXP0, a=IMAGES * TILES) for _ in range(4))
        r_one = part(8 * IMAGES * TILES, a=8)
        part = arena(mix)
        w_qkr, w_qk = part(HALVES * 2 * HID, a=HALVES), part(HALVES * 2 * HID, a=HALVES)
        w_v, rope = part(HALVES * HID, a=HALVES), part(HALVES * LEN, a=HALVES)
        bv_rows, qk_bias = part(HID), part(12)
        wg1, ws13, ws2 = part(HALVES * EXP1, a=HALVES), part(HALVES * 2 * DFE, a=HALVES), part(2 * HID, a=2)
        qkT = part(2 * HALVES * LEN, a=2 * HALVES)
        probs, probsT = part(TILES * LEN, a=TILES), part(TILES * LEN, a=TILES)
        soft_c = part(24)
        gated, silu_g = part(TILES * DFE, a=TILES), part(TILES * DFE, a=TILES)
        gatedT = part(2 * LEN, a=2)
        part = arena(mid)
        n3T, n4T = part(HALVES * LEN, a=HALVES), part(HALVES * LEN, a=HALVES)
        vals = [part(TILES * HID, a=TILES) for _ in range(2)]
        turn_src4 = part(TILES * HID, a=TILES)
        logit1 = sb("logit1", [P, T1, EXP1])
        n4T_last = sb("n4T_last", [P, HALVES, IMAGES])
        bias1 = sb("bias1", [P, EXP1])
        part = arena(spare)
        fetched = [part(TILES * HID, a=TILES) for _ in range(2)]
        part = arena(big)
        w13 = part(EXP1 * HALVES * 2 * DFE).rearrange("p (e h n) -> p e h n", e=EXP1, h=HALVES)
        w2s = part(EXP1 * 2 * HID).rearrange("p (e k n) -> p e k n", e=EXP1, k=2)
        part = arena(mix)
        score, biased, left, r1_tmp, sel, place, cumA, cumB = (part(T1 * EXP1, a=T1) for _ in range(8))
        hots = part(TOPK * T1 * EXP1, a=TOPK)
        hots2 = part(TOPK * T1 * EXP1, a=TOPK)
        one_k = part(6 * TOPK * T1, a=6)
        g_all = part(10 * T1 * GROUPS, a=10)
        g_pair = part(2 * T1 * GROUPS * GROUPS, a=2)
        steps_c = part(EXP1 * T1, a=EXP1)
        per_exp = part(6 * EXP1, a=6)
        xg = [part(HID) for _ in range(XR)]
        part = arena(spare)
        tile_cmp = part(NT1 * EXP1, a=NT1)
        lane_hot, tile_hot = [part(TOPK * P, a=TOPK) for _ in range(4)], [part(TOPK * NT1, a=TOPK) for _ in range(4)]
        row_no, slot_lane, slot_tile = (part(TOPK * T1, a=TOPK) for _ in range(3))
        slot_row = part(4 * NT1, a=4)
        part = arena(mid)
        xT1, gT1 = [part(HALVES * P, a=HALVES) for _ in range(2)], [part(2 * P, a=2) for _ in range(2)]
        sg1, gu1 = [part(DFE) for _ in range(2)], [part(DFE) for _ in range(2)]
        y1 = [part(HID) for _ in range(4)]
        part = arena(mix)
        ysum = [part(TOPK * TILES * HID).rearrange("p (k q c) -> p k q c", k=TOPK, q=TILES) for _ in range(2)]
        tile_exp = sb("tile_exp", [1, NT1], U32)
        rec_idx = sb("rec_idx", [P, NT1, 2], U32)
        idx_now = [sb(f"idx_now{k}", [P, 2], U32) for k in range(IDX)]
        tile_no = sb("tile_no", [1, NT1])
        weight1, last_w = sb("weight1", [P, T1, TOPK]), sb("last_w", [1, IMAGES * TOPK])
        b1_cols = sb("b1_cols", [P, EXP0, DFF // P])
        scratch_dve, scratch_pool = sb("scratch_dve", [1, 1]), sb("scratch_pool", [1, 3])
        gl7 = sb("gl7", [P, 1])
        gl8 = sb("gl8", [P, 1])
        from_now = [sb(f"from_now{k}", [P, TILES], U32) for k in range(2)]
        gate0 = sb("gate0", [P, IMAGES * TILES])
        slot_to = sb("slot_to", [P, IMAGES * TILES], U32)
        slot_from = sb("slot_from", [P, IMAGES * TILES], U32)
        turn_src = sb("turn_src", [P, TILES, HID])
        wg0 = sb("wg0", [P, HALVES, EXP0])
        logit0 = sb("logit0", [P, IMAGES, TILES, EXP0])
        h_all = sb("h_all", [P, IMAGES, TILES, HID])

        bank = [ctx.enter_context(nc.psum_tensor(f"bank{k}", [P, 512], F32)) for k in range(8)]

        ld_const, ld_img, ld_wav, ld_mix = sem("ld_const"), [sem("ld_img0"), sem("ld_img1")], sem("ld_wav"), sem("ld_mix")
        dve_done, act_done, pool_done = sem("dve_done"), sem("act_done"), sem("pool_done")
        dots_ready, sums_ready, logit_ready, exp_ready = sem("dots_ready"), sem("sums_ready"), sem("logit_ready"), sem("exp_ready")
        vgated, vin = sem("vgated"), sem("vin")
        var_ready, rstd_ready = sem("var_ready"), sem("rstd_ready")
        rec_ready, rows_stored = sem("rec_ready"), sem("rows_stored")
        normed_ready, turned, turned_out = sem("normed_ready"), sem("turned"), sem("turned_out")
        fold_done, fold_out, bc_summed, bc_ready = sem("fold_done"), sem("fold_out"), sem("bc_summed"), sem("bc_ready")
        stored = sem("stored")
        x_ready, z_ready, tap_done, conv_done, xconv_ready, zs_done = (sem(n) for n in (
            "x_ready", "z_ready", "tap_done", "conv_done", "xconv_ready", "zs_done"))
        y_ready, out_ready, outT_done, tok_ready, res_done = (sem(n) for n in (
            "y_ready", "out_ready", "outT_done", "tok_ready", "res_done"))
        bcsum_ready, bct_done, dt_ready, xb_done, soft_ready, dt_done, e_done = (sem(n) for n in (
            "bcsum_ready", "bct_done", "dt_ready", "xb_done", "soft_ready", "dt_done", "e_done"))
        n2_ready, n2_turned, n2T_done, log_ready, log_saved = (sem(n) for n in (
            "n2_ready", "n2_turned", "n2T_done", "log_ready", "log_saved"))
        (ld_att, fetched_in, h2_done, n3_ready, n3_turned, n3T_done, qk_ready, qk_done, v_ready, v_done, s_ready, m_ready, p_ready, pt_ready, pt_done, o_ready, oT_done, tokens_ready, h3_done, n4_ready, n4_turned, n4T_done, n4_stored, lg1_ready, lg1_saved, gu_ready, sg_done, hs_done, ht_ready, ht_done, mm2_ready, acc_done, w_qk_ready) = (sem(n) for n in (
            "a_ld_att", "a_fetched_in", "a_h2_done", "a_n3_ready", "a_n3_turned", "a_n3T_done", "a_qk_ready", "a_qk_done", "a_v_ready", "a_v_done", "a_s_ready", "a_m_ready", "a_p_ready", "a_pt_ready", "a_pt_done", "a_o_ready", "a_oT_done", "a_tokens_ready", "a_h3_done", "a_n4_ready", "a_n4_turned", "a_n4T_done", "a_n4_stored", "a_lg1_ready", "a_lg1_saved", "a_gu_ready", "a_sg_done", "a_hs_done", "a_ht_ready", "a_ht_done", "a_mm2_ready", "a_acc_done", "a_w_qk_ready"))
        (ld_w1, last_lg, sg_shift, sg_exp, ranks_in, rank_ready, cnt_ready, hots_ready, hots_used, weights_ready, weights_out, last_w_in, idx_ready, idx_copied, x_turned, xT_done, gu1_ready, sg1_done, g1_done, g1_turned, gT_done, y_ready2, y_done, last_stored) = (sem(n) for n in (
            "b_ld_w1", "b_last_lg", "b_sg_shift", "b_sg_exp", "b_ranks_in", "b_rank_ready", "b_cnt_ready", "b_hots_ready", "b_hots_used", "b_weights_ready", "b_weights_out", "b_last_w_in", "b_idx_ready", "b_idx_copied", "b_x_turned", "b_xT_done", "b_gu1_ready", "b_sg1_done", "b_g1_done", "b_g1_turned", "b_gT_done", "b_y_ready2", "b_y_done", "b_last_stored"))
        numbered = sem("numbered")
        y_done2, last_cols = sem("y_done2"), sem("last_cols")
        xg_in, y_sent, ys_in = [sem(f"xg_in{k}") for k in range(XR)], [sem(f"y_sent{k}") for k in range(4)], [sem(f"ys_in{k}") for k in range(2)]
        fetched_in = [sem("fetched_in0"), sem("fetched_in1")]
        h0_loaded, zeroed = sem("h0_loaded"), sem("zeroed")
        zero_ready, slots_zeroed, rows_kept = sem("zero_ready"), sem("slots_zeroed"), sem("rows_kept")
        shift_ready, exps_ready, hot_ready, pos_ready, slots_ready, sent = (sem(n) for n in (
            "shift_ready", "exps_ready", "hot_ready", "pos_ready", "slots_ready", "sent"))
        ld_b, w_loaded, xs_loaded = sem("ld_b"), [sem("w_loaded0"), sem("w_loaded1")], [sem("xs_loaded0"), sem("xs_loaded1")]
        xt_ready, xt_done, hid_ready, hid_done, eo_ready, eo_done = (sem(n) for n in (
            "xt_ready", "xt_done", "hid_ready", "hid_done", "eo_ready", "eo_done"))
        eo_stored = [sem("eo_stored0"), sem("eo_stored1")]

        block = ctx.enter_context(nc.Block())

        @block.sync
        def _(sp):
            sp.dma_start(img[:, 0], d["x"][0:4].rearrange("b (r j) c -> (b r) j c", j=8)).then_inc(ld_img[0], 16)
            sp.dma_start(mats[:], d["mats"]).then_inc(ld_const, 16)
            sp.dma_start(misc[:], d["misc"]).then_inc(ld_const, 16)
            for b in range(4):
                q = slice(32 * b, 32 * b + 32)
                sp.dma_start(w_l1[q].rearrange("p (s f) j -> p s (f j)", s=3),
                             d["Wd3"].rearrange("(s p f) j -> p s (f j)", s=3, p=32)).then_inc(ld_wav, 16)
                sp.dma_start(w_l2[q].rearrange("p (s f) j -> p s (f j)", s=3),
                             d["Wd2"].rearrange("(s p f) j -> p s (f j)", s=3, p=32)).then_inc(ld_wav, 16)
                sp.dma_start(w_l3[q].rearrange("p (s f) j -> p s (f j)", s=3),
                             d["Wd1"].rearrange("(s p f) j -> p s (f j)", s=3, p=32)).then_inc(ld_wav, 16)
                sp.dma_start(w_a[q], d["Wa"].rearrange("(p f) j -> p (f j)", p=32)).then_inc(ld_wav, 16)
            sp.dma_start(gbias, d["gbias"].partition_broadcast(P)).then_inc(ld_wav, 16)
            sp.dma_start(cls[0:1, 0:HID], d["cls_tok"]).then_inc(ld_wav, 16)
            sp.dma_start(img[:, 1], d["x"][4:8].rearrange("b (r j) c -> (b r) j c", j=8)).then_inc(ld_img[1], 16)
            for t, n in ((w_xdt, "w_xdt"), (w_dt, "w_dt"), (w_bc, "w_bc"), (w_in, "w_in"), (chan, "chan"), (w_out, "w_out"), (wg0, "wg0")):
                sp.dma_start(t[:], d[n]).then_inc(ld_mix, 16)
            for b in range(IMAGES):
                sp.dma_start(h0_rows[b * LEN:b * LEN + 1, :], d["cls_tok"]).then_inc(rows_stored, 16)
            for g in range(2):
                sp.wait_ge(rec_ready, g + 1)
                for b in range(4):
                    first = (4 * g + b) * LEN + 1
                    sp.dma_start(h0_rows[first:first + SIDE, :].rearrange("(r j) c -> r j c", j=8),
                                 rec[32 * b:32 * b + 32, g]).then_inc(rows_stored, 16)
            sp.wait_ge(rows_stored, 16 * 16)
            sp.wait_ge(zero_ready, 1)
            sp.dma_start(slots0.rearrange("(p r) c -> p (r c)", p=CAPP),
                         rows[0:CAPP].rearrange("p i q c -> p (i q c)")).then_inc(slots_zeroed, 16)
            sp.wait_ge(zeroed, 1)
            by_image = h0_rows.rearrange("(i t) c -> t i c", t=LEN)
            for q in range(2):
                sp.dma_start(h_all[:, :, q], by_image[q * P:(q + 1) * P]).then_inc(h0_loaded, 16)
            sp.dma_start(h_all[0:1, :, 2], by_image[2 * P:LEN]).then_inc(h0_loaded, 16)
            def load_weights(e, par):
                sp.dma_start(w1e[par].rearrange("p a b -> p (a b)"),
                             d["w1"][ds(e, 1)].rearrange("e p n -> (e p) n")).then_inc(w_loaded[par], 16)
                sp.dma_start(w2e[par].rearrange("p a b -> p (a b)"),
                             d["w2"][ds(e, 1)].rearrange("e p n -> (e p) n")).then_inc(w_loaded[par], 16)

            def load_slots(e, par):
                sp.dma_start(slot_rows[par][0:CAPP],
                             slots0[ds(e * CAP, CAP)].rearrange("(q p) c -> p q c", p=CAPP)).then_inc(xs_loaded[par], 16)

            def store_expert(e, par):
                sp.wait_ge(eo_done, e + 1)
                sp.dma_start(outs0[ds(e * CAP, CAP)].rearrange("(q p) c -> p q c", p=CAPP),
                             expert_rows[par][0:CAPP]).then_inc(eo_stored[par], 16)

            def expert(e, par):
                store_expert(e, par)
                load_weights(e + 2, par)
                load_slots(e + 2, par)

            sp.wait_ge(fold_done, CH)
            sp.wait_ge(bc_ready, 1)
            load_weights(0, 0)
            sp.wait_ge(log_saved, IMAGES)
            load_weights(1, 1)
            sp.dma_start(b2_rows.rearrange("p a b -> p (a b)"), d["b2"].partition_broadcast(P)).then_inc(ld_b, 16)
            sp.dma_start(b1_cols[:], d["b1"]).then_inc(ld_b, 16)
            sp.wait_ge(sent, 16 * IMAGES * TILES)
            load_slots(0, 0)
            load_slots(1, 1)
            staged(sp, 0, EXP0 - 3, expert)
            store_expert(EXP0 - 2, 0)
            store_expert(EXP0 - 1, 1)
            for par in range(2):
                sp.wait_ge(eo_stored[par], 16 * EXP0 // 2)
            if phases == 3:
                sp.dma_start(d["out"][0:EXP0 * CAP, :], outs0).then_inc(stored, 16)
                sp.dma_start(d["out"][2568:2568+128, 0:24], slot_from[:].bitcast(F32)).then_inc(stored, 16)
                sp.dma_start(d["out"][2568:2568+128, 24:48], gate0[:]).then_inc(stored, 16)
                sp.wait_ge(stored, 48)

            sp.wait_ge(eo_ready, EXP0)
            for t, n in ((w_qkr, "w_qk"), (w_v, "w_v"), (rope, "rope"), (wg1, "wg1"), (ws13, "ws13")):
                sp.dma_start(t, d[n]).then_inc(ld_att, 16)
            sp.dma_start(ws2[0:DK], d["ws2"]).then_inc(ld_att, 16)
            sp.dma_start(qk_bias, d["qk_bias"]).then_inc(ld_att, 16)
            sp.dma_start(bv_rows, d["bv"].partition_broadcast(P)).then_inc(ld_att, 16)
            sp.dma_start(bias1[:], d["gate_bias"].partition_broadcast(P)).then_inc(ld_w1, 16)
            sp.dma_start(w13.rearrange("p e h n -> p (e h n)"), d["w13"]).then_inc(ld_w1, 16)
            sp.dma_start(w2s[0:DK].rearrange("p e k n -> p (e k n)"), d["w2s"]).then_inc(ld_w1, 16)

            def store_norm(i, par):
                sp.wait_ge(n4_ready, i + 1)
                sp.dma_start(n4_rows[ds(i * LEN, 2 * P)].rearrange("(q p) c -> p q c", p=P),
                             turn_src4[:, 0:2]).then_inc(n4_stored, 16)
                sp.dma_start(n4_rows[ds(i * LEN + 2 * P, 1)], turn_src4[0:1, 2]).then_inc(n4_stored, 16)

            staged(sp, 0, IMAGES - 1, store_norm)
            sp.wait_ge(n4_stored, 32 * IMAGES)
            if phases == 4:
                sp.wait_ge(acc_done, IMAGES)
                sp.dma_start(d["out"][:, 0:6144], h_all[:].rearrange("p i q c -> p (i q c)")).then_inc(stored, 16)
                sp.dma_start(d["out"][:, 6144:6528], logit1.rearrange("p q e -> p (q e)")).then_inc(stored, 16)
                sp.wait_ge(stored, 32)

            sp.wait_ge(weights_ready, 1)
            sp.dma_start(last_weights, weight1[0:IMAGES, T1 - 1, :]).then_inc(weights_out, 16)
            sp.wait_ge(weights_out, 16)
            sp.dma_start(last_w[:], last_weights.rearrange("(o i) k -> o (i k)", o=1)).then_inc(last_w_in, 16)
            for k in range(4):
                sp.wait_ge(y_sent[k], 16 * NT1 // 4)
            y_rows = outs1.rearrange("(k i t) c -> i t k c", k=TOPK, t=LEN)
            o_rows = d["out"].rearrange("(i t) c -> i t c", t=LEN)

            def load_sum(i, par):
                for q in range(2):
                    sp.dma_start(ysum[par][:, :, q], y_rows[ds(i, 1), q * P:(q + 1) * P].rearrange(
                        "i t k c -> (i t) k c")).then_inc(ys_in[par], 16)
                sp.dma_start(ysum[par][0:1, :, 2], y_rows[ds(i, 1), 2 * P:LEN].rearrange(
                    "i t k c -> (i t) k c")).then_inc(ys_in[par], 16)

            def store_out(i):
                sp.wait_ge(y_done2, i + 1)
                sp.dma_start(o_rows[ds(i, 1), 0:2 * P].rearrange("i (q p) c -> p (i q) c", p=P),
                             h_all[:, ds(i, 1), 0:2].rearrange("p i q c -> p (i q) c")).then_inc(stored, 16)
                sp.dma_start(o_rows[ds(i, 1), 2 * P:LEN].rearrange("i t c -> (i t) c"),
                             h_all[0:1, ds(i, 1), 2].rearrange("p i c -> p (i c)")).then_inc(stored, 16)

            def finish(i, par):
                store_out(i)
                load_sum(i + 2, par)

            load_sum(0, 0)
            load_sum(1, 1)
            staged(sp, 0, IMAGES - 3, finish)
            store_out(IMAGES - 2)
            store_out(IMAGES - 1)
            sp.wait_ge(stored, 32 * IMAGES)

        @block.vector
        def _(dve):
            v = Signals(dve_done)
            lns = Signals(var_ready)

            def run(ins):
                v.on(ins)

            def chain():
                dve.wait_ge(dve_done, v.now())

            def tt(o, a, b, op):
                run(nc.vector.tensor_tensor(o, a, b, op))

            def haar(cur, R, C, bands, A):
                pairs = cur.rearrange("p r (c t) -> p r c t", t=2)
                s = sumc[:, 0:R * C // 2].rearrange("p (r c) -> p r c", r=R)
                f = difc[:, 0:R * C // 2].rearrange("p (r c) -> p r c", r=R)
                tt(s, pairs[:, :, :, 0], pairs[:, :, :, 1], ALU.add)
                tt(f, pairs[:, :, :, 0], pairs[:, :, :, 1], ALU.subtract)
                chain()
                s2 = s.rearrange("p (r t) c -> p t r c", t=2)
                f2 = f.rearrange("p (r t) c -> p t r c", t=2)
                bv = bands.rearrange("p (s r c) -> p s r c", s=3, r=R // 2)
                Av = A.rearrange("p (r c) -> p r c", r=R // 2)
                tt(Av, s2[:, 0], s2[:, 1], ALU.add)
                tt(bv[:, 0], s2[:, 0], s2[:, 1], ALU.subtract)
                tt(bv[:, 1], f2[:, 0], f2[:, 1], ALU.add)
                tt(bv[:, 2], f2[:, 0], f2[:, 1], ALU.subtract)
                chain()
                return Av

            def ihaar(cur, R, C, bands, lev, out):
                bv = bands.rearrange("p (s r c) -> p s r c", s=3, r=R)
                g = lambda k, s: gl[:, 4 + (s < 0), 1 + 3 * lev + k:2 + 3 * lev + k]
                lo = sumc[:, 0:2 * R * C].rearrange("p (r t c) -> p t r c", t=2, c=C)
                hi = difc[:, 0:2 * R * C].rearrange("p (r t c) -> p t r c", t=2, c=C)
                vv = vw[:, 0:R * C].rearrange("p (r c) -> p r c", r=R)
                run(nc.vector.tensor_scalar(vv, bv[:, 1], g(1, 1), None, ALU.mult))
                run(nc.vector.scalar_tensor_tensor(lo[:, 0], bv[:, 0], g(0, 1), cur, ALU.mult, ALU.add))
                run(nc.vector.scalar_tensor_tensor(lo[:, 1], bv[:, 0], g(0, -1), cur, ALU.mult, ALU.add))
                chain()
                run(nc.vector.scalar_tensor_tensor(hi[:, 0], bv[:, 2], g(2, 1), vv, ALU.mult, ALU.add))
                run(nc.vector.scalar_tensor_tensor(hi[:, 1], bv[:, 2], g(2, -1), vv, ALU.mult, ALU.add))
                chain()
                lo = sumc[:, 0:2 * R * C].rearrange("p (r c) -> p r c", c=C)
                hi = difc[:, 0:2 * R * C].rearrange("p (r c) -> p r c", c=C)
                pairs = out.rearrange("p r (c t) -> p r c t", t=2)
                tt(pairs[:, :, :, 0], lo, hi, ALU.add)
                tt(pairs[:, :, :, 1], lo, hi, ALU.subtract)
                chain()

            def settle():
                nc.vector.memset(scratch_dve[:], 0.0)

            def statistics(src, n, rows=P, at=0):
                st, ag = lnst[0:rows, at:at + n], lnstat[0:rows, at:at + n]
                settle()
                for k in range(n):
                    run(nc.vector.bn_stats(st[:, k, :], src[:, k, :]))
                chain()
                settle()
                for k in range(n):
                    last = nc.vector.bn_aggr(ag[:, k, 0:2], st[:, k, :])
                    if k < n - 1:
                        run(last)
                last.then_inc(var_ready, 1)
                lns.k += 1
                return lns.now()

            def normalise(dst, src, n, count, rows=P, ends=None, at=0):
                dve.wait_ge(rstd_ready, count)
                ag = lnstat[0:rows, at:at + n]
                for k in range(n):
                    ins = nc.vector.tensor_scalar(dst[:, k, :], src[:, k, :], ag[:, k, 0:1], ag[:, k, 2:3],
                                                  ALU.subtract, ALU.mult)
                    if k == n - 1 and ends is not None:
                        ins.then_inc(ends, 1)
                    else:
                        run(ins)

            def layernorm(dst, src, n, rows=P, ends=None):
                normalise(dst, src, n, statistics(src, n, rows), rows, ends)

            dve.wait_ge(ld_const, 32)
            dve.wait_ge(ld_wav, 18 * 16)
            layernorm(cls[0:1, HID:2 * HID].rearrange("p (k c) -> p k c", k=1),
                      cls[0:1, 0:HID].rearrange("p (k c) -> p k c", k=1), 1, 1)
            chain()
            nc.vector.tensor_copy(gl[0:1, 7, 0:1], cls[0:1, 0:1]).then_inc(normed_ready, 1)
            for g in range(2):
                dve.wait_ge(ld_img[g], 16)
                a1 = haar(img[:, g], 8, 256, B1, A1)
                a2 = haar(a1, 4, 128, B2, A2)
                haar(a2, 2, 64, B3, A3)
                pt = partial[:, g]
                last = None
                for col, (b, w, n, s) in enumerate(
                        [(A3, w_a, 32, 1 / 8)] + [(B3, w_l3[:, :, j], 96, 1 / 8) for j in range(3)]
                        + [(B2, w_l2[:, :, j], 384, 1 / 4) for j in range(3)]
                        + [(B1, w_l1[:, :, j], 1536, 1 / 2) for j in range(3)]):
                    last = nc.vector.tensor_tensor_reduce(dot_out[:, 0:n], b, w, s, 0.0, ALU.mult, ALU.add,
                                                          pt[:, col:col + 1])
                    if col < 9:
                        run(last)
                        chain()
                last.then_inc(dots_ready, 1)
                dve.wait_ge(sums_ready, g + 1)
                lg, ex = gl[:, 0], gl[:, 1]
                tt(lg, bank[0][:, 0:10], gbias, ALU.add)
                chain()
                l9 = lg[:, 1:10].rearrange("p (l k) -> p l k", k=3)
                run(nc.vector.tensor_reduce(gl[:, 2, 0:3], l9, AX.X, ALU.max))
                chain()
                tt(l9, l9, gl[:, 2, 0:3].unsqueeze(2).broadcast_to([P, 3, 3]), ALU.subtract)
                nc.vector.tensor_scalar(lg[:, 0:1], lg[:, 0:1], -1.0, None, ALU.mult).then_inc(logit_ready, 1)
                dve.wait_ge(exp_ready, g + 1)
                e9 = ex[:, 1:10].rearrange("p (l k) -> p l k", k=3)
                run(nc.vector.tensor_reduce(gl[:, 3, 0:3], e9, AX.X, ALU.add))
                run(nc.vector.tensor_scalar(gl[:, 3, 3:4], ex[:, 0:1], 1.0, None, ALU.add))
                chain()
                run(nc.vector.reciprocal(gl[:, 3, 4:8], gl[:, 3, 0:4]))
                run(nc.vector.memset(ex[:, 0:1], 1.0))
                chain()
                tt(gl[:, 4, 1:10].rearrange("p (l k) -> p l k", k=3), e9,
                   gl[:, 3, 4:7].unsqueeze(2).broadcast_to([P, 3, 3]), ALU.mult)
                run(nc.vector.tensor_copy(gl[:, 4, 0:1], gl[:, 3, 7:8]))
                chain()
                tt(gl[:, 4], gl[:, 4], misc[:, M_SCALE:M_SCALE + 10], ALU.mult)
                chain()
                run(nc.vector.tensor_scalar(gl[:, 5], gl[:, 4], -1.0, None, ALU.mult))
                run(nc.vector.tensor_scalar(A3g, A3, gl[:, 4, 0:1], None, ALU.mult))
                chain()
                ihaar(A3g.rearrange("p (r c) -> p r c", r=1), 1, 32, B3, 0, R2.rearrange("p (r c) -> p r c", r=2))
                ihaar(R2.rearrange("p (r c) -> p r c", r=2), 2, 64, B2, 1, R1.rearrange("p (r c) -> p r c", r=4))
                ihaar(R1.rearrange("p (r c) -> p r c", r=4), 4, 128, B1, 2, rec[:, g])
                nc.vector.tensor_copy(gl[:, 7, 0:1], rec[:, g, 7, 255:256]).then_inc(rec_ready, 1)
                if g == 1:
                    dve.wait_ge(turned, 1 + 4)
                layernorm(normed, rec[:, g], 8)
                chain()
                nc.vector.tensor_copy(gl[:, 7, 1:2], normed[:, 7, 255:256]).then_inc(normed_ready, 1)
            dve.wait_ge(ld_mix, 7 * 16)
            run(nc.vector.tensor_reduce(w_bcs[:], w_bc[:].rearrange("p k (b s) -> p k b s", s=STATE), AX.X, ALU.add))
            chain()
            for b in range(2):
                run(nc.vector.tensor_copy(w_bcr[:, b], w_bcs[:, :, b:b + 1].broadcast_to([P, CH, P])))
            chain()
            nc.vector.tensor_copy(gl[:, 7, 2:3], w_bcr[:, 1, 0, 0:1]).then_inc(bc_ready, 1)
            if phases == 1:
                return

            def taps(n, pair):
                for k in (2, 1, 0):
                    off = TAPS - 1 - k
                    for c in pair:
                        if k == 2:
                            dve.wait_ge(tap_done, 4 * n + (c + 1))
                        ins = nc.vector.scalar_tensor_tensor(conv[:, c, off:LEN], bank[c][:, 0:LEN - off],
                                                             chan[:, c, k:k + 1], conv[:, c, off:LEN], ALU.mult, ALU.add)
                        if k == 0 and c == pair[-1]:
                            ins.then_inc(conv_done, 1)
                        else:
                            run(ins)
                    if k:
                        chain()

            def step_size(i, par):
                dve.wait_ge(soft_ready, i + 1)
                nc.vector.scalar_tensor_tensor(dts, xb, 0.0, soft, ALU.max, ALU.subtract).then_inc(dt_done, 1)
                run(nc.vector.tensor_scalar(bct[par][:, 0], bct[par][:, 0], -0.25, -0.25, ALU.mult, ALU.add))
                run(nc.vector.tensor_scalar(bct[par][:, 1], bct[par][:, 1], 0.5, 0.5, ALU.mult, ALU.add))

            def gate(par, b):
                return bct[par][:, b:b + 1, :].broadcast_to([P, CH, LEN])

            def recur(i, par):
                chain()
                tt(gat, xconv[par], gate(par, 0), ALU.mult)
                dve.wait_ge(e_done, i + 1)
                run(nc.vector.tensor_scalar(al, es[par], 0.5, 0.5, ALU.mult, ALU.add))
                chain()
                run(nc.vector.scalar_tensor_tensor(gat, es[par], 1.0, gat, ALU.subtract, ALU.mult))
                run(nc.vector.tensor_scalar(al, al, 0.01, 0.99, ALU.max, ALU.min))
                chain()
                for c in range(CH):
                    run(nc.vector.tensor_tensor_scan(hs[:, c], al[:, c], gat[:, c], 0.0, ALU.mult, ALU.add))

            def read_out(i, par):
                chain()
                tt(hs, hs, gate(par, 1), ALU.mult)
                chain()
                for c in range(CH):
                    run(nc.vector.scalar_tensor_tensor(hs[:, c], xconv[par][:, c], chan[:, c, 6:7], hs[:, c],
                                                       ALU.mult, ALU.add))
                chain()
                after(dve, out_ready, 2 * i - 2)
                nc.vector.tensor_tensor(ys[par], hs, zs[par], ALU.mult).then_inc(y_ready, 1)

            def rows_of(i):
                return h_all[:, ds(i, 1)].rearrange("p i q c -> p (i q) c")

            def residual(i):
                dve.wait_ge(tok_ready, i + 1)
                pair = bank[2][:, :].rearrange("p (q c) -> p q c", q=2)
                h2 = h_all[:, ds(i, 1), 0:2].rearrange("p i q c -> p (i q) c")
                h3 = h_all[0:1, ds(i, 1), 2].rearrange("p i c -> p (i c)")
                tt(h2, h2, pair, ALU.add)
                nc.vector.tensor_tensor(h3, h3, bank[3][0:1, 0:HID], ALU.add).then_inc(res_done, 1)
                dve.wait_ge(res_done, i + 1)
                return statistics(rows_of(i), TILES)

            def save_logits(i):
                dve.wait_ge(log_ready, i + 1)
                lg = bank[3][:, 300:300 + TILES * EXP0].rearrange("p (q e) -> p q e", q=TILES)
                run(nc.vector.tensor_copy(logit0[:, ds(i, 1), 0:2].rearrange("p i q e -> p (i q) e"), lg[:, 0:2]))
                nc.vector.tensor_copy(logit0[0:1, ds(i, 1), 2].rearrange("p i e -> p (i e)"), lg[0:1, 2]).then_inc(log_saved, 1)

            dve.wait_ge(h0_loaded, 48)

            def stage(n, par, a=True, b=True, c=True, d=True):
                if a:
                    taps(n, (0, 1))
                if d:
                    save_logits(n - 3)
                if a:
                    taps(n, (2, 3))
                if b:
                    step_size(n - 1, 1 - par)
                    recur(n - 1, 1 - par)
                if c:
                    count = residual(n - 2)
                if b:
                    read_out(n - 1, 1 - par)
                if c:
                    after(dve, rows_kept, n - 2)
                    after(dve, n2_turned, n - 2)
                    normalise(turn_src, rows_of(n - 2), TILES, count, ends=n2_ready)

            stage(0, 0, b=False, c=False, d=False)
            stage(1, 1, c=False, d=False)
            stage(2, 0, d=False)
            staged(dve, 3, 6, stage, ((v, PER_MIX), (lns, 2)))
            stage(7, 1)
            stage(IMAGES, 0, a=False)
            stage(IMAGES + 1, 1, a=False, b=False)
            stage(IMAGES + 2, 0, a=False, b=False, c=False)

            T0 = IMAGES * TILES
            wide = lambda a: a.unsqueeze(2).broadcast_to([P, T0, EXP0])
            row_of = lambda off, n: misc[:, off:off + n].unsqueeze(1).broadcast_to([P, T0, n])
            lg = logit0[:].rearrange("p i q e -> p (i q) e")
            valid = misc[:, M_VALID:M_VALID + T0]
            mx, sm, posv, basev, keep, dest = (r_one[:, k] for k in range(6))
            chain()
            dve.wait_ge(log_saved, IMAGES)
            run(nc.vector.tensor_reduce(mx, lg, AX.X, ALU.max))
            chain()
            nc.vector.tensor_tensor(r_exp, lg, wide(mx), ALU.subtract).then_inc(shift_ready, 1)
            tt(r_hot, lg, wide(mx), ALU.is_equal)
            chain()
            tt(r_hot, r_hot, row_of(M_FIRST0, EXP0), ALU.mult)
            chain()
            run(nc.vector.tensor_reduce(mx, r_hot, AX.X, ALU.max))
            chain()
            tt(r_hot, r_hot, wide(mx), ALU.is_equal)
            chain()
            tt(r_hot, r_hot, wide(valid), ALU.mult)
            chain()

            def earlier_tiles(hot, a, b, n):
                run(nc.vector.memset(a[:, 0:1], 0.0))
                run(nc.vector.tensor_copy(a[:, 1:n], hot[:, 0:n - 1]))
                chain()
                step = 1
                while step < n:
                    tt(b[:, step:n], a[:, step:n], a[:, 0:n - step], ALU.add)
                    run(nc.vector.tensor_copy(b[:, 0:step], a[:, 0:step]))
                    chain()
                    a, b, step = b, a, 2 * step
                return a

            cum = earlier_tiles(r_hot, r_cum, r_tmp, T0)
            assert cum is r_tmp
            nc.vector.tensor_copy(gl7[:], r_hot[:, 0, 0:1]).then_inc(hot_ready, 1)
            dve.wait_ge(exps_ready, 1)
            run(nc.vector.tensor_reduce(sm, r_exp, AX.X, ALU.add))
            tt(r_cum, r_hot, row_of(M_BASE0, EXP0), ALU.mult)
            chain()
            run(nc.vector.reciprocal(sm, sm))
            run(nc.vector.tensor_reduce(basev, r_cum, AX.X, ALU.add))
            dve.wait_ge(pos_ready, 1)
            chain()
            tt(r_cum, r_hot, bank[0][:, 0:T0 * EXP0].rearrange("p (t e) -> p t e", e=EXP0), ALU.mult)
            chain()
            run(nc.vector.tensor_reduce(posv, r_cum, AX.X, ALU.add))
            chain()
            run(nc.vector.tensor_scalar(keep, posv, float(CAP), None, ALU.is_lt))
            tt(dest, posv, basev, ALU.add)
            chain()
            tt(keep, keep, valid, ALU.mult)
            chain()
            tt(gate0[:], sm, keep, ALU.mult)
            tt(posv, dest, keep, ALU.mult)
            run(nc.vector.scalar_tensor_tensor(dest, dest, -FAR, keep, ALU.add, ALU.mult))
            chain()
            run(nc.vector.tensor_copy(slot_from[:], posv))
            nc.vector.tensor_scalar(slot_to[:], dest, FAR, None, ALU.add).then_inc(slots_ready, 1)

            def slots_out(e, par):
                dve.wait_ge(xt_ready, e + 1)
                run(nc.vector.tensor_copy(slotT[par][:, 0], bank[0][:, 0:CAP]))
                nc.vector.tensor_copy(slotT[par][:, 1], bank[1][:, 0:CAP]).then_inc(xt_done, 1)

            def expert(e, par, more=True):
                if more:
                    slots_out(e + 1, 1 - par)
                dve.wait_ge(eo_ready, e + 1)
                after(dve, eo_stored[par], 8 * (e - par))
                b2 = b2_rows[0:CAPP, ds(e, 1), :]
                run(nc.vector.tensor_tensor(expert_rows[par][0:CAPP, 0:2],
                                            bank[6][0:CAPP, :].rearrange("p (q c) -> p q c", q=2),
                                            b2.broadcast_to([CAPP, 2, HID]), ALU.add))
                nc.vector.tensor_tensor(expert_rows[par][0:CAPP, 2:3], bank[7][0:CAPP, 0:HID].unsqueeze(1), b2,
                                        ALU.add).then_inc(eo_done, 1)

            dve.wait_ge(ld_b, 32)
            slots_out(0, 0)
            expert(0, 0)
            expert(1, 1)
            staged(dve, 2, 5, expert, ((v, 4),))
            expert(6, 0)
            expert(7, 1, more=False)

            dve.wait_ge(ld_att, 16 * 8)
            raw, fold = (w.rearrange("p h (o t) -> p (h o) t", t=2) for w in (w_qkr, w_qk))
            tt(fold[:, :, 0], raw[:, :, 0], raw[:, :, 1], ALU.subtract)
            tt(fold[:, :, 1], raw[:, :, 0], raw[:, :, 1], ALU.add)
            run(nc.vector.scalar_tensor_tensor(qk_bias[:, 0:4], qk_bias[:, 4:8], qk_bias[:, 8:9], qk_bias[:, 0:4],
                                               ALU.mult, ALU.add))
            chain()
            run(nc.vector.memset(logit1[:], 0.0))
            nc.vector.tensor_copy(gl7[:], w_qk[:, 1, 511:512]).then_inc(w_qk_ready, 1)

            def combine(i, par):
                dve.wait_ge(fetched_in[par], 24 * (i + (2 - par)))
                for q in range(TILES):
                    k = ROWS[q]
                    h = h_all[0:k, ds(i, 1), q].rearrange("p i c -> p (i c)")
                    g = gate0[0:k, ds(i * TILES + q, 1)]
                    ins = nc.vector.scalar_tensor_tensor(h, fetched[par][0:k, q], g, h, ALU.mult, ALU.add)
                    run(ins) if q < TILES - 1 else ins.then_inc(h2_done, 1)
                after(dve, h2_done, i + 1)
                return statistics(rows_of(i), TILES, at=4)

            def combined(i, count):
                after(dve, n3_turned, i)
                normalise(turn_src, rows_of(i), TILES, count, ends=n3_ready, at=4)

            def maxima(i, par):
                for q in range(TILES):
                    k = ROWS[q]
                    dve.wait_ge(s_ready, 3 * i + (q + 1))
                    if q == 0:
                        after(dve, p_ready, 3 * i)
                    run(nc.vector.tensor_reduce(soft_c[0:k, q:q + 1], bank[2 + q][0:k, 0:LEN], AX.X, ALU.max))
                chain()
                for q in range(TILES):
                    k = ROWS[q]
                    nc.vector.tensor_scalar(soft_c[0:k, 3 + q:4 + q], soft_c[0:k, q:q + 1], -float(HEAD) ** -0.5, None,
                                            ALU.mult).then_inc(m_ready, 1)

            def rotate(n, quarters):
                after(dve, s_ready, 3 * n)
                for g in quarters:
                    dve.wait_ge(qk_ready, 4 * n + (g + 1))
                    nc.vector.scalar_tensor_tensor(qkT[:, g], bank[g % 2][:, 0:LEN], qk_bias[:, g:g + 1],
                                                   rope[:, g % 2], ALU.add, ALU.mult).then_inc(qk_done, 1)

            def shared_gate(j, par):
                dve.wait_ge(lg1_ready, j + 1)
                lg = bank[7][:, 300:300 + 2 * EXP1].rearrange("p (q e) -> p q e", q=2)
                nc.vector.tensor_copy(logit1[:, ds(j * 2, 2)], lg[:, 0:2]).then_inc(lg1_saved, 1)
                after(dve, ht_ready, 2 * j)
                for q in range(TILES):
                    k = ROWS[q]
                    dve.wait_ge(sg_done, 3 * j + (q + 1))
                    nc.vector.tensor_tensor(gated[0:k, q], silu_g[0:k, q], bank[6 + q % 2][0:k, DFE:2 * DFE],
                                            ALU.mult).then_inc(hs_done, 1)

            def values(n, par):
                dve.wait_ge(v_ready, n + 1)
                after(dve, o_ready, 2 * n - 2)
                run(nc.vector.tensor_tensor(vals[par][:, 0:2], bank[0][:, :].rearrange("p (q c) -> p q c", q=2),
                                            bv_rows.unsqueeze(1).broadcast_to([P, 2, HID]), ALU.add))
                nc.vector.tensor_tensor(vals[par][0:1, 2], bank[1][0:1, 0:HID], bv_rows[0:1], ALU.add).then_inc(v_done, 1)

            def shared_out(j, par):
                dve.wait_ge(mm2_ready, j + 1)
                h2 = h_all[:, ds(j, 1), 0:2].rearrange("p i q c -> p (i q) c")
                h3 = h_all[0:1, ds(j, 1), 2].rearrange("p i c -> p (i c)")
                run(nc.vector.tensor_tensor(h2, h2, bank[6][:, :].rearrange("p (q c) -> p q c", q=2), ALU.add))
                nc.vector.tensor_tensor(h3, h3, bank[7][0:1, 0:HID], ALU.add).then_inc(acc_done, 1)

            def attended(i, par):
                dve.wait_ge(tokens_ready, i + 1)
                dve.wait_ge(p_ready, 3 * i + 3)
                run(nc.vector.reciprocal(soft_c[:, 9:11], soft_c[:, 6:8]))
                run(nc.vector.reciprocal(soft_c[0:1, 11:12], soft_c[0:1, 8:9]))
                chain()
                for q in range(TILES):
                    k = ROWS[q]
                    h = h_all[0:k, ds(i, 1), q].rearrange("p i c -> p (i c)")
                    o = bank[2][0:k, q * HID:(q + 1) * HID] if q < 2 else bank[3][0:1, 0:HID]
                    ins = nc.vector.scalar_tensor_tensor(h, o, soft_c[0:k, 9 + q:10 + q], h, ALU.mult, ALU.add)
                    run(ins) if q < TILES - 1 else ins.then_inc(h3_done, 1)
                after(dve, h3_done, i + 1)
                statistics(rows_of(i), TILES)

            def attended_norm(i, count):
                after(dve, n4_turned, i)
                after(dve, n4_stored, 32 * i)
                normalise(turn_src4, rows_of(i), TILES, count, ends=n4_ready)

            def stage(n, par, a=True, b=True, c=True, ahead=True):
                if b:
                    maxima(n - 1, 1 - par)
                if a:
                    rotate(n, (0, 1))
                if c:
                    attended_norm(n - 2, lns.now())
                if a:
                    rotate(n, (2, 3))
                if c:
                    shared_gate(n - 2, par)
                if ahead:
                    ahead_count = combine(n + 1, 1 - par)
                if a:
                    values(n, par)
                if ahead:
                    combined(n + 1, ahead_count)
                if c:
                    shared_out(n - 2, par)
                if b:
                    attended(n - 1, 1 - par)

            combined(0, combine(0, 0))
            stage(0, 0, b=False, c=False)
            stage(1, 1, c=False)
            stage(2, 0)
            staged(dve, 3, 6, stage, ((v, PER_ATT), (lns, 4)))
            stage(7, 1, ahead=False)
            stage(8, 0, a=False, ahead=False)
            stage(9, 1, a=False, b=False, ahead=False)

            dve.wait_ge(ld_w1, 48)
            dve.wait_ge(last_lg, 1)
            run(nc.vector.tensor_copy(logit1[0:IMAGES, T1 - 1], bank[0][0:IMAGES, 0:EXP1]))
            chain()
            nc.vector.tensor_scalar(score, logit1[:], -1.0, None, ALU.mult).then_inc(sg_shift, 1)
            dve.wait_ge(sg_exp, 1)
            run(nc.vector.tensor_scalar(score, score, 1.0, None, ALU.add))
            chain()
            run(nc.vector.reciprocal(score, score))
            chain()
            tt(biased, score, bias1[:].unsqueeze(1).broadcast_to([P, T1, EXP1]), ALU.add)
            chain()
            quad = biased.rearrange("p t (g k) -> p (t g) k", g=GROUPS)
            hi1, lo1, hi2, lo2, top, mid_, low, gsum, gkeep, gpen = (g_all[:, k] for k in range(10))
            tt(hi1, quad[:, :, 0], quad[:, :, 1], ALU.max)
            tt(lo1, quad[:, :, 0], quad[:, :, 1], ALU.min)
            tt(hi2, quad[:, :, 2], quad[:, :, 3], ALU.max)
            tt(lo2, quad[:, :, 2], quad[:, :, 3], ALU.min)
            chain()
            tt(top, hi1, hi2, ALU.max)
            tt(mid_, hi1, hi2, ALU.min)
            tt(low, lo1, lo2, ALU.max)
            chain()
            tt(mid_, mid_, low, ALU.max)
            chain()
            tt(gsum, top, mid_, ALU.add)
            chain()
            gs = gsum.rearrange("p (t g) -> p t g", g=GROUPS)
            other = gs.unsqueeze(2).broadcast_to([P, T1, GROUPS, GROUPS])
            own = gs.unsqueeze(3).broadcast_to([P, T1, GROUPS, GROUPS])
            cmp = g_pair[:, 0].rearrange("p (t g k) -> p t g k", t=T1, g=GROUPS)
            same = g_pair[:, 1].rearrange("p (t g k) -> p t g k", t=T1, g=GROUPS)
            tt(cmp, other, own, ALU.is_gt)
            tt(same, other, own, ALU.is_equal)
            chain()
            tt(g_pair[:, 1].rearrange("p (t n) -> p t n", t=T1), g_pair[:, 1].rearrange("p (t n) -> p t n", t=T1),
               misc[:, M_LOWER:M_LOWER + GROUPS * GROUPS].unsqueeze(1).broadcast_to([P, T1, GROUPS * GROUPS]), ALU.mult)
            chain()
            tt(g_pair[:, 0], g_pair[:, 0], g_pair[:, 1], ALU.add)
            chain()
            run(nc.vector.tensor_reduce(gkeep, g_pair[:, 0].rearrange("p (n k) -> p n k", k=GROUPS), AX.X, ALU.add))
            chain()
            run(nc.vector.tensor_scalar(gkeep, gkeep, 2.0, None, ALU.is_lt))
            chain()
            run(nc.vector.tensor_scalar(gpen, gkeep, LOW, LOW, ALU.mult, ALU.subtract))
            four = lambda a: a.unsqueeze(2).broadcast_to([P, T1 * GROUPS, GROUPS])
            leftq = left.rearrange("p t (g k) -> p (t g) k", g=GROUPS)
            tt(leftq, quad, four(gkeep), ALU.mult)
            chain()
            tt(leftq, leftq, four(gpen), ALU.add)
            chain()
            exps = lambda a: a.unsqueeze(2).broadcast_to([P, T1, EXP1])
            best = one_k[:, 0, 0:T1]
            for k in range(TOPK):
                hot = hots[:, k].rearrange("p (t e) -> p t e", e=EXP1)
                run(nc.vector.tensor_reduce(best, left, AX.X, ALU.max))
                chain()
                tt(r1_tmp, left, exps(best), ALU.is_equal)
                chain()
                tt(r1_tmp, r1_tmp, misc[:, M_FIRST1:M_FIRST1 + EXP1].unsqueeze(1).broadcast_to([P, T1, EXP1]), ALU.mult)
                chain()
                run(nc.vector.tensor_reduce(best, r1_tmp, AX.X, ALU.max))
                chain()
                tt(hot, r1_tmp, exps(best), ALU.is_equal)
                chain()
                run(nc.vector.scalar_tensor_tensor(left, hot, -4.0 * LOW, left, ALU.mult, ALU.add))
                if k == 0:
                    run(nc.vector.tensor_copy(sel, hot))
                else:
                    tt(sel, sel, hot, ALU.add)
                chain()
            tt(sel, sel, exps(misc[:, M_VALID1:M_VALID1 + T1]), ALU.mult)
            chain()
            cum = earlier_tiles(sel, cumA, cumB, T1)
            assert cum is cumB
            tt(per_exp[:, 0], cum[:, T1 - 1], sel[:, T1 - 1], ALU.add)
            chain()
            nc.vector.tensor_copy(gl7[:], per_exp[:, 0, 0:1]).then_inc(ranks_in, 1)
            flat = lambda a: a.rearrange("p t e -> p (t e)")
            dve.wait_ge(cnt_ready, 1)
            cnt, tiles_of, first, other_, ends = (per_exp[:, k] for k in range(1, 6))
            run(nc.vector.tensor_copy(cnt, bank[1][:, 0:EXP1]))
            chain()
            tt(steps_c, cnt.unsqueeze(2).broadcast_to([P, EXP1, T1]),
               misc[:, M_STEPS:M_STEPS + T1].unsqueeze(1).broadcast_to([P, EXP1, T1]), ALU.is_gt)
            chain()
            run(nc.vector.tensor_reduce(tiles_of, steps_c, AX.X, ALU.add))
            chain()
            one = lambda a: a.unsqueeze(2)
            earlier_tiles(one(tiles_of), one(first), one(other_), EXP1)
            start = first
            tt(ends, start, tiles_of, ALU.add)
            run(nc.vector.tensor_scalar(cnt, start, float(P), None, ALU.mult))
            chain()
            dve.wait_ge(rank_ready, 1)
            tt(place, bank[0][:, 0:T1 * EXP1].rearrange("p (t e) -> p t e", e=EXP1),
               cnt.unsqueeze(1).broadcast_to([P, T1, EXP1]), ALU.add)
            chain()
            tt(hots2, hots, flat(place).unsqueeze(1).broadcast_to([P, TOPK, T1 * EXP1]), ALU.mult)
            chain()
            run(nc.vector.tensor_reduce(one_k[:, 2], hots2.rearrange("p k (t e) -> p (k t) e", e=EXP1), AX.X, ALU.add))
            chain()
            slot = one_k[:, 2].rearrange("p (k t) -> p k t", k=TOPK)
            run(nc.vector.tensor_scalar(slot_tile, slot, 1.0 / P, 1.0 / (2 * P) - 0.5, ALU.mult, ALU.add))
            for k in range(TOPK):
                run(nc.vector.tensor_scalar(row_no[:, k], misc[:, M_TOKEN:M_TOKEN + T1], float(k * TOKENS + 1), None, ALU.add))
            chain()
            run(nc.vector.tensor_scalar(slot_tile, slot_tile, ROUND, ROUND, ALU.add, ALU.subtract))
            chain()
            run(nc.vector.scalar_tensor_tensor(slot_lane, slot_tile, -float(P), slot, ALU.mult, ALU.add))
            chain()

            def one_hots(t, par):
                after(dve, hots_used, t - 3)
                for hot, width, base, at in ((lane_hot, P, M_LANE, slot_lane), (tile_hot, NT1, M_TILE, slot_tile)):
                    ins = nc.vector.tensor_tensor(
                        hot[par], misc[:, base:base + width].unsqueeze(1).broadcast_to([P, TOPK, width]),
                        at[:, :, ds(t, 1)].broadcast_to([P, TOPK, width]), ALU.is_equal)
                    run(ins) if hot is lane_hot else ins.then_inc(hots_ready, 1)

            for r in range(4):
                one_hots(r, r)
            fours(dve, one_hots, ((v, 4),))
            one_hots(T1 - 1, 0)
            tt(tile_cmp[0:1], ends[0:1].unsqueeze(1).broadcast_to([1, NT1, EXP1]),
               misc[0:1, M_TILE:M_TILE + NT1].unsqueeze(2).broadcast_to([1, NT1, EXP1]), ALU.is_le)
            chain()
            run(nc.vector.tensor_reduce(tile_no[:], tile_cmp[0:1], AX.X, ALU.add))
            chain()
            run(nc.vector.tensor_scalar(tile_exp[:], tile_no[:], float(EXP1 - 1), None, ALU.min))
            dve.wait_ge(hots_used, T1)
            number, above, more_, empty = (slot_row[:, k] for k in range(4))
            run(nc.vector.tensor_copy(number, bank[2][:, 0:NT1]))
            chain()
            run(nc.vector.tensor_scalar(above, number, float(TOKENS), -float(TOKENS), ALU.is_gt, ALU.mult))
            run(nc.vector.tensor_scalar(empty, number, 0.0, FAR, ALU.is_equal, ALU.mult))
            for k in range(2, TOPK):
                run(nc.vector.tensor_scalar(more_, number, float(k * TOKENS), -float(TOKENS), ALU.is_gt, ALU.mult))
                chain()
                tt(above, above, more_, ALU.add)
                chain()
            run(nc.vector.scalar_tensor_tensor(rec_idx[:, :, 1], number, -1.0, empty, ALU.add, ALU.add))
            tt(above, above, number, ALU.add)
            chain()
            nc.vector.tensor_scalar(rec_idx[:, :, 0], above, -1.0, 0.0, ALU.add, ALU.max).then_inc(idx_ready, 1)
            tt(hots2, hots, flat(score).unsqueeze(1).broadcast_to([P, TOPK, T1 * EXP1]), ALU.mult)
            chain()
            wk = one_k[:, 1].rearrange("p (k t) -> p k t", k=TOPK)
            run(nc.vector.tensor_reduce(one_k[:, 1], hots2.rearrange("p k (t e) -> p (k t) e", e=EXP1), AX.X, ALU.add))
            chain()
            total = one_k[:, 0, 0:T1]
            tt(total, wk[:, 0], wk[:, 1], ALU.add)
            chain()
            tt(total, total, wk[:, 2], ALU.add)
            chain()
            tt(total, total, wk[:, 3], ALU.add)
            chain()
            run(nc.vector.tensor_scalar(total, total, 1e-20, None, ALU.add))
            chain()
            run(nc.vector.reciprocal(total, total))
            chain()
            tt(wk, wk, total.unsqueeze(1).broadcast_to([P, TOPK, T1]), ALU.mult)
            chain()
            nc.vector.tensor_scalar(weight1[:].rearrange("p t k -> p k t"), wk, 2.5, None, ALU.mult).then_inc(weights_ready, 1)
            chain()

            def gate(j, par):
                dve.wait_ge(sg1_done, j + 1)
                after(dve, g1_turned, j - 1)
                nc.vector.tensor_tensor(gu1[par], sg1[par], bank[2 + par][:, DFE:2 * DFE], ALU.mult).then_inc(g1_done, 1)

            def rows_out(j, r):
                dve.wait_ge(y_ready2, j + 1)
                after(dve, y_sent[r], 4 * (j - r))
                nc.vector.tensor_copy(y1[r], bank[6 + r % 2][:, 0:HID]).then_inc(y_done, 1)

            for j in range(4):
                gate(j, j % 2)
                if j >= 2:
                    rows_out(j - 2, j - 2)
            gate(4, 0)
            rows_out(2, 2)
            gate(5, 1)
            rows_out(3, 3)
            with dve.Fori(0, (NT1 - 8) // 4) as p:
                for r in range(4):
                    gate(4 * p + (6 + r), r % 2)
                    rows_out(4 * p + (4 + r), r)
            gate(NT1 - 2, 0)
            rows_out(NT1 - 4, 0)
            gate(NT1 - 1, 1)
            rows_out(NT1 - 3, 1)
            rows_out(NT1 - 2, 2)
            rows_out(NT1 - 1, 3)

            def sum_up(i, par):
                dve.wait_ge(ys_in[par], 24 * (i + (2 - par)))
                for k in range(TOPK):
                    for q in range(TILES):
                        rows_ = ROWS[q]
                        h = h_all[0:rows_, ds(i, 1), q].rearrange("p i c -> p (i c)")
                        w = weight1[:, ds(2 * i + q, 1), k] if q < 2 else last_w[0:1, ds(TOPK * i + k, 1)]
                        ins = nc.vector.scalar_tensor_tensor(h, ysum[par][0:rows_, k, q], w, h, ALU.mult, ALU.add)
                        ins.then_inc(y_done2, 1) if (k, q) == (TOPK - 1, TILES - 1) else run(ins)
                    if k < TOPK - 1:
                        chain()

            dve.wait_ge(last_w_in, 16)
            staged(dve, 0, IMAGES - 1, sum_up, ((v, 22),))

        @block.gpsimd
        def _(pool):
            def settle(j, col):
                if not isinstance(j, int):
                    nc.gpsimd.tensor_tensor(scratch_pool[0:1, col:col + 1], scratch_pool[0:1, 2:3],
                                            scratch_pool[0:1, 2:3], ALU.add)

            g = Signals(pool_done)
            lns = Signals(rstd_ready)

            def inverse_std(rows=P, n=TILES, at=0):
                ln = lnstat[0:rows, at:at + n]
                var, y, w, t = (ln[:, :, k:k + 1] for k in range(1, 5))

                def step(ins):
                    g.on(ins)
                    pool.wait_ge(pool_done, g.now())

                lns.k += 1
                pool.wait_ge(var_ready, lns.now())
                eps, minus_half, three_halves = (misc[0:rows, M_NEWTON + k:M_NEWTON + k + 1].unsqueeze(1).broadcast_to(
                    [rows, n, 1]) for k in range(3))
                step(nc.gpsimd.tensor_tensor(w, var, eps, ALU.add))
                settle(lns.now(), 0)
                g.on(nc.gpsimd.tensor_scalar(y.bitcast(U32), w.bitcast(U32), -0.5, 1597463007.0, ALU.mult, ALU.add))
                pool.wait_ge(pool_done, g.now())
                step(nc.gpsimd.tensor_tensor(w, w, minus_half, ALU.mult))
                for k in range(3):
                    step(nc.gpsimd.tensor_tensor(t, y, y, ALU.mult))
                    step(nc.gpsimd.tensor_tensor(t, t, w, ALU.mult))
                    step(nc.gpsimd.tensor_tensor(t, t, three_halves, ALU.add))
                    ins = nc.gpsimd.tensor_tensor(y, y, t, ALU.mult)
                    step(ins) if k < 2 else ins.then_inc(rstd_ready, 1)

            nc.gpsimd.memset(scratch_pool[:], 0.0).then_inc(pool_done, 1)
            g.k += 1
            pool.wait_ge(pool_done, 1)
            nc.gpsimd.memset(rows, 0.0).then_inc(zero_ready, 1)
            nc.gpsimd.memset(logit0[:], 0.0)
            nc.gpsimd.memset(h_all[:, :, 2], 0.0).then_inc(zeroed, 1)

            inverse_std(1, 1)
            for _ in range(2):
                inverse_std(P, 8)
            pool.wait_ge(slots_zeroed, 16)

            def keep_rows(i, par):
                inverse_std()
                pool.wait_ge(n2_ready, i + 1)
                nc.gpsimd.tensor_copy(rows[:, ds(i, 1)].rearrange("p i q c -> p (i q c)"),
                                      turn_src[:].rearrange("p q c -> p (q c)")).then_inc(rows_kept, 1)

            staged(pool, 0, IMAGES - 1, keep_rows, ((g, PER_STD), (lns, 2)))
            pool.wait_ge(rows_kept, IMAGES)

            pool.wait_ge(slots_ready, 1)
            for t in range(IMAGES * TILES):
                nc.gpsimd.indirect_dma_start(slots0, bass.IndirectOffsetOnAxis(ap=slot_to[:, t:t + 1], axis=0),
                                             rows[:, t // TILES, t % TILES], None, bounds_check=EXP0 * CAP - 1,
                                             oob_is_err=False).then_inc(sent, 16)
            for par in range(2):
                pool.wait_ge(eo_stored[par], 16 * EXP0 // 2)
            pool.wait_ge(sent, 16 * IMAGES * TILES)
            def fetch_rows(i, par):
                after(pool, h2_done, i - 1)
                g.on(nc.gpsimd.tensor_copy(from_now[par][:], slot_from[:, ds(i * TILES, TILES)]))
                pool.wait_ge(pool_done, g.now())
                settle(i, 0)
                for q in range(TILES):
                    k = max(2, ROWS[q])
                    nc.gpsimd.indirect_dma_start(fetched[par][0:k, q], None, outs0,
                                                 bass.IndirectOffsetOnAxis(ap=from_now[par][0:k, q:q + 1], axis=0))\
                        .then_inc(fetched_in[par], 16)

            def stage(n, par, a=True, b=True, ahead=True):
                if ahead:
                    inverse_std(at=4)
                if b:
                    inverse_std()
                if a:
                    fetch_rows(n + 3, 1 - par)

            fetch_rows(0, 0)
            fetch_rows(1, 1)
            inverse_std(at=4)
            fetch_rows(2, 0)
            stage(0, 0, b=False)
            stage(1, 1)
            stage(2, 0)
            staged(pool, 3, 4, stage, ((g, PER_STD4), (lns, 4)))
            stage(5, 1, a=False)
            stage(6, 0, a=False)
            stage(7, 1, a=False, ahead=False)
            stage(8, 0, a=False, ahead=False)

            def number(t, par):
                pool.wait_ge(hots_ready, t + 1)
                nc.gpsimd.tensor_tensor(tile_hot[par], tile_hot[par], row_no[:, :, ds(t, 1)].broadcast_to([P, TOPK, NT1]),
                                        ALU.mult).then_inc(numbered, 1)

            for r in range(4):
                number(r, r)
            fours(pool, number)
            number(T1 - 1, 0)
            pool.wait_ge(idx_ready, 1)
            pool.wait_ge(n4_stored, 32 * IMAGES)

            def fetch(j, r):
                after(pool, x_turned, j - (XR - 1))
                after(pool, y_sent[r % 4], 4 * (j - r % 4) - 4 * IDX + 16)
                nc.gpsimd.tensor_copy(idx_now[r][:], rec_idx[:, ds(j, 1)].rearrange("p j w -> p (j w)")).then_inc(idx_copied, 1)
                pool.wait_ge(idx_copied, j + 1)
                settle(j, 0)
                nc.gpsimd.indirect_dma_start(xg[r % XR], None, n4_rows, bass.IndirectOffsetOnAxis(ap=idx_now[r][:, 0:1], axis=0))\
                    .then_inc(xg_in[r % XR], 16)

            def send(j, r):
                pool.wait_ge(y_done, j + 1)
                settle(j, 1)
                nc.gpsimd.indirect_dma_start(outs1, bass.IndirectOffsetOnAxis(ap=idx_now[r][:, 1:2], axis=0), y1[r % 4], None,
                                             bounds_check=TOPK * TOKENS - 1, oob_is_err=False).then_inc(y_sent[r % 4], 16)

            for j in range(IDX):
                if j >= LAG:
                    send(j - LAG, j - LAG)
                fetch(j, j)
            with pool.Fori(1, NT1 // IDX) as p:
                for r in range(IDX):
                    send(IDX * p + (r - LAG), (r - LAG) % IDX)
                    fetch(IDX * p + r, r)
            for j in range(NT1 - LAG, NT1):
                send(j, j % IDX)

        @block.scalar
        def _(act):
            s = Signals(act_done)

            act.wait_ge(ld_const, 32)
            act.wait_ge(turned, 1)
            for h in range(HALVES):
                ins = nc.scalar.activation(nT0[:, h, :].rearrange("p (i t) -> p i t", t=LEN)[:, :, 0],
                                           bank[1][:, h:h + 1].broadcast_to([P, IMAGES]), ACT.Copy)
                ins.then_inc(turned_out, 1)
            for g in range(2):
                act.wait_ge(logit_ready, g + 1)
                nc.scalar.activation(gl[:, 1], gl[:, 0], ACT.Exp).then_inc(exp_ready, 1)
                for n in range(4):
                    h, jj = n // 2, 4 * (n % 2)
                    act.wait_ge(turned, 1 + 4 * g + n + 1)
                    dst = nT0[:, h, :].rearrange("p (i t) -> p i t", t=LEN)[:, 4 * g:4 * g + 4, 1:LEN]
                    dst = dst.rearrange("p i (r j) -> p j i r", j=8)[:, jj:jj + 4]
                    nc.scalar.activation(dst, bank[4 + n % 4][:, :].rearrange("p (j i r) -> p j i r", j=4, i=4),
                                         ACT.Copy).then_inc(turned_out, 1)
            for c in range(CH):
                act.wait_ge(fold_done, c + 1)
                nc.scalar.activation(w_fold[:, c], bank[2 + c % 2][:, :], ACT.Copy).then_inc(fold_out, 1)
            if phases == 1:
                return
            act.wait_ge(ld_mix, 7 * 16)
            act.wait_ge(rows_stored, 16 * 16)
            act.wait_ge(bc_ready, 1)

            def tap(n, c):
                act.wait_ge(x_ready, 4 * n + (c + 1))
                nc.scalar.activation(conv[:, c], bank[c][:, 0:LEN], ACT.Identity, bias=chan[:, c, 4:5],
                                     scale=chan[:, c, 3:4]).then_inc(tap_done, 1)

            def gate_silus(n, par, tiles):
                after(act, y_ready, n - 1)
                for c in tiles:
                    act.wait_ge(z_ready, 4 * n + (c + 1))
                    ins = nc.scalar.activation(zs[par][:, c], bank[4 + c][:, 0:LEN], ACT.Silu)
                    s.on(ins) if c < CH - 1 else ins.then_inc(zs_done, 1)

            def conv_silu(n, par):
                act.wait_ge(conv_done, 2 * n + 2)
                nc.scalar.activation(xconv[par], conv, ACT.Silu).then_inc(xconv_ready, 1)

            def out_rows(i):
                for h in range(HALVES):
                    act.wait_ge(out_ready, 2 * i + (h + 1))
                    if h == 0:
                        after(act, tok_ready, i)
                    ins = nc.scalar.activation(outT[:, h], bank[h][:, 0:LEN], ACT.Copy)
                    s.on(ins) if h == 0 else ins.then_inc(outT_done, 1)

            def steps(n, par):
                act.wait_ge(bcsum_ready, n + 1)
                for b in range(2):
                    ins = nc.scalar.activation(bct[par][:, b], bank[4 + b][:, 0:LEN], ACT.Tanh, scale=0.5 / STATE)
                    s.on(ins) if b == 0 else ins.then_inc(bct_done, 1)
                after(act, dt_done, n)
                for k, c in enumerate(DT_ORDER):
                    act.wait_ge(dt_ready, 4 * n + (k + 1))
                    nc.scalar.activation(xb[:, c], bank[(6 + c) % 8][:, 0:LEN], ACT.Identity,
                                         bias=chan[:, c, 5:6]).then_inc(xb_done, 1)

            def log_sigmoid(i, part):
                if part == 0:
                    act.wait_ge(xb_done, 4 * i + 4)
                    s.on(nc.scalar.activation(soft, xb, ACT.Tanh, scale=0.5))
                    return
                act.wait_ge(act_done, s.now())
                if part == 1:
                    s.on(nc.scalar.activation(soft, soft, ACT.Abs))
                else:
                    nc.scalar.activation(soft, soft, ACT.Ln, bias=misc[:, M_HALF:M_HALF + 1], scale=0.5).then_inc(soft_ready, 1)

            def decay(i, par):
                act.wait_ge(dt_done, i + 1)
                after(act, y_ready, i - 1)
                nc.scalar.activation(es[par], dts, ACT.Tanh, scale=0.05).then_inc(e_done, 1)

            def norm_out(i, turned_sem, done, dst):
                act.wait_ge(turned_sem, i + 1)
                s.on(nc.scalar.activation(dst[:, :, 0:2 * P].rearrange("p h (q t) -> p q h t", q=2),
                                          bank[2][:, :].rearrange("p (q h t) -> p q h t", q=2, h=2), ACT.Copy))
                nc.scalar.activation(dst[:, :, 2 * P:LEN], bank[3][:, 256:258].unsqueeze(2), ACT.Copy).then_inc(done, 1)

            def stage(n, par, a=True, b=True, c=True, d=True):
                if a:
                    tap(n, 0)
                    tap(n, 1)
                if d:
                    norm_out(n - 3, n2_turned, n2T_done, n2T)
                if b:
                    log_sigmoid(n - 1, 0)
                if a:
                    tap(n, 2)
                if b:
                    log_sigmoid(n - 1, 1)
                if a:
                    tap(n, 3)
                if b:
                    log_sigmoid(n - 1, 2)
                if a:
                    gate_silus(n, par, (0,))
                if b:
                    decay(n - 1, 1 - par)
                if a:
                    gate_silus(n, par, (1, 2, 3))
                    conv_silu(n, par)
                if c:
                    out_rows(n - 2)
                if a:
                    steps(n, par)

            stage(0, 0, b=False, c=False, d=False)
            stage(1, 1, c=False, d=False)
            stage(2, 0, d=False)
            staged(act, 3, 6, stage, ((s, PER_MIX_ACT),))
            stage(7, 1)
            stage(IMAGES, 0, a=False)
            stage(IMAGES + 1, 1, a=False, b=False)
            stage(IMAGES + 2, 0, a=False, b=False, c=False)

            act.wait_ge(shift_ready, 1)
            nc.scalar.activation(r_exp, r_exp, ACT.Exp).then_inc(exps_ready, 1)
            act.wait_ge(ld_b, 32)

            def expert(e, par):
                for m in range(DFF // P):
                    act.wait_ge(hid_ready, 8 * e + (m + 1))
                    nc.scalar.activation(hidden[par][:, m], bank[2 + m % 4][:, 0:CAP], ACT.Relu,
                                         bias=b1_cols[:, ds(e, 1), m]).then_inc(hid_done, 1)

            staged(act, 0, EXP0 - 1, expert)

            def turned_rows(i, ready, done, dst, b):
                act.wait_ge(ready, i + 1)
                s.on(nc.scalar.activation(dst[:, :, 0:2 * P].rearrange("p h (q t) -> p q h t", q=2),
                                          bank[b][:, :].rearrange("p (q h t) -> p q h t", q=2, h=2), ACT.Copy))
                nc.scalar.activation(dst[:, :, 2 * P:LEN], bank[b + 1][:, 256:258].unsqueeze(2), ACT.Copy).then_inc(done, 1)

            def exponents(i, par):
                after(act, pt_ready, 3 * i)
                after(act, h3_done, i)
                for q in range(TILES):
                    k = ROWS[q]
                    act.wait_ge(m_ready, 3 * i + (q + 1))
                    nc.scalar.activation(probs[0:k, q], bank[2 + q][0:k, 0:LEN], ACT.Exp, bias=soft_c[0:k, 3 + q:4 + q],
                                         scale=float(HEAD) ** -0.5, accum_out=soft_c[0:k, 6 + q:7 + q]).then_inc(p_ready, 1)

            def probs_out(i, par):
                after(act, o_ready, 2 * i)
                for q in range(TILES):
                    k = ROWS[q]
                    act.wait_ge(pt_ready, 3 * i + (q + 1))
                    nc.scalar.activation(probsT[0:k, q], bank[(5, 2, 3)[q]][0:k, 0:LEN], ACT.Copy).then_inc(pt_done, 1)

            def shared_silu(j, par):
                after(act, hs_done, 3 * j)
                for q in range(TILES):
                    k = ROWS[q]
                    act.wait_ge(gu_ready, 3 * j + (q + 1))
                    nc.scalar.activation(silu_g[0:k, q], bank[6 + q % 2][0:k, 0:DFE], ACT.Silu).then_inc(sg_done, 1)

            def gated_out(j, par):
                after(act, mm2_ready, j)
                for k in range(2):
                    act.wait_ge(ht_ready, 2 * j + (k + 1))
                    nc.scalar.activation(gatedT[0:DK, k], bank[7 - k][0:DK, 0:LEN], ACT.Copy).then_inc(ht_done, 1)

            def attended(i, par):
                after(act, tokens_ready, i)
                for h in range(HALVES):
                    act.wait_ge(o_ready, 2 * i + (h + 1))
                    ins = nc.scalar.activation(outT[:, h], bank[4 + h][:, 0:LEN], ACT.Copy)
                    s.on(ins) if h == 0 else ins.then_inc(oT_done, 1)

            def stage(n, par, a=True, b=True, c=True, ahead=True):
                if a:
                    after(act, qk_ready, 4 * n)
                    after(act, v_ready, n)
                    turned_rows(n, n3_turned, n3T_done, n3T, 0)
                if b:
                    exponents(n - 1, 1 - par)
                if c:
                    after(act, gu_ready, 3 * (n - 2))
                    turned_rows(n - 2, n4_turned, n4T_done, n4T, 6)
                    act.wait_ge(n4T_done, n - 1)
                    s.on(nc.scalar.activation(n4T_last[:, :, ds(n - 2, 1)], n4T[:, :, 2 * P:LEN], ACT.Copy))
                if c:
                    shared_silu(n - 2, par)
                if b:
                    probs_out(n - 1, 1 - par)
                if c:
                    gated_out(n - 2, par)
                if b:
                    attended(n - 1, 1 - par)

            stage(0, 0, b=False, c=False)
            stage(1, 1, c=False)
            stage(2, 0)
            staged(act, 3, 6, stage, ((s, PER_ATT_ACT),))
            stage(7, 1, ahead=False)
            stage(8, 0, a=False, ahead=False)
            stage(9, 1, a=False, b=False, ahead=False)

            nc.scalar.activation(gl8[:], n4T_last[:, 0, 0:1], ACT.Copy).then_inc(last_cols, 1)
            act.wait_ge(sg_shift, 1)
            nc.scalar.activation(score, score, ACT.Exp).then_inc(sg_exp, 1)

            def x_out(j, par):
                act.wait_ge(x_turned, j + 1)
                nc.scalar.activation(xT1[par], bank[par][:, 0:2 * P].rearrange("p (h t) -> p h t", h=HALVES),
                                     ACT.Copy).then_inc(xT_done, 1)

            def silu(j, par):
                act.wait_ge(gu1_ready, j + 1)
                after(act, g1_done, j - 1)
                nc.scalar.activation(sg1[par], bank[2 + par][:, 0:DFE], ACT.Silu).then_inc(sg1_done, 1)

            def gated1_out(j, par):
                act.wait_ge(g1_turned, j + 1)
                nc.scalar.activation(gT1[par][0:DK], bank[4 + par][0:DK, 0:2 * P].rearrange("p (k t) -> p k t", k=2),
                                     ACT.Copy).then_inc(gT_done, 1)

            def tile(j, par, ahead=True, now=True, late=True):
                if ahead:
                    x_out(j + 1, 1 - par)
                if now:
                    silu(j, par)
                if late:
                    gated1_out(j - 1, 1 - par)

            x_out(0, 0)
            tile(0, 0, late=False)
            tile(1, 1)
            tile(2, 0)
            staged(act, 3, NT1 - 2, tile)
            tile(NT1 - 1, 1, ahead=False)
            tile(NT1, 0, ahead=False, now=False)

        @block.tensor
        def _(pe):
            pe.wait_ge(ld_const, 32)
            pe.wait_ge(normed_ready, 1)
            for h in range(HALVES):
                mm = nc.tensor.transpose(bank[1][:, h:h + 1], cls[0:1, HID + h * P:HID + (h + 1) * P], ident[0:1, 0:1])
            mm.then_inc(turned, 1)
            for g in range(2):
                pe.wait_ge(dots_ready, g + 1)
                nc.tensor.matmul(bank[0][:, 0:10], same_image, partial[:, g], start=True, stop=True).then_inc(sums_ready, 1)
                pe.wait_ge(normed_ready, 1 + g + 1)
                for n in range(4):
                    h, jj = n // 2, 4 * (n % 2)
                    if g:
                        pe.wait_ge(turned_out, 2 + n + 1)
                    for j in range(4):
                        mm = nc.tensor.transpose(bank[4 + n][:, j * P:(j + 1) * P], normed[:, jj + j, h * P:(h + 1) * P], ident)
                    mm.then_inc(turned, 1)
            pe.wait_ge(ld_mix, 7 * 16)
            for c in range(CH):
                if c >= 2:
                    pe.wait_ge(fold_out, c - 1)
                for k in range(CH):
                    mm = nc.tensor.matmul(bank[2 + c % 2][:, :], w_xdt[:, k, c * P:(c + 1) * P], w_dt[:, k],
                                          start=(k == 0), stop=(k == CH - 1))
                mm.then_inc(fold_done, 1)
            if phases == 1:
                return
            pe.wait_ge(fold_out, CH)
            pe.wait_ge(turned_out, 10)
            pe.wait_ge(bc_ready, 1)

            def dense(out, weights, moving, last=None):
                for k in range(len(weights)):
                    mm = nc.tensor.matmul(out, weights[k], moving[k], start=(k == 0), stop=(k == len(weights) - 1))
                return mm

            def project(n, b):
                x = [nT0[:, h, ds(n * LEN, LEN)] for h in range(HALVES)]
                dense(bank[b][:, 0:LEN], [w_in[:, h, b * P:(b + 1) * P] for h in range(HALVES)], x)\
                    .then_inc(x_ready if b < CH else z_ready, 1)

            def out_rows(i, par, conv_count):
                pe.wait_ge(conv_done, conv_count)
                pe.wait_ge(y_ready, i + 1)
                for h in range(HALVES):
                    dense(bank[h][:, 0:LEN], [w_out[:, c, h * P:(h + 1) * P] for c in range(CH)],
                          [ys[par][:, c] for c in range(CH)]).then_inc(out_ready, 1)

            def turn_rows(src, done):
                for q in range(TILES):
                    for h in range(HALVES):
                        o = bank[2][:, q * HID + h * P:q * HID + (h + 1) * P] if q < 2 else bank[3][0:1, h * P:(h + 1) * P]
                        mm = nc.tensor.transpose(o, src[:, h, q * P:q * P + ROWS[q]], ident)
                mm.then_inc(done, 1)

            def turn_norm(i, ready, done):
                pe.wait_ge(ready, i + 1)
                for q in range(TILES):
                    for h in range(HALVES):
                        k = ROWS[q]
                        o = bank[2][:, (q * 2 + h) * P:(q * 2 + h + 1) * P] if q < 2 else bank[3][:, 256 + h:257 + h]
                        src = turn_src[0:k, q, h * P:(h + 1) * P]
                        mm = nc.tensor.transpose(o, src, ident[0:k, 0:k])
                mm.then_inc(done, 1)

            def gate_sums(n, par):
                pe.wait_ge(xconv_ready, n + 1)
                pe.wait_ge(zs_done, n + 1)
                for b in range(2):
                    mm = dense(bank[4 + b][:, 0:LEN], [w_bcr[:, b, c] for c in range(CH)],
                               [xconv[par][:, c] for c in range(CH)])
                mm.then_inc(bcsum_ready, 1)

            def steps(n, par):
                after(pe, outT_done, n - 1)
                for c in DT_ORDER:
                    dense(bank[(6 + c) % 8][:, 0:LEN], [w_fold[:, k, c * P:(c + 1) * P] for k in range(CH)],
                          [xconv[par][:, k] for k in range(CH)]).then_inc(dt_ready, 1)

            def logits(i, done, wg, nT, n_exp, out):
                pe.wait_ge(done, i + 1)
                for q in range(TILES):
                    k = ROWS[q]
                    mm = dense(bank[3][0:k, 300 + q * n_exp:300 + (q + 1) * n_exp],
                               [nT[:, h, q * P:q * P + k] for h in range(HALVES)], [wg[:, h] for h in range(HALVES)])
                mm.then_inc(out, 1)

            def stage(n, par, a=True, b=True, c=True, d=True):
                if a:
                    for b_ in range(2):
                        after(pe, xb_done, 4 * n + (b_ - 3))
                        project(n, b_)
                if d:
                    turn_norm(n - 3, n2_ready, n2_turned)
                if a:
                    after(pe, bct_done, n)
                    project(n, 4)
                if d:
                    logits(n - 3, n2T_done, wg0, n2T, EXP0, log_ready)
                if a:
                    project(n, 2)
                    after(pe, log_saved, n - 2)
                    project(n, 3)
                    project(n, 5)
                    after(pe, xb_done, 4 * n)
                    project(n, 6)
                    project(n, 7)
                if c:
                    out_rows(n - 2, par, 2 * n + 1 if a else 2 * IMAGES)
                if a:
                    gate_sums(n, par)
                if c:
                    pe.wait_ge(outT_done, n - 1)
                    after(pe, log_saved, n - 2)
                    turn_rows(outT, tok_ready)
                if a:
                    steps(n, par)

            stage(0, 0, b=False, c=False, d=False)
            stage(1, 1, c=False, d=False)
            stage(2, 0, d=False)
            staged(pe, 3, 6, stage)
            stage(7, 1)
            stage(IMAGES, 0, a=False)
            stage(IMAGES + 1, 1, a=False, b=False)
            stage(IMAGES + 2, 0, a=False, b=False, c=False)

            pe.wait_ge(hot_ready, 1)
            flat = lambda a: a.rearrange("p t e -> p (t e)")
            dense(bank[0][:, 0:IMAGES * TILES * EXP0], [before, ones], [flat(r_hot), flat(r_tmp)]).then_inc(pos_ready, 1)

            def turn_slots(e, par):
                pe.wait_ge(xs_loaded[par], 8 * (e + (2 - par)))
                after(pe, xt_done, e)
                for h in range(HALVES):
                    for q in range(3):
                        mm = nc.tensor.transpose(bank[h][:, q * CAPP:(q + 1) * CAPP],
                                                 slot_rows[par][0:CAPP, q, h * P:(h + 1) * P], ident[0:CAPP, 0:CAPP])
                mm.then_inc(xt_ready, 1)

            def expert(e, par, more=True):
                pe.wait_ge(w_loaded[par], 16 * (e + (2 - par)))
                pe.wait_ge(xt_done, e + 1)
                x = [slotT[par][:, h] for h in range(HALVES)]
                for m in range(DFF // P):
                    after(pe, hid_done, 8 * e + (m - 3))
                    dense(bank[2 + m % 4][:, 0:CAP], [w1e[par][:, h, m * P:(m + 1) * P] for h in range(HALVES)],
                          x).then_inc(hid_ready, 1)
                if more:
                    turn_slots(e + 1, 1 - par)
                pe.wait_ge(hid_done, 8 * e + 8)
                after(pe, eo_done, e)
                for q in range(3):
                    o = bank[6][0:CAPP, q * HID:(q + 1) * HID] if q < 2 else bank[7][0:CAPP, 0:HID]
                    mm = dense(o, [hidden[par][:, m, q * CAPP:(q + 1) * CAPP] for m in range(DFF // P)],
                               [w2e[par][:, m] for m in range(DFF // P)])
                mm.then_inc(eo_ready, 1)

            pe.wait_ge(slots_ready, 1)
            turn_slots(0, 0)
            expert(0, 0)
            staged(pe, 1, 6, expert)
            expert(7, 1, more=False)

            def turn_rows_in(i, src, ready, done, b):
                pe.wait_ge(ready, i + 1)
                for q in range(TILES):
                    for h in range(HALVES):
                        k = ROWS[q]
                        o = bank[b][:, (q * 2 + h) * P:(q * 2 + h + 1) * P] if q < 2 else bank[b + 1][:, 256 + h:257 + h]
                        mm = nc.tensor.transpose(o, src[0:k, q, h * P:(h + 1) * P], ident[0:k, 0:k])
                mm.then_inc(done, 1)

            def tile_of(x, q):
                return x[:, q * P:q * P + ROWS[q]]

            def query_keys(n, quarters):
                for g in quarters:
                    if g >= 2:
                        pe.wait_ge(qk_done, 4 * n + (g - 1))
                    dense(bank[g % 2][:, 0:LEN], [w_qk[:, h, g * P:(g + 1) * P] for h in range(HALVES)],
                          [n3T[:, h] for h in range(HALVES)]).then_inc(qk_ready, 1)

            def stage(n, par, a=True, b=True, c=True, ahead=True):
                i, j = n - 1, n - 2
                if a:
                    after(pe, v_done, n)
                    turn_rows_in(n, turn_src, n3_ready, n3_turned, 0)
                if b:
                    pe.wait_ge(qk_done, 4 * i + 4)
                    after(pe, h3_done, i)
                    after(pe, oT_done, i)
                    for q in range(TILES):
                        dense(bank[2 + q][0:ROWS[q], 0:LEN], [tile_of(qkT[:, h], q) for h in range(HALVES)],
                              [qkT[:, HALVES + h] for h in range(HALVES)]).then_inc(s_ready, 1)
                if a:
                    pe.wait_ge(n3T_done, n + 1)
                    query_keys(n, (0, 1))
                if c:
                    after(pe, acc_done, j)
                    turn_rows_in(j, turn_src4, n4_ready, n4_turned, 6)
                if a:
                    query_keys(n, (2, 3))
                if c:
                    pe.wait_ge(n4T_done, j + 1)
                    for q in range(2):
                        k = ROWS[q]
                        mm = dense(bank[7][0:k, 300 + q * EXP1:300 + (q + 1) * EXP1],
                                   [tile_of(n4T[:, h], q) for h in range(HALVES)], [wg1[:, h] for h in range(HALVES)])
                    mm.then_inc(lg1_ready, 1)
                    for q in range(TILES):
                        k = ROWS[q]
                        if q == 1:
                            pe.wait_ge(lg1_saved, j + 1)
                        if q == 2:
                            pe.wait_ge(hs_done, 3 * j + 1)
                        dense(bank[6 + q % 2][0:k, 0:2 * DFE], [tile_of(n4T[:, h], q) for h in range(HALVES)],
                              [ws13[:, h] for h in range(HALVES)]).then_inc(gu_ready, 1)
                if b:
                    pe.wait_ge(p_ready, 3 * i + 3)
                    for kt in range(TILES):
                        for q in range(TILES):
                            mm = nc.tensor.transpose(bank[(5, 2, 3)[kt]][0:ROWS[kt], q * P:q * P + ROWS[q]],
                                                     tile_of(probs[0:ROWS[q], q], kt), ident[0:ROWS[q], 0:ROWS[q]])
                        mm.then_inc(pt_ready, 1)
                if a:
                    pe.wait_ge(qk_done, 4 * n + 4)
                    for q in range(TILES):
                        k = ROWS[q]
                        mm = dense(bank[0][:, q * HID:(q + 1) * HID] if q < 2 else bank[1][0:1, 0:HID],
                                   [tile_of(n3T[:, h], q) for h in range(HALVES)], [w_v[:, h] for h in range(HALVES)])
                    mm.then_inc(v_ready, 1)
                if c:
                    pe.wait_ge(hs_done, 3 * j + 3)
                    for k in range(2):
                        for q in range(TILES):
                            mm = nc.tensor.transpose(bank[7 - k][0:DK, q * P:q * P + ROWS[q]],
                                                     gated[0:ROWS[q], q, k * DK:(k + 1) * DK], ident[0:ROWS[q], 0:ROWS[q]])
                        mm.then_inc(ht_ready, 1)
                if b:
                    pe.wait_ge(pt_done, 3 * i + 3)
                    pe.wait_ge(v_done, i + 1)
                    for h in range(HALVES):
                        dense(bank[4 + h][:, 0:LEN],
                              [vals[1 - par][0:ROWS[kt], kt, h * P:(h + 1) * P] for kt in range(TILES)],
                              [probsT[0:ROWS[kt], kt] for kt in range(TILES)]).then_inc(o_ready, 1)
                if c:
                    pe.wait_ge(ht_done, 2 * j + 2)
                    for q in range(TILES):
                        mm = dense(bank[6][:, q * HID:(q + 1) * HID] if q < 2 else bank[7][0:1, 0:HID],
                                   [tile_of(gatedT[0:DK, k], q) for k in range(2)], [ws2[0:DK, k] for k in range(2)])
                    mm.then_inc(mm2_ready, 1)
                if b:
                    pe.wait_ge(oT_done, i + 1)
                    turn_rows(outT, tokens_ready)

            pe.wait_ge(w_qk_ready, 1)
            stage(0, 0, b=False, c=False)
            stage(1, 1, c=False)
            stage(2, 0)
            staged(pe, 3, 6, stage)
            stage(7, 1)
            stage(8, 0, a=False)
            stage(9, 1, a=False, b=False)

            pe.wait_ge(last_cols, 1)
            dense(bank[0][0:IMAGES, 0:EXP1], [n4T_last[:, h] for h in range(HALVES)],
                  [wg1[:, h] for h in range(HALVES)]).then_inc(last_lg, 1)
            pe.wait_ge(ranks_in, 1)
            dense(bank[1][:, 0:EXP1], [ones], [per_exp[:, 0]]).then_inc(cnt_ready, 1)
            dense(bank[0][:, 0:T1 * EXP1], [before, ones], [flat(sel), flat(cumB)]).then_inc(rank_ready, 1)

            def slot_table(t, par, first=False, last=False):
                rows_ = IMAGES if last else P
                pe.wait_ge(numbered, t + 1)
                for k in range(TOPK):
                    mm = nc.tensor.matmul(bank[2][:, 0:NT1], lane_hot[par][0:rows_, k], tile_hot[par][0:rows_, k],
                                          start=first and k == 0, stop=last and k == TOPK - 1)
                mm.then_inc(hots_used, 1)

            for r in range(4):
                slot_table(r, r, first=r == 0)
            fours(pe, slot_table)
            slot_table(T1 - 1, 0, last=True)

            def turn_x(j, par, r):
                pe.wait_ge(xg_in[r], 16 // XR * (j + (XR - r)))
                after(pe, xT_done, j - 1)
                for h in range(HALVES):
                    mm = nc.tensor.transpose(bank[par][:, h * P:(h + 1) * P], xg[r][:, h * P:(h + 1) * P], ident)
                mm.then_inc(x_turned, 1)

            def expert_of(j):
                return pe.value_load(tile_exp[0:1, ds(j, 1)], min_val=0, max_val=EXP1 - 1)

            def gate_up(j, par):
                e = expert_of(j)
                pe.wait_ge(xT_done, j + 1)
                after(pe, g1_done, j - 1)
                dense(bank[2 + par][:, 0:2 * DFE], [xT1[par][:, h] for h in range(HALVES)],
                      [w13[:, ds(e, 1), h].rearrange("p e n -> p (e n)") for h in range(HALVES)]).then_inc(gu1_ready, 1)

            def turn_gated(j, par):
                pe.wait_ge(g1_done, j + 1)
                after(pe, gT_done, j - 1)
                for k in range(2):
                    mm = nc.tensor.transpose(bank[4 + par][0:DK, k * P:(k + 1) * P], gu1[par][:, k * DK:(k + 1) * DK], ident)
                mm.then_inc(g1_turned, 1)

            def down(j, par):
                e = expert_of(j)
                pe.wait_ge(gT_done, j + 1)
                after(pe, y_done, j - 1)
                dense(bank[6 + par][:, 0:HID], [gT1[par][0:DK, k] for k in range(2)],
                      [w2s[0:DK, ds(e, 1), k].rearrange("p e n -> p (e n)") for k in range(2)]).then_inc(y_ready2, 1)

            def tile(j, r, ahead=True, now=True, late=True, last=True):
                par = r % 2
                if ahead:
                    turn_x(j + 1, 1 - par, (r + 1) % XR)
                if now:
                    gate_up(j, par)
                if late:
                    turn_gated(j - 1, 1 - par)
                if last:
                    down(j - 2, par)

            pe.wait_ge(idx_ready, 1)
            turn_x(0, 0, 0)
            tile(0, 0, late=False, last=False)
            tile(1, 1, last=False)
            for j in range(2, XR):
                tile(j, j)
            with pe.Fori(1, NT1 // XR - 1) as p:
                for r in range(XR):
                    tile(XR * p + r, r)
            for j in range(NT1 - XR, NT1 - 1):
                tile(j, j % XR)
            tile(NT1 - 1, XR - 1, ahead=False)
            tile(NT1, 0, ahead=False, now=False)
            tile(NT1 + 1, 1, ahead=False, now=False, late=False)
    return nc


def rows_on_partitions(w):
    k, n = w.shape
    return w.reshape(k // P, P, n).transpose(1, 0, 2)


def lay_out(a):
    o = dict(constants())
    o["x"] = a["x"].reshape(IMAGES, SIDE, SIDE)
    o["cls_tok"] = a["cls_tok"].reshape(1, HID)
    for n in ("Wa", "Wd1", "Wd2", "Wd3"):
        o[n] = a["L0_tok_" + n]
    o["gbias"] = np.concatenate([a["L0_tok_" + n] for n in ("ba", "bd1", "bd2", "bd3")])
    wx = a["L0_attn_W_x"]
    o["w_in"] = rows_on_partitions(a["L0_attn_W_in"].T)
    o["w_dt"] = rows_on_partitions(a["L0_attn_W_dt"].T)
    o["w_xdt"] = rows_on_partitions(wx[2 * STATE:])
    o["w_bc"] = rows_on_partitions(wx[:2 * STATE].T)
    o["w_out"] = rows_on_partitions(a["L0_attn_W_out"].T)
    chan = np.concatenate([a["L0_attn_conv_w"][:, 0, :], a["L0_attn_conv_b"][:, None], a["L0_attn_b_dt"][:, None],
                           a["L0_attn_D"][:, None], a["L0_attn_D"][:, None]], 1)
    o["chan"] = rows_on_partitions(chan)
    o["w1"] = a["L0_ffn_w1"].reshape(EXP0, HALVES, P, DFF).transpose(0, 2, 1, 3).reshape(EXP0, P, -1)
    o["w2"] = a["L0_ffn_w2"].reshape(EXP0, DFF // P, P, HID).transpose(0, 2, 1, 3).reshape(EXP0, P, -1)
    o["b1"] = a["L0_ffn_b1"].reshape(EXP0, DFF // P, P).transpose(2, 0, 1)
    o["b2"] = a["L0_ffn_b2"].reshape(-1)
    wq, wk, bq, bk = (a["L1_attn_" + n] for n in ("Wq", "Wk", "bq", "bk"))
    o["w_qk"] = rows_on_partitions(np.concatenate([wq.T, wk.T], 1))
    bias = np.concatenate([bq, bk]).reshape(4, P)
    pair = bias.reshape(4, P // 2, 2)[:, :, ::-1].reshape(4, P)
    sign = np.broadcast_to(np.tile(np.array([-1, 1], np.float32), P // 2), (4, P))
    o["qk_bias"] = np.concatenate([bias, pair, sign]).T
    o["w_v"] = rows_on_partitions(a["L1_attn_Wv"].T)
    o["bv"] = a["L1_attn_bv"]
    o["wg1"] = rows_on_partitions(a["L1_ffn_gate_w"].T)
    o["ws13"] = rows_on_partitions(np.concatenate([a["L1_ffn_ws1"].T, a["L1_ffn_ws3"].T], 1))
    o["ws2"] = a["L1_ffn_ws2"].T.reshape(2, DK, HID).transpose(1, 0, 2)
    o["gate_bias"] = a["L1_ffn_gate_bias"]
    w13 = np.concatenate([a["L1_ffn_w1"], a["L1_ffn_w3"]], 1)
    o["w13"] = w13.transpose(2, 0, 1).reshape(HALVES, P, EXP1, 2 * DFE).transpose(1, 2, 0, 3).reshape(P, -1)
    w2 = a["L1_ffn_w2"].transpose(2, 0, 1).reshape(2, DK, EXP1, HID)
    o["w2s"] = w2.transpose(1, 2, 0, 3).reshape(DK, -1)
    o["wg0"] = rows_on_partitions(a["L0_ffn_wg"])
    return {k: np.ascontiguousarray(v) for k, v in o.items()}


def kernel(**inputs):
    import concourse.bacc as bacc
    from concourse.bass_utils import run_bass_kernel_spmd

    nc = bacc.Bacc("TRN2", target_bir_lowering=False, num_devices=1)
    arrays = {f"in_{n}": v for n, v in lay_out({n: np.asarray(v) for n, v in inputs.items()}).items()}
    d = {n[3:]: nc.dram_tensor(n, v.shape, mybir.dt.from_np(v.dtype), kind="ExternalInput").ap()
         for n, v in arrays.items()}
    d["out"] = nc.dram_tensor("out", (TOKENS, HID), F32, kind="ExternalOutput").ap()
    build(nc, d)
    r = run_bass_kernel_spmd(nc, [arrays], core_ids=[0])
    return r.results[0]["out"].reshape(IMAGES, LEN, HID)
```

```python
from contextlib import ExitStack, contextmanager

import numpy as np

import concourse.bass as bass
from concourse import mybir

F32 = mybir.dt.float32
U32 = mybir.dt.uint32
ALU = mybir.AluOpType
ACT = mybir.ActivationFunctionType
AX = mybir.AxisListType
ds = bass.ds

P = 128
IMAGES, SIDE, HID = 8, 256, 256
LEN = SIDE + 1
TOKENS = IMAGES * LEN
HALVES = HID // P
TILES = 3
ROWS = (P, P, 1)
EPS = 1e-5
INNER, STATE, TAPS = 512, 16, 4
CH = INNER // P
EXP0, DFF = 8, 1024
CAP = int(1.25 * TOKENS / EXP0)
CAPP = CAP // 3
EXP1, DFE, TOPK, GROUPS = 16, 192, 4, 4
DK = DFE // 2
HEAD = 128
NT1 = (TOKENS * TOPK + EXP1 * (P - 1)) // P
FAR = 1.0e6
LOW = 1.0e30
T1 = 2 * IMAGES + 1
XR, IDX, LAG = 8, 16, 7
SLOT_TILES = 3 * EXP0
DT_ORDER = (2, 3, 0, 1)
ROUND = 1.5 * 2.0 ** 23


class Signals:

    def __init__(self, sem):
        self.sem, self.base, self.k = sem, 0, 0

    def on(self, ins):
        ins.then_inc(self.sem, 1)
        self.k += 1
        return self.base + self.k

    def now(self):
        return self.base + self.k

    @contextmanager
    def loop(self, trip, trips, per):
        start = self.base + self.k
        self.base, self.k = start + trip * per, 0
        yield
        assert self.k == per, (self.k, per)
        self.base, self.k = start + trips * per, 0


def staged(eng, first, last, body, signals=()):
    trips = (last - first + 1) // 2
    with ExitStack() as ctx:
        p = ctx.enter_context(eng.Fori(0, trips))
        for s, per in signals:
            ctx.enter_context(s.loop(p, trips, per))
        body(2 * p + first, first % 2)
        body(2 * p + (first + 1), (first + 1) % 2)


def fours(eng, body, signals=()):
    assert T1 % 4 == 1
    with ExitStack() as ctx:
        p = ctx.enter_context(eng.Fori(1, T1 // 4))
        for s, per in signals:
            ctx.enter_context(s.loop(p - 1, T1 // 4 - 1, per))
        for r in range(4):
            body(4 * p + r, r)


def after(eng, sem, value):
    if not isinstance(value, int) or value > 0:
        eng.wait_ge(sem, value)


def constants():
    k = np.arange(P)
    ident = np.eye(P, dtype=np.float32)
    before = (k[:, None] < k[None, :]).astype(np.float32)
    same_image = (k[:, None] // 32 == k[None, :] // 32).astype(np.float32)
    ones = np.ones((P, P), np.float32)
    mats = np.stack([ident, before, same_image, ones], 1)
    pos = np.arange(LEN, dtype=np.float32)
    inv = np.float32(10000.0) ** (np.arange(0, HEAD, 2, dtype=np.float32) / np.float32(HEAD))
    radians = (pos[:, None] / inv).astype(np.float32)
    sincos = np.stack((np.sin(radians), np.cos(radians)), -1).reshape(LEN, -1)
    rope = np.repeat(sincos, 2, axis=-1).astype(np.float32)
    rope = np.ascontiguousarray(rope.T.reshape(HALVES, P, LEN).transpose(1, 0, 2))
    valid = np.ones((P, IMAGES, TILES), np.float32)
    valid[1:, :, 2] = 0
    gate_scale = np.array([1 / 64.] + [1 / 64.] * 3 + [1 / 16.] * 3 + [1 / 4.] * 3, np.float32)
    e0 = np.arange(EXP0, dtype=np.float32)
    e1 = np.arange(EXP1, dtype=np.float32)
    row = np.concatenate([gate_scale, EXP0 - e0, e0 * CAP, EXP1 - e1])
    row = np.broadcast_to(row, (P, row.size))
    token = np.zeros((P, T1))
    for i in range(IMAGES):
        for q in range(2):
            token[:, 2 * i + q] = i * LEN + q * P + k
    token[:IMAGES, T1 - 1] = k[:IMAGES] * LEN + 2 * P
    valid1 = np.ones((P, T1))
    valid1[IMAGES:, T1 - 1] = 0
    bcast = lambda r: np.broadcast_to(np.asarray(r).reshape(-1), (P, np.asarray(r).size))
    row0 = (np.arange(IMAGES)[:, None] * LEN + np.arange(TILES)[None] * P).reshape(1, -1) + k[:, None] + 1
    g = np.arange(GROUPS)
    misc = np.concatenate([row, valid.reshape(P, -1), np.full((P, 1), 0.5), token, valid1,
                           bcast([EPS, -0.5, 1.5]),
                           bcast(g[:, None] > g[None, :]), bcast(np.arange(T1) * P), bcast(np.arange(NT1)), bcast(k), row0], 1)
    return {"mats": mats, "rope": rope, "misc": np.ascontiguousarray(misc.astype(np.float32))}


PER_MIX, PER_MIX_ACT = 68, 16
PER_ATT, PER_ATT_ACT = 50, 8
PER_STD, PER_STD4 = 28, 58
M_SCALE, M_FIRST0, M_BASE0, M_FIRST1, M_VALID, M_HALF = 0, 10, 18, 26, 42, 66
M_TOKEN = 67
M_VALID1 = M_TOKEN + T1
M_NEWTON = M_VALID1 + T1
M_LOWER = M_NEWTON + 3
M_STEPS = M_LOWER + GROUPS * GROUPS
M_TILE = M_STEPS + T1
M_LANE = M_TILE + NT1
M_ROW0 = M_LANE + P
M_END = M_ROW0 + IMAGES * TILES


def build(nc, d, phases=9):
    ctx = ExitStack()
    with ctx:
        def sb(name, shape, dt=F32):
            return ctx.enter_context(nc.sbuf_tensor(name, shape, dt))

        def sem(name):
            return ctx.enter_context(nc.semaphore(name))

        def dram(name, shape, dt=F32):
            return nc.dram_tensor(name, shape, dt, kind="Internal").ap()

        h0_rows = dram("h0_rows", (TOKENS, HID))
        n2_rows = dram("n2_rows", (TOKENS, HID))
        outs0 = dram("outs0", (EXP0 * CAP, HID))
        n4_rows = dram("n4_rows", (TOKENS, HID))
        last_weights = dram("last_weights", (IMAGES, TOPK))
        outs1 = dram("outs1", (TOPK * TOKENS, HID))

        mats = sb("mats", [P, 4, P])
        ident, before, same_image, ones = (mats[:, k, :] for k in range(4))
        misc = sb("misc_c", [P, M_END])
        big, mid, mix, spare = sb("big", [P, 20480]), sb("mid", [P, 4112]), sb("mix", [P, 10240]), sb("spare", [P, 6144])

        def arena(mem):
            at = [0]

            def part(n, **dims):
                at[0] += n
                assert at[0] <= mem.shape[1], at[0]
                p = mem[:, at[0] - n:at[0]]
                return p.rearrange("p (a b) -> p a b", **dims) if dims else p

            return part

        part = arena(big)

        img = part(2 * 2048).rearrange("p (g r c) -> p g r c", g=2, r=8)
        w_l1 = part(4608).rearrange("p (f j) -> p f j", j=3)
        w_l2 = part(1152).rearrange("p (f j) -> p f j", j=3)
        w_l3 = part(288).rearrange("p (f j) -> p f j", j=3)
        w_a = part(32)
        gbias = part(10)
        sumc = part(1024)
        difc = part(1024)
        bands_of = [[part(n) for n in (512, 128, 32, 1536, 384, 96)]]
        R2, R1 = part(128), part(512)
        A3g = part(32)
        vw = part(512)
        dot_out = part(1536)
        partial = part(20).rearrange("p (g n) -> p g n", g=2)
        gl = part(160).rearrange("p (k g n) -> p k g n", k=8, g=2)
        rec = img
        lnstat = sb("lnstat", [P, 8, 8])
        lnst = sb("lnst", [P, 8, 6])
        normed = part(2048).rearrange("p (r c) -> p r c", r=8)
        cls = part(512)

        nT0 = arena(mid)(HALVES * TOKENS, a=HALVES)
        part = arena(mix)
        w_in = part(HALVES * 2 * INNER, a=HALVES)
        w_dt = part(CH * INNER, a=CH)
        w_xdt = part(CH * INNER, a=CH)
        w_fold = part(CH * INNER, a=CH)
        w_bcr = part(2 * CH * P).rearrange("p (b k m) -> p b k m", b=2, k=CH)
        w_out = part(CH * HID, a=CH)
        w_bc = sb("w_bc", [P, CH, 2 * STATE])
        w_bcs = sb("w_bcs", [P, CH, 2])
        chan = sb("chan", [P, CH, 8])
        part = arena(big)
        conv, xb, soft, dts, al, om, gat, hs = (part(CH * LEN, a=CH) for _ in range(8))
        xconv, zs, es, ys = ([part(CH * LEN, a=CH) for _ in range(2)] for _ in range(4))
        bct = [part(2 * LEN, a=2) for _ in range(2)]
        outT = sb("outT", [P, HALVES, LEN])
        n2T = sb("n2T", [P, HALVES, LEN])
        part = arena(spare)
        bands_of.append([part(n) for n in (512, 128, 32, 1536, 384, 96)])
        part = arena(spare)
        lane_hot0, tile_hot0 = (part(IMAGES * TILES * n, a=IMAGES * TILES) for n in (CAPP, SLOT_TILES))
        slot_lane0, slot_tile0, slot_no0 = (part(IMAGES * TILES) for _ in range(3))

        part = arena(mix)
        part(2048)
        w1e, w2e = zip(*[(part(HALVES * DFF, a=HALVES), part(DFF // P * HID, a=DFF // P)) for _ in range(2)])
        part = arena(big)
        b2_rows = part(EXP0 * HID, a=EXP0)
        slot_rows = [part(3 * HID, a=3) for _ in range(2)]
        slotT = [part(HALVES * CAP, a=HALVES) for _ in range(2)]
        hidden = [part(DFF // P * CAP, a=DFF // P) for _ in range(2)]
        expert_rows = [part(3 * HID, a=3) for _ in range(2)]
        r_exp, r_hot, r_cum, r_tmp = (part(IMAGES * TILES * EXP0, a=IMAGES * TILES) for _ in range(4))
        r_one = part(8 * IMAGES * TILES, a=8)
        part = arena(mix)
        w_qkr, w_qk = part(HALVES * 2 * HID, a=HALVES), part(HALVES * 2 * HID, a=HALVES)
        w_v, rope = part(HALVES * HID, a=HALVES), part(HALVES * LEN, a=HALVES)
        bv_rows, qk_bias = part(HID), part(12)
        qkT = part(2 * HALVES * LEN, a=2 * HALVES)
        probs, probsT = part(TILES * LEN, a=TILES), part(TILES * LEN, a=TILES)
        soft_c = part(24)
        part(1300)
        wg1, ws13, ws2 = part(HALVES * EXP1, a=HALVES), part(HALVES * 2 * DFE, a=HALVES), part(2 * HID, a=2)
        gated, silu_g = part(TILES * DFE, a=TILES), part(TILES * DFE, a=TILES)
        gatedT = part(2 * LEN, a=2)
        part = arena(mid)
        n3T, n4T = part(HALVES * LEN, a=HALVES), part(HALVES * LEN, a=HALVES)
        vals = [part(TILES * HID, a=TILES) for _ in range(2)]
        turn_src4 = part(TILES * HID, a=TILES)
        logit1 = sb("logit1", [P, T1, EXP1])
        n4T_last = sb("n4T_last", [P, HALVES, IMAGES])
        bias1 = sb("bias1", [P, EXP1])
        part = arena(spare)
        fetched = [part(TILES * HID, a=TILES) for _ in range(2)]
        part = arena(big)
        w13 = part(EXP1 * HALVES * 2 * DFE).rearrange("p (e h n) -> p e h n", e=EXP1, h=HALVES)
        w2s = part(EXP1 * 2 * HID).rearrange("p (e k n) -> p e k n", e=EXP1, k=2)
        part = arena(mix)
        score, biased, left, r1_tmp, sel, place, cumA, cumB = (part(T1 * EXP1, a=T1) for _ in range(8))
        hots = part(TOPK * T1 * EXP1, a=TOPK)
        hots2 = part(TOPK * T1 * EXP1, a=TOPK)
        one_k = part(6 * TOPK * T1, a=6)
        g_all = part(10 * T1 * GROUPS, a=10)
        g_pair = part(2 * T1 * GROUPS * GROUPS, a=2)
        steps_c = part(EXP1 * T1, a=EXP1)
        per_exp = part(6 * EXP1, a=6)
        xg = [part(HID) for _ in range(XR)]
        part = arena(spare)
        tile_cmp = part(NT1 * EXP1, a=NT1)
        lane_hot, tile_hot = [part(TOPK * P, a=TOPK) for _ in range(4)], [part(TOPK * NT1, a=TOPK) for _ in range(4)]
        row_no, slot_lane, slot_tile = (part(TOPK * T1, a=TOPK) for _ in range(3))
        slot_row = part(4 * NT1, a=4)
        part = arena(mid)
        xT1, gT1 = [part(HALVES * P, a=HALVES) for _ in range(2)], [part(2 * P, a=2) for _ in range(2)]
        sg1, gu1 = [part(DFE) for _ in range(2)], [part(DFE) for _ in range(2)]
        y1 = [part(HID) for _ in range(4)]
        part = arena(big)
        ysum = [part(TOPK * TILES * HID).rearrange("p (k q c) -> p k q c", k=TOPK, q=TILES) for _ in range(4)]
        tile_exp = sb("tile_exp", [1, NT1], U32)
        rec_idx = sb("rec_idx", [P, NT1, 2], U32)
        idx_now = [sb(f"idx_now{k}", [P, 2], U32) for k in range(IDX)]
        tile_no = sb("tile_no", [1, NT1])
        weight1, last_w = sb("weight1", [P, T1, TOPK]), sb("last_w", [1, IMAGES * TOPK])
        b1_cols = sb("b1_cols", [P, EXP0, DFF // P])
        scratch_dve, scratch_pool = sb("scratch_dve", [1, 1]), sb("scratch_pool", [1, 3])
        gl7 = sb("gl7", [P, 1])
        gl8 = sb("gl8", [P, 1])
        from_now = [sb(f"from_now{k}", [P, TILES], U32) for k in range(2)]
        gate0 = sb("gate0", [P, IMAGES * TILES])
        slot_src = sb("slot_src", [P, SLOT_TILES], U32)
        src_now = [sb(f"src_now{k}", [P, 3], U32) for k in range(2)]
        slot_from = sb("slot_from", [P, IMAGES * TILES], U32)
        turn_src = sb("turn_src", [P, TILES, HID])
        wg0 = sb("wg0", [P, HALVES, EXP0])
        logit0 = sb("logit0", [P, IMAGES, TILES, EXP0])
        h_all = sb("h_all", [P, IMAGES, TILES, HID])

        bank = [ctx.enter_context(nc.psum_tensor(f"bank{k}", [P, 512], F32)) for k in range(8)]

        ld_const, ld_img, ld_wav, ld_wav1, ld_mix = (
            sem("ld_const"), [sem("ld_img0"), sem("ld_img1")], sem("ld_wav"), sem("ld_wav1"), sem("ld_mix"))
        dve_done, act_done, pool_done = sem("dve_done"), sem("act_done"), sem("pool_done")
        dots_ready, sums_ready, logit_ready, exp_ready = sem("dots_ready"), sem("sums_ready"), sem("logit_ready"), sem("exp_ready")
        vgated, vin = sem("vgated"), sem("vin")
        var_ready, rstd_ready = sem("var_ready"), sem("rstd_ready")
        rec_ready, rows_stored = sem("rec_ready"), sem("rows_stored")
        normed_ready, turned, turned_out = sem("normed_ready"), sem("turned"), sem("turned_out")
        fold_done, fold_out, bc_summed, bc_ready = sem("fold_done"), sem("fold_out"), sem("bc_summed"), sem("bc_ready")
        stored = sem("stored")
        x_ready, z_ready, tap_done, conv_done, xconv_ready, zs_done = (sem(n) for n in (
            "x_ready", "z_ready", "tap_done", "conv_done", "xconv_ready", "zs_done"))
        y_ready, out_ready, outT_done, tok_ready, res_done = (sem(n) for n in (
            "y_ready", "out_ready", "outT_done", "tok_ready", "res_done"))
        bcsum_ready, bct_done, dt_ready, xb_done, soft_ready, dt_done, e_done = (sem(n) for n in (
            "bcsum_ready", "bct_done", "dt_ready", "xb_done", "soft_ready", "dt_done", "e_done"))
        n2_ready, n2_turned, n2T_done, log_ready, log_saved = (sem(n) for n in (
            "n2_ready", "n2_turned", "n2T_done", "log_ready", "log_saved"))
        (ld_att, fetched_in, h2_done, n3_ready, n3_turned, n3T_done, qk_ready, qk_done, v_ready, v_done, s_ready, m_ready, p_ready, pt_ready, pt_done, o_ready, oT_done, tokens_ready, h3_done, n4_ready, n4_turned, n4T_done, n4_stored, lg1_ready, lg1_saved, gu_ready, sg_done, hs_done, ht_ready, ht_done, mm2_ready, acc_done, w_qk_ready) = (sem(n) for n in (
            "a_ld_att", "a_fetched_in", "a_h2_done", "a_n3_ready", "a_n3_turned", "a_n3T_done", "a_qk_ready", "a_qk_done", "a_v_ready", "a_v_done", "a_s_ready", "a_m_ready", "a_p_ready", "a_pt_ready", "a_pt_done", "a_o_ready", "a_oT_done", "a_tokens_ready", "a_h3_done", "a_n4_ready", "a_n4_turned", "a_n4T_done", "a_n4_stored", "a_lg1_ready", "a_lg1_saved", "a_gu_ready", "a_sg_done", "a_hs_done", "a_ht_ready", "a_ht_done", "a_mm2_ready", "a_acc_done", "a_w_qk_ready"))
        (ld_w1, last_lg, sg_shift, sg_exp, ranks_in, rank_ready, cnt_ready, hots_ready, hots_used, weights_ready, weights_out, last_w_in, idx_ready, idx_copied, x_turned, xT_done, gu1_ready, sg1_done, g1_done, g1_turned, gT_done, y_ready2, y_done, last_stored) = (sem(n) for n in (
            "b_ld_w1", "b_last_lg", "b_sg_shift", "b_sg_exp", "b_ranks_in", "b_rank_ready", "b_cnt_ready", "b_hots_ready", "b_hots_used", "b_weights_ready", "b_weights_out", "b_last_w_in", "b_idx_ready", "b_idx_copied", "b_x_turned", "b_xT_done", "b_gu1_ready", "b_sg1_done", "b_g1_done", "b_g1_turned", "b_gT_done", "b_y_ready2", "b_y_done", "b_last_stored"))
        numbered = sem("numbered")
        y_done2, last_cols = sem("y_done2"), sem("last_cols")
        xg_in, y_sent, ys_in = [sem(f"xg_in{k}") for k in range(XR)], [sem(f"y_sent{k}") for k in range(4)], [sem(f"ys_in{k}") for k in range(4)]
        fetched_in = [sem("fetched_in0"), sem("fetched_in1")]
        ld_shared = sem("ld_shared")
        last_scaled, last_done = sem("last_scaled"), sem("last_done")
        h0_loaded, zeroed = sem("h0_loaded"), sem("zeroed")
        n2_stored, hots0_ready, table0_ready = sem("n2_stored"), sem("hots0_ready"), sem("table0_ready")
        shift_ready, exps_ready, hot_ready, pos_ready, slots_ready = (sem(n) for n in (
            "shift_ready", "exps_ready", "hot_ready", "pos_ready", "slots_ready"))
        ld_b, w_loaded, xs_loaded = sem("ld_b"), [sem("w_loaded0"), sem("w_loaded1")], [sem("xs_loaded0"), sem("xs_loaded1")]
        xt_ready, xt_done, hid_ready, hid_done, eo_ready, eo_done = (sem(n) for n in (
            "xt_ready", "xt_done", "hid_ready", "hid_done", "eo_ready", "eo_done"))
        eo_stored = [sem("eo_stored0"), sem("eo_stored1")]

        block = ctx.enter_context(nc.Block())

        @block.sync
        def _(sp):
            sp.dma_start(img[:, 0], d["x"][0:4].rearrange("b (r j) c -> (b r) j c", j=8)).then_inc(ld_img[0], 16)
            sp.dma_start(mats[:], d["mats"]).then_inc(ld_const, 16)
            sp.dma_start(misc[:], d["misc"]).then_inc(ld_const, 16)
            sp.dma_start(gbias, d["gbias"].partition_broadcast(P)).then_inc(ld_wav, 16)
            sp.dma_start(cls[0:1, 0:HID], d["cls_tok"]).then_inc(ld_wav, 16)

            def gate_weights(w, name, ready):
                for b in range(4):
                    sp.dma_start(w[32 * b:32 * b + 32].rearrange("p (s f) j -> p s (f j)", s=3),
                                 d[name].rearrange("(s p f) j -> p s (f j)", s=3, p=32)).then_inc(ready, 16)

            for b in range(4):
                sp.dma_start(w_a[32 * b:32 * b + 32], d["Wa"].rearrange("(p f) j -> p (f j)", p=32)).then_inc(ld_wav, 16)
            gate_weights(w_l3, "Wd1", ld_wav)
            gate_weights(w_l2, "Wd2", ld_wav)
            sp.dma_start(img[:, 1], d["x"][4:8].rearrange("b (r j) c -> (b r) j c", j=8)).then_inc(ld_img[1], 16)
            gate_weights(w_l1, "Wd3", ld_wav1)
            for t, n in ((w_xdt, "w_xdt"), (w_dt, "w_dt"), (w_bc, "w_bc"), (w_in, "w_in"), (chan, "chan"), (w_out, "w_out"), (wg0, "wg0")):
                sp.dma_start(t[:], d[n]).then_inc(ld_mix, 16)
            for b in range(IMAGES):
                sp.dma_start(h0_rows[b * LEN:b * LEN + 1, :], d["cls_tok"]).then_inc(rows_stored, 16)
            for g in range(2):
                sp.wait_ge(rec_ready, g + 1)
                for b in range(4):
                    first = (4 * g + b) * LEN + 1
                    sp.dma_start(h0_rows[first:first + SIDE, :].rearrange("(r j) c -> r j c", j=8),
                                 rec[32 * b:32 * b + 32, g]).then_inc(rows_stored, 16)
            sp.wait_ge(rows_stored, 16 * 16)
            sp.wait_ge(zeroed, 1)
            by_image = h0_rows.rearrange("(i t) c -> t i c", t=LEN)
            for q in range(2):
                sp.dma_start(h_all[:, :, q], by_image[q * P:(q + 1) * P]).then_inc(h0_loaded, 16)
            sp.dma_start(h_all[0:1, :, 2], by_image[2 * P:LEN]).then_inc(h0_loaded, 16)
            def load_weights(e, par):
                sp.dma_start(w1e[par].rearrange("p a b -> p (a b)"),
                             d["w1"][ds(e, 1)].rearrange("e p n -> (e p) n")).then_inc(w_loaded[par], 16)
                sp.dma_start(w2e[par].rearrange("p a b -> p (a b)"),
                             d["w2"][ds(e, 1)].rearrange("e p n -> (e p) n")).then_inc(w_loaded[par], 16)

            def store_norm2(i, par):
                sp.wait_ge(n2_ready, i + 1)
                sp.dma_start(n2_rows[ds(i * LEN, 2 * P)].rearrange("(q p) c -> p q c", p=P),
                             turn_src[:, 0:2]).then_inc(n2_stored, 16)
                sp.dma_start(n2_rows[ds(i * LEN + 2 * P, 1)], turn_src[0:1, 2]).then_inc(n2_stored, 16)

            def store_expert(e, par):
                sp.wait_ge(eo_done, e + 1)
                sp.dma_start(outs0[ds(e * CAP, CAP)].rearrange("(q p) c -> p q c", p=CAPP),
                             expert_rows[par][0:CAPP]).then_inc(eo_stored[par], 16)

            def expert(e, par):
                store_expert(e, par)
                load_weights(e + 2, par)

            sp.wait_ge(fold_done, CH)
            sp.wait_ge(bc_ready, 1)
            load_weights(0, 0)
            staged(sp, 0, IMAGES - 1, store_norm2)
            sp.wait_ge(log_saved, IMAGES)
            load_weights(1, 1)
            sp.dma_start(b2_rows.rearrange("p a b -> p (a b)"), d["b2"].partition_broadcast(P)).then_inc(ld_b, 16)
            sp.dma_start(b1_cols[:], d["b1"]).then_inc(ld_b, 16)
            staged(sp, 0, EXP0 - 3, expert)
            store_expert(EXP0 - 2, 0)
            for t, n in ((w_qkr, "w_qk"), (w_v, "w_v"), (rope, "rope")):
                sp.dma_start(t, d[n]).then_inc(ld_att, 16)
            sp.dma_start(qk_bias, d["qk_bias"]).then_inc(ld_att, 16)
            sp.dma_start(bv_rows, d["bv"].partition_broadcast(P)).then_inc(ld_att, 16)
            store_expert(EXP0 - 1, 1)
            sp.dma_start(wg1, d["wg1"]).then_inc(ld_shared, 16)
            sp.dma_start(ws13, d["ws13"]).then_inc(ld_shared, 16)
            sp.dma_start(ws2[0:DK], d["ws2"]).then_inc(ld_shared, 16)
            sp.dma_start(bias1[:], d["gate_bias"].partition_broadcast(P)).then_inc(ld_w1, 16)

            def load_experts(i):
                sp.dma_start(w13[:, ds(2 * i, 2)].rearrange("p e h n -> p (e h n)"),
                             d["w13"].rearrange("p (e n) -> p e n", e=EXP1)[:, ds(2 * i, 2)].rearrange("p e n -> p (e n)"))\
                    .then_inc(ld_w1, 16)
                sp.dma_start(w2s[0:DK, ds(2 * i, 2)].rearrange("p e k n -> p (e k n)"),
                             d["w2s"].rearrange("p (e n) -> p e n", e=EXP1)[:, ds(2 * i, 2)].rearrange("p e n -> p (e n)"))\
                    .then_inc(ld_w1, 16)

            def store_norm(i, par):
                sp.wait_ge(n4_ready, i + 1)
                load_experts(i)
                sp.dma_start(n4_rows[ds(i * LEN, 2 * P)].rearrange("(q p) c -> p q c", p=P),
                             turn_src4[:, 0:2]).then_inc(n4_stored, 16)
                sp.dma_start(n4_rows[ds(i * LEN + 2 * P, 1)], turn_src4[0:1, 2]).then_inc(n4_stored, 16)

            staged(sp, 0, IMAGES - 1, store_norm)
            sp.wait_ge(n4_stored, 32 * IMAGES)
            if phases == 4:
                sp.wait_ge(acc_done, IMAGES)
                sp.dma_start(d["out"][:, 0:6144], h_all[:].rearrange("p i q c -> p (i q c)")).then_inc(stored, 16)
                sp.dma_start(d["out"][:, 6144:6528], logit1.rearrange("p q e -> p (q e)")).then_inc(stored, 16)
                sp.wait_ge(stored, 32)

            sp.wait_ge(weights_ready, 1)
            sp.dma_start(last_weights, weight1[0:IMAGES, T1 - 1, :]).then_inc(weights_out, 16)
            sp.wait_ge(weights_out, 16)
            sp.dma_start(last_w[:], last_weights.rearrange("(o i) k -> o (i k)", o=1)).then_inc(last_w_in, 16)
            for k in range(4):
                sp.wait_ge(y_sent[k], 16 * NT1 // 4)
            y_rows = outs1.rearrange("(k i t) c -> i t k c", k=TOPK, t=LEN)
            o_rows = d["out"].rearrange("(i t) c -> i t c", t=LEN)

            def load_sum(i, r):
                for q in range(2):
                    sp.dma_start(ysum[r][:, :, q], y_rows[ds(i, 1), q * P:(q + 1) * P].rearrange(
                        "i t k c -> (i t) k c")).then_inc(ys_in[r], 16)
                sp.dma_start(ysum[r][0:1, :, 2], y_rows[ds(i, 1), 2 * P:LEN].rearrange(
                    "i t k c -> (i t) k c")).then_inc(ys_in[r], 16)

            def store_out(i):
                sp.wait_ge(y_done2, i + 1)
                sp.dma_start(o_rows[ds(i, 1), 0:2 * P].rearrange("i (q p) c -> p (i q) c", p=P),
                             h_all[:, ds(i, 1), 0:2].rearrange("p i q c -> p (i q) c")).then_inc(stored, 16)
                sp.dma_start(o_rows[ds(i, 1), 2 * P:LEN].rearrange("i t c -> (i t) c"),
                             h_all[0:1, ds(i, 1), 2].rearrange("p i c -> p (i c)")).then_inc(stored, 16)

            for i in range(4):
                load_sum(i, i)
            for i in range(IMAGES):
                store_out(i)
                if i + 4 < IMAGES:
                    load_sum(i + 4, i)
            sp.wait_ge(stored, 32 * IMAGES)

        @block.vector
        def _(dve):
            v = Signals(dve_done)
            lns = Signals(var_ready)

            def run(ins):
                v.on(ins)

            def chain():
                dve.wait_ge(dve_done, v.now())

            def tt(o, a, b, op):
                run(nc.vector.tensor_tensor(o, a, b, op))

            def haar(cur, R, C, bands, A):
                pairs = cur.rearrange("p r (c t) -> p r c t", t=2)
                s = sumc[:, 0:R * C // 2].rearrange("p (r c) -> p r c", r=R)
                f = difc[:, 0:R * C // 2].rearrange("p (r c) -> p r c", r=R)
                tt(s, pairs[:, :, :, 0], pairs[:, :, :, 1], ALU.add)
                tt(f, pairs[:, :, :, 0], pairs[:, :, :, 1], ALU.subtract)
                chain()
                s2 = s.rearrange("p (r t) c -> p t r c", t=2)
                f2 = f.rearrange("p (r t) c -> p t r c", t=2)
                bv = bands.rearrange("p (s r c) -> p s r c", s=3, r=R // 2)
                Av = A.rearrange("p (r c) -> p r c", r=R // 2)
                tt(Av, s2[:, 0], s2[:, 1], ALU.add)
                tt(bv[:, 0], s2[:, 0], s2[:, 1], ALU.subtract)
                tt(bv[:, 1], f2[:, 0], f2[:, 1], ALU.add)
                tt(bv[:, 2], f2[:, 0], f2[:, 1], ALU.subtract)
                chain()
                return Av

            def ihaar(group, cur, R, C, bands, lev, out):
                bv = bands.rearrange("p (s r c) -> p s r c", s=3, r=R)
                g = lambda k, s: gl[:, 4 + (s < 0), group, 1 + 3 * lev + k:2 + 3 * lev + k]
                lo = sumc[:, 0:2 * R * C].rearrange("p (r t c) -> p t r c", t=2, c=C)
                hi = difc[:, 0:2 * R * C].rearrange("p (r t c) -> p t r c", t=2, c=C)
                vv = vw[:, 0:R * C].rearrange("p (r c) -> p r c", r=R)
                run(nc.vector.tensor_scalar(vv, bv[:, 1], g(1, 1), None, ALU.mult))
                run(nc.vector.scalar_tensor_tensor(lo[:, 0], bv[:, 0], g(0, 1), cur, ALU.mult, ALU.add))
                run(nc.vector.scalar_tensor_tensor(lo[:, 1], bv[:, 0], g(0, -1), cur, ALU.mult, ALU.add))
                chain()
                run(nc.vector.scalar_tensor_tensor(hi[:, 0], bv[:, 2], g(2, 1), vv, ALU.mult, ALU.add))
                run(nc.vector.scalar_tensor_tensor(hi[:, 1], bv[:, 2], g(2, -1), vv, ALU.mult, ALU.add))
                chain()
                lo = sumc[:, 0:2 * R * C].rearrange("p (r c) -> p r c", c=C)
                hi = difc[:, 0:2 * R * C].rearrange("p (r c) -> p r c", c=C)
                pairs = out.rearrange("p r (c t) -> p r c t", t=2)
                tt(pairs[:, :, :, 0], lo, hi, ALU.add)
                tt(pairs[:, :, :, 1], lo, hi, ALU.subtract)
                chain()

            def settle():
                nc.vector.memset(scratch_dve[:], 0.0)

            def statistics(src, n, rows=P, at=0):
                st, ag = lnst[0:rows, at:at + n], lnstat[0:rows, at:at + n]
                settle()
                for k in range(n):
                    run(nc.vector.bn_stats(st[:, k, :], src[:, k, :]))
                chain()
                settle()
                for k in range(n):
                    last = nc.vector.bn_aggr(ag[:, k, 0:2], st[:, k, :])
                    if k < n - 1:
                        run(last)
                last.then_inc(var_ready, 1)
                lns.k += 1
                return lns.now()

            def normalise(dst, src, n, count, rows=P, ends=None, at=0):
                dve.wait_ge(rstd_ready, count)
                ag = lnstat[0:rows, at:at + n]
                for k in range(n):
                    ins = nc.vector.tensor_scalar(dst[:, k, :], src[:, k, :], ag[:, k, 0:1], ag[:, k, 2:3],
                                                  ALU.subtract, ALU.mult)
                    if k == n - 1 and ends is not None:
                        ins.then_inc(ends, 1)
                    else:
                        run(ins)

            def layernorm(dst, src, n, rows=P, ends=None):
                normalise(dst, src, n, statistics(src, n, rows), rows, ends)

            def analyse(g):
                A1, A2, A3, B1, B2, B3 = bands_of[g]
                dve.wait_ge(ld_img[g], 16)
                a1 = haar(img[:, g], 8, 256, B1, A1)
                a2 = haar(a1, 4, 128, B2, A2)
                haar(a2, 2, 64, B3, A3)

            def dots(g, cols):
                A1, A2, A3, B1, B2, B3 = bands_of[g]
                for col in cols:
                    b, w, n, scale = ((A3, w_a, 32, 1 / 8), *((B3, w_l3[:, :, j], 96, 1 / 8) for j in range(3)),
                                      *((B2, w_l2[:, :, j], 384, 1 / 4) for j in range(3)),
                                      *((B1, w_l1[:, :, j], 1536, 1 / 2) for j in range(3)))[col]
                    ins = nc.vector.tensor_tensor_reduce(dot_out[:, 0:n], b, w, scale, 0.0, ALU.mult, ALU.add,
                                                         partial[:, g, col:col + 1])
                    if (g, col) == (1, 9):
                        ins.then_inc(dots_ready, 1)
                    else:
                        run(ins)
                        chain()

            analyse(0)
            dve.wait_ge(ld_wav, 14 * 16)
            dots(0, range(7))
            analyse(1)
            dots(1, range(7))
            cls_rows = cls[0:1].rearrange("p (k c) -> p k c", k=2)
            count = statistics(cls_rows[:, 0:1], 1, 1)
            dve.wait_ge(ld_wav1, 4 * 16)
            dots(0, range(7, 10))
            normalise(cls_rows[:, 1:2], cls_rows[:, 0:1], 1, count, 1)
            chain()
            nc.vector.tensor_copy(gl[0:1, 7, 0, 0:1], cls[0:1, 0:1]).then_inc(normed_ready, 1)
            dots(1, range(7, 10))
            dve.wait_ge(sums_ready, 1)
            lg, ex = gl[:, 0], gl[:, 1]
            tt(lg, bank[0][:, 0:20].rearrange("p (g n) -> p g n", g=2), gbias.unsqueeze(1).broadcast_to([P, 2, 10]), ALU.add)
            chain()
            triples = lambda a: a[:, :, 1:10].rearrange("p g (l k) -> p g l k", k=3)
            spread = lambda a: a.unsqueeze(3).broadcast_to([P, 2, 3, 3])
            run(nc.vector.tensor_reduce(gl[:, 2, :, 0:3], triples(lg), AX.X, ALU.max))
            chain()
            tt(triples(lg), triples(lg), spread(gl[:, 2, :, 0:3]), ALU.subtract)
            nc.vector.tensor_scalar(lg[:, :, 0:1], lg[:, :, 0:1], -1.0, None, ALU.mult).then_inc(logit_ready, 1)
            dve.wait_ge(exp_ready, 1)
            run(nc.vector.tensor_reduce(gl[:, 3, :, 0:3], triples(ex), AX.X, ALU.add))
            run(nc.vector.tensor_scalar(gl[:, 3, :, 3:4], ex[:, :, 0:1], 1.0, None, ALU.add))
            chain()
            run(nc.vector.reciprocal(gl[:, 3, :, 4:8], gl[:, 3, :, 0:4]))
            chain()
            tt(triples(gl[:, 4]), triples(ex), spread(gl[:, 3, :, 4:7]), ALU.mult)
            run(nc.vector.tensor_copy(gl[:, 4, :, 0:1], gl[:, 3, :, 7:8]))
            chain()
            tt(gl[:, 4], gl[:, 4], misc[:, M_SCALE:M_SCALE + 10].unsqueeze(1).broadcast_to([P, 2, 10]), ALU.mult)
            chain()
            run(nc.vector.tensor_scalar(gl[:, 5], gl[:, 4], -1.0, None, ALU.mult))
            chain()

            def synthesise(g):
                A1, A2, A3, B1, B2, B3 = bands_of[g]
                run(nc.vector.tensor_scalar(A3g, A3, gl[:, 4, g, 0:1], None, ALU.mult))
                chain()
                ihaar(g, A3g.rearrange("p (r c) -> p r c", r=1), 1, 32, B3, 0, R2.rearrange("p (r c) -> p r c", r=2))
                ihaar(g, R2.rearrange("p (r c) -> p r c", r=2), 2, 64, B2, 1, R1.rearrange("p (r c) -> p r c", r=4))
                ihaar(g, R1.rearrange("p (r c) -> p r c", r=4), 4, 128, B1, 2, rec[:, g])
                nc.vector.tensor_copy(gl[:, 7, 0, 0:1], rec[:, g, 7, 255:256]).then_inc(rec_ready, 1)

            def norm_group(g, count):
                if g == 1:
                    dve.wait_ge(turned, 1 + 4)
                normalise(normed, rec[:, g], 8, count)
                chain()
                nc.vector.tensor_copy(gl[:, 7, 0, 1:2], normed[:, 7, 255:256]).then_inc(normed_ready, 1)

            synthesise(0)
            count = statistics(rec[:, 0], 8)
            synthesise(1)
            norm_group(0, count)
            count = statistics(rec[:, 1], 8)
            dve.wait_ge(ld_mix, 7 * 16)
            run(nc.vector.tensor_reduce(w_bcs[:], w_bc[:].rearrange("p k (b s) -> p k b s", s=STATE), AX.X, ALU.add))
            chain()
            for b in range(2):
                run(nc.vector.tensor_copy(w_bcr[:, b], w_bcs[:, :, b:b + 1].broadcast_to([P, CH, P])))
            chain()
            norm_group(1, count)
            nc.vector.tensor_copy(gl[:, 7, 0, 2:3], w_bcr[:, 1, 0, 0:1]).then_inc(bc_ready, 1)
            if phases == 1:
                return

            def taps(n, pair):
                for k in (2, 1, 0):
                    off = TAPS - 1 - k
                    for c in pair:
                        if k == 2:
                            dve.wait_ge(tap_done, 4 * n + (c + 1))
                        ins = nc.vector.scalar_tensor_tensor(conv[:, c, off:LEN], bank[c][:, 0:LEN - off],
                                                             chan[:, c, k:k + 1], conv[:, c, off:LEN], ALU.mult, ALU.add)
                        if k == 0 and c == pair[-1]:
                            ins.then_inc(conv_done, 1)
                        else:
                            run(ins)
                    if k:
                        chain()

            def step_size(i, par):
                dve.wait_ge(soft_ready, i + 1)
                nc.vector.scalar_tensor_tensor(dts, xb, 0.0, soft, ALU.max, ALU.subtract).then_inc(dt_done, 1)
                run(nc.vector.tensor_scalar(bct[par][:, 0], bct[par][:, 0], -0.25, -0.25, ALU.mult, ALU.add))
                run(nc.vector.tensor_scalar(bct[par][:, 1], bct[par][:, 1], 0.5, 0.5, ALU.mult, ALU.add))

            def gate(par, b):
                return bct[par][:, b:b + 1, :].broadcast_to([P, CH, LEN])

            def recur(i, par):
                chain()
                tt(gat, xconv[par], gate(par, 0), ALU.mult)
                dve.wait_ge(e_done, i + 1)
                run(nc.vector.tensor_scalar(al, es[par], 0.5, 0.5, ALU.mult, ALU.add))
                chain()
                run(nc.vector.scalar_tensor_tensor(gat, es[par], 1.0, gat, ALU.subtract, ALU.mult))
                run(nc.vector.tensor_scalar(al, al, 0.01, 0.99, ALU.max, ALU.min))
                chain()
                for c in range(CH):
                    run(nc.vector.tensor_tensor_scan(hs[:, c], al[:, c], gat[:, c], 0.0, ALU.mult, ALU.add))

            def read_out(i, par):
                chain()
                tt(hs, hs, gate(par, 1), ALU.mult)
                chain()
                for c in range(CH):
                    run(nc.vector.scalar_tensor_tensor(hs[:, c], xconv[par][:, c], chan[:, c, 6:7], hs[:, c],
                                                       ALU.mult, ALU.add))
                chain()
                after(dve, out_ready, 2 * i - 2)
                nc.vector.tensor_tensor(ys[par], hs, zs[par], ALU.mult).then_inc(y_ready, 1)

            def rows_of(i):
                return h_all[:, ds(i, 1)].rearrange("p i q c -> p (i q) c")

            def residual(i):
                dve.wait_ge(tok_ready, i + 1)
                pair = bank[2][:, :].rearrange("p (q c) -> p q c", q=2)
                h2 = h_all[:, ds(i, 1), 0:2].rearrange("p i q c -> p (i q) c")
                h3 = h_all[0:1, ds(i, 1), 2].rearrange("p i c -> p (i c)")
                tt(h2, h2, pair, ALU.add)
                nc.vector.tensor_tensor(h3, h3, bank[3][0:1, 0:HID], ALU.add).then_inc(res_done, 1)
                dve.wait_ge(res_done, i + 1)
                return statistics(rows_of(i), TILES)

            def save_logits(i):
                dve.wait_ge(log_ready, i + 1)
                lg = bank[3][:, 300:300 + TILES * EXP0].rearrange("p (q e) -> p q e", q=TILES)
                run(nc.vector.tensor_copy(logit0[:, ds(i, 1), 0:2].rearrange("p i q e -> p (i q) e"), lg[:, 0:2]))
                nc.vector.tensor_copy(logit0[0:1, ds(i, 1), 2].rearrange("p i e -> p (i e)"), lg[0:1, 2]).then_inc(log_saved, 1)


            def stage(n, par, a=True, b=True, c=True, d=True):
                if a:
                    taps(n, (0, 1))
                if d:
                    save_logits(n - 3)
                if a:
                    taps(n, (2, 3))
                if b:
                    step_size(n - 1, 1 - par)
                    recur(n - 1, 1 - par)
                if c:
                    count = residual(n - 2)
                if b:
                    read_out(n - 1, 1 - par)
                if c:
                    after(dve, n2_stored, 32 * (n - 2))
                    after(dve, n2_turned, n - 2)
                    normalise(turn_src, rows_of(n - 2), TILES, count, ends=n2_ready)

            stage(0, 0, b=False, c=False, d=False)
            stage(1, 1, c=False, d=False)
            dve.wait_ge(h0_loaded, 48)
            stage(2, 0, d=False)
            staged(dve, 3, 6, stage, ((v, PER_MIX), (lns, 2)))
            stage(7, 1)
            stage(IMAGES, 0, a=False)
            stage(IMAGES + 1, 1, a=False, b=False)
            stage(IMAGES + 2, 0, a=False, b=False, c=False)

            T0 = IMAGES * TILES
            wide = lambda a: a.unsqueeze(2).broadcast_to([P, T0, EXP0])
            row_of = lambda off, n: misc[:, off:off + n].unsqueeze(1).broadcast_to([P, T0, n])
            lg = logit0[:].rearrange("p i q e -> p (i q) e")
            valid = misc[:, M_VALID:M_VALID + T0]
            mx, sm, posv, basev, keep, dest = (r_one[:, k] for k in range(6))
            chain()
            dve.wait_ge(log_saved, IMAGES)
            run(nc.vector.tensor_reduce(mx, lg, AX.X, ALU.max))
            chain()
            nc.vector.tensor_tensor(r_exp, lg, wide(mx), ALU.subtract).then_inc(shift_ready, 1)
            tt(r_hot, lg, wide(mx), ALU.is_equal)
            chain()
            tt(r_hot, r_hot, row_of(M_FIRST0, EXP0), ALU.mult)
            chain()
            run(nc.vector.tensor_reduce(mx, r_hot, AX.X, ALU.max))
            chain()
            tt(r_hot, r_hot, wide(mx), ALU.is_equal)
            chain()
            tt(r_hot, r_hot, wide(valid), ALU.mult)
            chain()

            def earlier_tiles(hot, a, b, n):
                run(nc.vector.memset(a[:, 0:1], 0.0))
                run(nc.vector.tensor_copy(a[:, 1:n], hot[:, 0:n - 1]))
                chain()
                step = 1
                while step < n:
                    tt(b[:, step:n], a[:, step:n], a[:, 0:n - step], ALU.add)
                    run(nc.vector.tensor_copy(b[:, 0:step], a[:, 0:step]))
                    chain()
                    a, b, step = b, a, 2 * step
                return a

            cum = earlier_tiles(r_hot, r_cum, r_tmp, T0)
            assert cum is r_tmp
            nc.vector.tensor_copy(gl7[:], r_hot[:, 0, 0:1]).then_inc(hot_ready, 1)
            dve.wait_ge(exps_ready, 1)
            run(nc.vector.tensor_reduce(sm, r_exp, AX.X, ALU.add))
            tt(r_cum, r_hot, row_of(M_BASE0, EXP0), ALU.mult)
            chain()
            run(nc.vector.reciprocal(sm, sm))
            run(nc.vector.tensor_reduce(basev, r_cum, AX.X, ALU.add))
            dve.wait_ge(pos_ready, 1)
            chain()
            tt(r_cum, r_hot, bank[0][:, 0:T0 * EXP0].rearrange("p (t e) -> p t e", e=EXP0), ALU.mult)
            chain()
            run(nc.vector.tensor_reduce(posv, r_cum, AX.X, ALU.add))
            chain()
            run(nc.vector.tensor_scalar(keep, posv, float(CAP), None, ALU.is_lt))
            tt(dest, posv, basev, ALU.add)
            chain()
            tt(keep, keep, valid, ALU.mult)
            chain()
            tt(gate0[:], sm, keep, ALU.mult)
            tt(posv, dest, keep, ALU.mult)
            run(nc.vector.scalar_tensor_tensor(dest, dest, -FAR, keep, ALU.add, ALU.mult))
            chain()
            run(nc.vector.tensor_copy(slot_from[:], posv))
            run(nc.vector.tensor_scalar(slot_no0, dest, FAR, None, ALU.add))
            chain()
            run(nc.vector.tensor_scalar(slot_tile0, slot_no0, 1.0 / CAPP, 0.5 / CAPP - 0.5, ALU.mult, ALU.add))
            chain()
            run(nc.vector.tensor_scalar(slot_tile0, slot_tile0, ROUND, ROUND, ALU.add, ALU.subtract))
            chain()
            run(nc.vector.scalar_tensor_tensor(slot_lane0, slot_tile0, -float(CAPP), slot_no0, ALU.mult, ALU.add))
            for hot, width, base, at in ((tile_hot0, SLOT_TILES, M_TILE, slot_tile0), (lane_hot0, CAPP, M_LANE, slot_lane0)):
                tt(hot, misc[:, base:base + width].unsqueeze(1).broadcast_to([P, T0, width]),
                   at.unsqueeze(2).broadcast_to([P, T0, width]), ALU.is_equal)
                chain()
            nc.vector.tensor_tensor(tile_hot0, tile_hot0, misc[:, M_ROW0:M_ROW0 + T0].unsqueeze(2).broadcast_to(
                [P, T0, SLOT_TILES]), ALU.mult).then_inc(hots0_ready, 1)
            dve.wait_ge(table0_ready, 1)
            nc.vector.tensor_scalar(slot_src[0:CAPP], bank[1][0:CAPP, 0:SLOT_TILES], -1.0, 0.0,
                                    ALU.add, ALU.max).then_inc(slots_ready, 1)

            def slots_out(e, par):
                dve.wait_ge(xt_ready, e + 1)
                run(nc.vector.tensor_copy(slotT[par][:, 0], bank[0][:, 0:CAP]))
                nc.vector.tensor_copy(slotT[par][:, 1], bank[1][:, 0:CAP]).then_inc(xt_done, 1)

            def expert(e, par, more=True):
                if more:
                    slots_out(e + 1, 1 - par)
                dve.wait_ge(eo_ready, e + 1)
                after(dve, eo_stored[par], 8 * (e - par))
                b2 = b2_rows[0:CAPP, ds(e, 1), :]
                run(nc.vector.tensor_tensor(expert_rows[par][0:CAPP, 0:2],
                                            bank[6][0:CAPP, :].rearrange("p (q c) -> p q c", q=2),
                                            b2.broadcast_to([CAPP, 2, HID]), ALU.add))
                nc.vector.tensor_tensor(expert_rows[par][0:CAPP, 2:3], bank[7][0:CAPP, 0:HID].unsqueeze(1), b2,
                                        ALU.add).then_inc(eo_done, 1)

            dve.wait_ge(ld_b, 32)
            slots_out(0, 0)
            expert(0, 0)
            expert(1, 1)
            staged(dve, 2, 5, expert, ((v, 4),))
            expert(6, 0)

            dve.wait_ge(ld_att, 16 * 5)
            raw, fold = (w.rearrange("p h (o t) -> p (h o) t", t=2) for w in (w_qkr, w_qk))
            tt(fold[:, :, 0], raw[:, :, 0], raw[:, :, 1], ALU.subtract)
            tt(fold[:, :, 1], raw[:, :, 0], raw[:, :, 1], ALU.add)
            run(nc.vector.scalar_tensor_tensor(qk_bias[:, 0:4], qk_bias[:, 4:8], qk_bias[:, 8:9], qk_bias[:, 0:4],
                                               ALU.mult, ALU.add))
            chain()
            run(nc.vector.memset(logit1[:], 0.0))
            nc.vector.tensor_copy(gl7[:], w_qk[:, 1, 511:512]).then_inc(w_qk_ready, 1)

            expert(7, 1, more=False)

            def combine(i, par):
                dve.wait_ge(fetched_in[par], 24 * (i + (2 - par)))
                for q in range(TILES):
                    k = ROWS[q]
                    h = h_all[0:k, ds(i, 1), q].rearrange("p i c -> p (i c)")
                    g = gate0[0:k, ds(i * TILES + q, 1)]
                    ins = nc.vector.scalar_tensor_tensor(h, fetched[par][0:k, q], g, h, ALU.mult, ALU.add)
                    run(ins) if q < TILES - 1 else ins.then_inc(h2_done, 1)
                after(dve, h2_done, i + 1)
                return statistics(rows_of(i), TILES, at=4)

            def combined(i, count):
                after(dve, n3_turned, i)
                normalise(turn_src, rows_of(i), TILES, count, ends=n3_ready, at=4)

            def maxima(i, par):
                for q in range(TILES):
                    k = ROWS[q]
                    dve.wait_ge(s_ready, 3 * i + (q + 1))
                    if q == 0:
                        after(dve, p_ready, 3 * i)
                    run(nc.vector.tensor_reduce(soft_c[0:k, q:q + 1], bank[2 + q][0:k, 0:LEN], AX.X, ALU.max))
                chain()
                for q in range(TILES):
                    k = ROWS[q]
                    nc.vector.tensor_scalar(soft_c[0:k, 3 + q:4 + q], soft_c[0:k, q:q + 1], -float(HEAD) ** -0.5, None,
                                            ALU.mult).then_inc(m_ready, 1)

            def rotate(n, quarters):
                after(dve, s_ready, 3 * n)
                for g in quarters:
                    dve.wait_ge(qk_ready, 4 * n + (g + 1))
                    nc.vector.scalar_tensor_tensor(qkT[:, g], bank[g % 2][:, 0:LEN], qk_bias[:, g:g + 1],
                                                   rope[:, g % 2], ALU.add, ALU.mult).then_inc(qk_done, 1)

            def save_logits1(j):
                dve.wait_ge(lg1_ready, j + 1)
                lg = bank[7][:, 300:300 + 2 * EXP1].rearrange("p (q e) -> p q e", q=2)
                nc.vector.tensor_copy(logit1[:, ds(j * 2, 2)], lg[:, 0:2]).then_inc(lg1_saved, 1)

            def shared_gate(j, q):
                k = ROWS[q]
                if q == 0:
                    after(dve, ht_ready, 2 * j)
                dve.wait_ge(sg_done, 3 * j + (q + 1))
                nc.vector.tensor_tensor(gated[0:k, q], silu_g[0:k, q], bank[6 + q % 2][0:k, DFE:2 * DFE],
                                        ALU.mult).then_inc(hs_done, 1)

            def values(n, par):
                dve.wait_ge(v_ready, n + 1)
                after(dve, o_ready, 2 * n - 2)
                run(nc.vector.tensor_tensor(vals[par][:, 0:2], bank[0][:, :].rearrange("p (q c) -> p q c", q=2),
                                            bv_rows.unsqueeze(1).broadcast_to([P, 2, HID]), ALU.add))
                nc.vector.tensor_tensor(vals[par][0:1, 2], bank[1][0:1, 0:HID], bv_rows[0:1], ALU.add).then_inc(v_done, 1)

            def shared_out(j):
                dve.wait_ge(mm2_ready, j + 1)
                h2 = h_all[:, ds(j, 1), 0:2].rearrange("p i q c -> p (i q) c")
                h3 = h_all[0:1, ds(j, 1), 2].rearrange("p i c -> p (i c)")
                run(nc.vector.tensor_tensor(h2, h2, bank[6][:, :].rearrange("p (q c) -> p q c", q=2), ALU.add))
                nc.vector.tensor_tensor(h3, h3, bank[7][0:1, 0:HID], ALU.add).then_inc(acc_done, 1)

            def attended(i, par):
                dve.wait_ge(tokens_ready, i + 1)
                dve.wait_ge(p_ready, 3 * i + 3)
                run(nc.vector.reciprocal(soft_c[:, 9:11], soft_c[:, 6:8]))
                run(nc.vector.reciprocal(soft_c[0:1, 11:12], soft_c[0:1, 8:9]))
                chain()
                for q in range(TILES):
                    k = ROWS[q]
                    h = h_all[0:k, ds(i, 1), q].rearrange("p i c -> p (i c)")
                    o = bank[2][0:k, q * HID:(q + 1) * HID] if q < 2 else bank[3][0:1, 0:HID]
                    ins = nc.vector.scalar_tensor_tensor(h, o, soft_c[0:k, 9 + q:10 + q], h, ALU.mult, ALU.add)
                    run(ins) if q < TILES - 1 else ins.then_inc(h3_done, 1)
                after(dve, h3_done, i + 1)
                statistics(rows_of(i), TILES)

            def attended_norm(i, count):
                after(dve, n4_turned, i)
                after(dve, n4_stored, 32 * i)
                normalise(turn_src4, rows_of(i), TILES, count, ends=n4_ready)

            def stage(n, par, a=True, b=True, c=True, ahead=True):
                if b:
                    maxima(n - 1, 1 - par)
                if c:
                    attended_norm(n - 2, lns.now())
                if a:
                    rotate(n, range(4))
                if c:
                    save_logits1(n - 2)
                    for q in range(TILES):
                        shared_gate(n - 2, q)
                if ahead:
                    ahead_count = combine(n + 1, 1 - par)
                if a:
                    values(n, par)
                if ahead:
                    combined(n + 1, ahead_count)
                if c:
                    shared_out(n - 2)
                if b:
                    attended(n - 1, 1 - par)

            combined(0, combine(0, 0))
            stage(0, 0, b=False, c=False)
            stage(1, 1, c=False)
            stage(2, 0)
            staged(dve, 3, 6, stage, ((v, PER_ATT), (lns, 4)))
            stage(7, 1, ahead=False)
            stage(8, 0, a=False, ahead=False)
            attended_norm(IMAGES - 1, lns.now())
            save_logits1(IMAGES - 1)

            dve.wait_ge(ld_w1, 16 + 32 * EXP1 // 2)
            dve.wait_ge(last_lg, 1)
            run(nc.vector.tensor_copy(logit1[0:IMAGES, T1 - 1], bank[0][0:IMAGES, 0:EXP1]))
            chain()
            nc.vector.tensor_scalar(score, logit1[:], -1.0, None, ALU.mult).then_inc(sg_shift, 1)
            dve.wait_ge(sg_exp, 1)
            run(nc.vector.tensor_scalar(score, score, 1.0, None, ALU.add))
            chain()
            run(nc.vector.reciprocal(score, score))
            chain()
            tt(biased, score, bias1[:].unsqueeze(1).broadcast_to([P, T1, EXP1]), ALU.add)
            chain()
            quad = biased.rearrange("p t (g k) -> p (t g) k", g=GROUPS)
            hi1, lo1, hi2, lo2, top, mid_, low, gsum, gkeep, gpen = (g_all[:, k] for k in range(10))
            tt(hi1, quad[:, :, 0], quad[:, :, 1], ALU.max)
            tt(lo1, quad[:, :, 0], quad[:, :, 1], ALU.min)
            tt(hi2, quad[:, :, 2], quad[:, :, 3], ALU.max)
            tt(lo2, quad[:, :, 2], quad[:, :, 3], ALU.min)
            chain()
            tt(top, hi1, hi2, ALU.max)
            tt(mid_, hi1, hi2, ALU.min)
            tt(low, lo1, lo2, ALU.max)
            chain()
            tt(mid_, mid_, low, ALU.max)
            chain()
            tt(gsum, top, mid_, ALU.add)
            shared_gate(IMAGES - 1, 0)
            chain()
            gs = gsum.rearrange("p (t g) -> p t g", g=GROUPS)
            other = gs.unsqueeze(2).broadcast_to([P, T1, GROUPS, GROUPS])
            own = gs.unsqueeze(3).broadcast_to([P, T1, GROUPS, GROUPS])
            cmp = g_pair[:, 0].rearrange("p (t g k) -> p t g k", t=T1, g=GROUPS)
            same = g_pair[:, 1].rearrange("p (t g k) -> p t g k", t=T1, g=GROUPS)
            tt(cmp, other, own, ALU.is_gt)
            tt(same, other, own, ALU.is_equal)
            chain()
            tt(g_pair[:, 1].rearrange("p (t n) -> p t n", t=T1), g_pair[:, 1].rearrange("p (t n) -> p t n", t=T1),
               misc[:, M_LOWER:M_LOWER + GROUPS * GROUPS].unsqueeze(1).broadcast_to([P, T1, GROUPS * GROUPS]), ALU.mult)
            chain()
            tt(g_pair[:, 0], g_pair[:, 0], g_pair[:, 1], ALU.add)
            chain()
            run(nc.vector.tensor_reduce(gkeep, g_pair[:, 0].rearrange("p (n k) -> p n k", k=GROUPS), AX.X, ALU.add))
            chain()
            run(nc.vector.tensor_scalar(gkeep, gkeep, 2.0, None, ALU.is_lt))
            chain()
            run(nc.vector.tensor_scalar(gpen, gkeep, LOW, LOW, ALU.mult, ALU.subtract))
            four = lambda a: a.unsqueeze(2).broadcast_to([P, T1 * GROUPS, GROUPS])
            leftq = left.rearrange("p t (g k) -> p (t g) k", g=GROUPS)
            shared_gate(IMAGES - 1, 1)
            tt(leftq, quad, four(gkeep), ALU.mult)
            chain()
            tt(leftq, leftq, four(gpen), ALU.add)
            chain()
            exps = lambda a: a.unsqueeze(2).broadcast_to([P, T1, EXP1])
            best = one_k[:, 0, 0:T1]
            for k in range(TOPK):
                hot = hots[:, k].rearrange("p (t e) -> p t e", e=EXP1)
                run(nc.vector.tensor_reduce(best, left, AX.X, ALU.max))
                chain()
                tt(r1_tmp, left, exps(best), ALU.is_equal)
                chain()
                tt(r1_tmp, r1_tmp, misc[:, M_FIRST1:M_FIRST1 + EXP1].unsqueeze(1).broadcast_to([P, T1, EXP1]), ALU.mult)
                chain()
                run(nc.vector.tensor_reduce(best, r1_tmp, AX.X, ALU.max))
                chain()
                tt(hot, r1_tmp, exps(best), ALU.is_equal)
                chain()
                run(nc.vector.scalar_tensor_tensor(left, hot, -4.0 * LOW, left, ALU.mult, ALU.add))
                if k == 0:
                    run(nc.vector.tensor_copy(sel, hot))
                else:
                    tt(sel, sel, hot, ALU.add)
                if k == 0:
                    shared_gate(IMAGES - 1, 2)
                if k == 2:
                    shared_out(IMAGES - 1)
                chain()
            tt(sel, sel, exps(misc[:, M_VALID1:M_VALID1 + T1]), ALU.mult)
            chain()
            cum = earlier_tiles(sel, cumA, cumB, T1)
            assert cum is cumB
            tt(per_exp[:, 0], cum[:, T1 - 1], sel[:, T1 - 1], ALU.add)
            chain()
            nc.vector.tensor_copy(gl7[:], per_exp[:, 0, 0:1]).then_inc(ranks_in, 1)
            flat = lambda a: a.rearrange("p t e -> p (t e)")
            dve.wait_ge(cnt_ready, 1)
            cnt, tiles_of, first, other_, ends = (per_exp[:, k] for k in range(1, 6))
            run(nc.vector.tensor_copy(cnt, bank[1][:, 0:EXP1]))
            chain()
            tt(steps_c, cnt.unsqueeze(2).broadcast_to([P, EXP1, T1]),
               misc[:, M_STEPS:M_STEPS + T1].unsqueeze(1).broadcast_to([P, EXP1, T1]), ALU.is_gt)
            chain()
            run(nc.vector.tensor_reduce(tiles_of, steps_c, AX.X, ALU.add))
            chain()
            one = lambda a: a.unsqueeze(2)
            earlier_tiles(one(tiles_of), one(first), one(other_), EXP1)
            start = first
            tt(ends, start, tiles_of, ALU.add)
            run(nc.vector.tensor_scalar(cnt, start, float(P), None, ALU.mult))
            chain()
            dve.wait_ge(rank_ready, 1)
            tt(place, bank[0][:, 0:T1 * EXP1].rearrange("p (t e) -> p t e", e=EXP1),
               cnt.unsqueeze(1).broadcast_to([P, T1, EXP1]), ALU.add)
            chain()
            tt(hots2, hots, flat(place).unsqueeze(1).broadcast_to([P, TOPK, T1 * EXP1]), ALU.mult)
            chain()
            run(nc.vector.tensor_reduce(one_k[:, 2], hots2.rearrange("p k (t e) -> p (k t) e", e=EXP1), AX.X, ALU.add))
            chain()
            slot = one_k[:, 2].rearrange("p (k t) -> p k t", k=TOPK)
            run(nc.vector.tensor_scalar(slot_tile, slot, 1.0 / P, 1.0 / (2 * P) - 0.5, ALU.mult, ALU.add))
            for k in range(TOPK):
                run(nc.vector.tensor_scalar(row_no[:, k], misc[:, M_TOKEN:M_TOKEN + T1], float(k * TOKENS + 1), None, ALU.add))
            chain()
            run(nc.vector.tensor_scalar(slot_tile, slot_tile, ROUND, ROUND, ALU.add, ALU.subtract))
            chain()
            run(nc.vector.scalar_tensor_tensor(slot_lane, slot_tile, -float(P), slot, ALU.mult, ALU.add))
            chain()

            def one_hots(t, par):
                after(dve, hots_used, t - 3)
                for hot, width, base, at in ((lane_hot, P, M_LANE, slot_lane), (tile_hot, NT1, M_TILE, slot_tile)):
                    ins = nc.vector.tensor_tensor(
                        hot[par], misc[:, base:base + width].unsqueeze(1).broadcast_to([P, TOPK, width]),
                        at[:, :, ds(t, 1)].broadcast_to([P, TOPK, width]), ALU.is_equal)
                    run(ins) if hot is lane_hot else ins.then_inc(hots_ready, 1)

            for r in range(4):
                one_hots(r, r)
            fours(dve, one_hots, ((v, 4),))
            one_hots(T1 - 1, 0)
            tt(tile_cmp[0:1], ends[0:1].unsqueeze(1).broadcast_to([1, NT1, EXP1]),
               misc[0:1, M_TILE:M_TILE + NT1].unsqueeze(2).broadcast_to([1, NT1, EXP1]), ALU.is_le)
            chain()
            run(nc.vector.tensor_reduce(tile_no[:], tile_cmp[0:1], AX.X, ALU.add))
            chain()
            run(nc.vector.tensor_scalar(tile_exp[:], tile_no[:], float(EXP1 - 1), None, ALU.min))
            dve.wait_ge(hots_used, T1)
            number, above, more_, empty = (slot_row[:, k] for k in range(4))
            run(nc.vector.tensor_copy(number, bank[2][:, 0:NT1]))
            chain()
            run(nc.vector.tensor_scalar(above, number, float(TOKENS), -float(TOKENS), ALU.is_gt, ALU.mult))
            run(nc.vector.tensor_scalar(empty, number, 0.0, FAR, ALU.is_equal, ALU.mult))
            for k in range(2, TOPK):
                run(nc.vector.tensor_scalar(more_, number, float(k * TOKENS), -float(TOKENS), ALU.is_gt, ALU.mult))
                chain()
                tt(above, above, more_, ALU.add)
                chain()
            run(nc.vector.scalar_tensor_tensor(rec_idx[:, :, 1], number, -1.0, empty, ALU.add, ALU.add))
            tt(above, above, number, ALU.add)
            chain()
            nc.vector.tensor_scalar(rec_idx[:, :, 0], above, -1.0, 0.0, ALU.add, ALU.max).then_inc(idx_ready, 1)
            tt(hots2, hots, flat(score).unsqueeze(1).broadcast_to([P, TOPK, T1 * EXP1]), ALU.mult)
            chain()
            wk = one_k[:, 1].rearrange("p (k t) -> p k t", k=TOPK)
            run(nc.vector.tensor_reduce(one_k[:, 1], hots2.rearrange("p k (t e) -> p (k t) e", e=EXP1), AX.X, ALU.add))
            chain()
            total = one_k[:, 0, 0:T1]
            tt(total, wk[:, 0], wk[:, 1], ALU.add)
            chain()
            tt(total, total, wk[:, 2], ALU.add)
            chain()
            tt(total, total, wk[:, 3], ALU.add)
            chain()
            run(nc.vector.tensor_scalar(total, total, 1e-20, None, ALU.add))
            chain()
            run(nc.vector.reciprocal(total, total))
            chain()
            tt(wk, wk, total.unsqueeze(1).broadcast_to([P, TOPK, T1]), ALU.mult)
            chain()
            nc.vector.tensor_scalar(weight1[:].rearrange("p t k -> p k t"), wk, 2.5, None, ALU.mult).then_inc(weights_ready, 1)
            chain()

            def gate(j, par):
                dve.wait_ge(sg1_done, j + 1)
                after(dve, g1_turned, j - 1)
                nc.vector.tensor_tensor(gu1[par], sg1[par], bank[2 + par][:, DFE:2 * DFE], ALU.mult).then_inc(g1_done, 1)

            def rows_out(j, r):
                dve.wait_ge(y_ready2, j + 1)
                after(dve, y_sent[r], 4 * (j - r))
                nc.vector.tensor_copy(y1[r], bank[6 + r % 2][:, 0:HID]).then_inc(y_done, 1)

            for j in range(4):
                gate(j, j % 2)
                if j >= 2:
                    rows_out(j - 2, j - 2)
            gate(4, 0)
            rows_out(2, 2)
            gate(5, 1)
            rows_out(3, 3)
            with dve.Fori(0, (NT1 - 8) // 4) as p:
                for r in range(4):
                    gate(4 * p + (6 + r), r % 2)
                    rows_out(4 * p + (4 + r), r)
            gate(NT1 - 2, 0)
            rows_out(NT1 - 4, 0)
            gate(NT1 - 1, 1)
            rows_out(NT1 - 3, 1)
            rows_out(NT1 - 2, 2)
            rows_out(NT1 - 1, 3)

            def sum_up(i, r):
                dve.wait_ge(ys_in[r], 12 * (i + (4 - r)))
                for k in range(TOPK):
                    for q in range(2):
                        h = h_all[:, ds(i, 1), q].rearrange("p i c -> p (i c)")
                        ins = nc.vector.scalar_tensor_tensor(h, ysum[r][:, k, q], weight1[:, ds(2 * i + q, 1), k], h,
                                                             ALU.mult, ALU.add)
                        run(ins)
                    if k < TOPK - 1:
                        chain()
                dve.wait_ge(last_done, i + 1)
                h3 = h_all[0:1, ds(i, 1), 2].rearrange("p i c -> p (i c)")
                nc.vector.tensor_tensor(h3, h3, ysum[r][0:1, 0, 2], ALU.add).then_inc(y_done2, 1)

            with dve.Fori(0, IMAGES // 4) as p:
                with v.loop(p, IMAGES // 4, 32):
                    for r in range(4):
                        sum_up(4 * p + r, r)

        @block.gpsimd
        def _(pool):
            def settle(j, col):
                if not isinstance(j, int):
                    nc.gpsimd.tensor_tensor(scratch_pool[0:1, col:col + 1], scratch_pool[0:1, 2:3],
                                            scratch_pool[0:1, 2:3], ALU.add)

            g = Signals(pool_done)
            lns = Signals(rstd_ready)

            def inverse_std(rows=P, n=TILES, at=0):
                ln = lnstat[0:rows, at:at + n]
                var, y, w, t = (ln[:, :, k:k + 1] for k in range(1, 5))

                def step(ins):
                    g.on(ins)
                    pool.wait_ge(pool_done, g.now())

                lns.k += 1
                pool.wait_ge(var_ready, lns.now())
                eps, minus_half, three_halves = (misc[0:rows, M_NEWTON + k:M_NEWTON + k + 1].unsqueeze(1).broadcast_to(
                    [rows, n, 1]) for k in range(3))
                step(nc.gpsimd.tensor_tensor(w, var, eps, ALU.add))
                settle(lns.now(), 0)
                g.on(nc.gpsimd.tensor_scalar(y.bitcast(U32), w.bitcast(U32), -0.5, 1597463007.0, ALU.mult, ALU.add))
                pool.wait_ge(pool_done, g.now())
                step(nc.gpsimd.tensor_tensor(w, w, minus_half, ALU.mult))
                for k in range(3):
                    step(nc.gpsimd.tensor_tensor(t, y, y, ALU.mult))
                    step(nc.gpsimd.tensor_tensor(t, t, w, ALU.mult))
                    step(nc.gpsimd.tensor_tensor(t, t, three_halves, ALU.add))
                    ins = nc.gpsimd.tensor_tensor(y, y, t, ALU.mult)
                    step(ins) if k < 2 else ins.then_inc(rstd_ready, 1)

            nc.gpsimd.memset(scratch_pool[:], 0.0).then_inc(pool_done, 1)
            g.k += 1
            pool.wait_ge(pool_done, 1)
            nc.gpsimd.memset(logit0[:], 0.0)
            nc.gpsimd.memset(h_all[:, :, 2], 0.0).then_inc(zeroed, 1)

            inverse_std(1, 1)
            for _ in range(2):
                inverse_std(P, 8)
            staged(pool, 0, IMAGES - 1, lambda i, par: inverse_std(), ((g, PER_STD), (lns, 2)))

            def fetch_slots(e, par):
                after(pool, xt_ready, e - 1)
                g.on(nc.gpsimd.tensor_copy(src_now[par][0:CAPP], slot_src[0:CAPP, ds(e * 3, 3)]))
                pool.wait_ge(pool_done, g.now())
                settle(e, 0)
                for q in range(3):
                    nc.gpsimd.indirect_dma_start(slot_rows[par][0:CAPP, q], None, n2_rows,
                                                 bass.IndirectOffsetOnAxis(ap=src_now[par][0:CAPP, q:q + 1], axis=0))\
                        .then_inc(xs_loaded[par], 16)

            pool.wait_ge(slots_ready, 1)
            pool.wait_ge(n2_stored, 32 * IMAGES)
            fetch_slots(0, 0)
            fetch_slots(1, 1)
            staged(pool, 2, EXP0 - 1, fetch_slots, ((g, 2),))
            for par in range(2):
                pool.wait_ge(eo_stored[par], 16 * EXP0 // 2)
            def fetch_rows(i, par):
                after(pool, h2_done, i - 1)
                g.on(nc.gpsimd.tensor_copy(from_now[par][:], slot_from[:, ds(i * TILES, TILES)]))
                pool.wait_ge(pool_done, g.now())
                settle(i, 0)
                for q in range(TILES):
                    k = max(2, ROWS[q])
                    nc.gpsimd.indirect_dma_start(fetched[par][0:k, q], None, outs0,
                                                 bass.IndirectOffsetOnAxis(ap=from_now[par][0:k, q:q + 1], axis=0))\
                        .then_inc(fetched_in[par], 16)

            def stage(n, par, a=True, b=True, ahead=True):
                if ahead:
                    inverse_std(at=4)
                if b:
                    inverse_std()
                if a:
                    fetch_rows(n + 3, 1 - par)

            fetch_rows(0, 0)
            inverse_std(at=4)
            fetch_rows(1, 1)
            fetch_rows(2, 0)
            stage(0, 0, b=False)
            stage(1, 1)
            stage(2, 0)
            staged(pool, 3, 4, stage, ((g, PER_STD4), (lns, 4)))
            stage(5, 1, a=False)
            stage(6, 0, a=False)
            stage(7, 1, a=False, ahead=False)
            stage(8, 0, a=False, ahead=False)

            def number(t, par):
                pool.wait_ge(hots_ready, t + 1)
                nc.gpsimd.tensor_tensor(tile_hot[par], tile_hot[par], row_no[:, :, ds(t, 1)].broadcast_to([P, TOPK, NT1]),
                                        ALU.mult).then_inc(numbered, 1)

            for r in range(4):
                number(r, r)
            fours(pool, number)
            number(T1 - 1, 0)
            pool.wait_ge(idx_ready, 1)
            pool.wait_ge(n4_stored, 32 * IMAGES)

            def fetch(j, r):
                after(pool, x_turned, j - (XR - 1))
                after(pool, y_sent[r % 4], 4 * (j - r % 4) - 4 * IDX + 16)
                nc.gpsimd.tensor_copy(idx_now[r][:], rec_idx[:, ds(j, 1)].rearrange("p j w -> p (j w)")).then_inc(idx_copied, 1)
                pool.wait_ge(idx_copied, j + 1)
                settle(j, 0)
                nc.gpsimd.indirect_dma_start(xg[r % XR], None, n4_rows, bass.IndirectOffsetOnAxis(ap=idx_now[r][:, 0:1], axis=0))\
                    .then_inc(xg_in[r % XR], 16)

            def send(j, r):
                pool.wait_ge(y_done, j + 1)
                settle(j, 1)
                nc.gpsimd.indirect_dma_start(outs1, bass.IndirectOffsetOnAxis(ap=idx_now[r][:, 1:2], axis=0), y1[r % 4], None,
                                             bounds_check=TOPK * TOKENS - 1, oob_is_err=False).then_inc(y_sent[r % 4], 16)

            for j in range(IDX):
                if j >= LAG:
                    send(j - LAG, j - LAG)
                fetch(j, j)
            with pool.Fori(1, NT1 // IDX) as p:
                for r in range(IDX):
                    send(IDX * p + (r - LAG), (r - LAG) % IDX)
                    fetch(IDX * p + r, r)
            for j in range(NT1 - LAG, NT1):
                send(j, j % IDX)

            def sum_last(i, r):
                pool.wait_ge(last_scaled, i + 1)
                row = lambda k: ysum[r][0:1, k, 2]
                g.on(nc.gpsimd.tensor_tensor(row(0), row(0), row(1), ALU.add))
                g.on(nc.gpsimd.tensor_tensor(row(2), row(2), row(3), ALU.add))
                pool.wait_ge(pool_done, g.now())
                nc.gpsimd.tensor_tensor(row(0), row(0), row(2), ALU.add).then_inc(last_done, 1)

            with pool.Fori(0, IMAGES // 4) as p:
                with g.loop(p, IMAGES // 4, 8):
                    for r in range(4):
                        sum_last(4 * p + r, r)

        @block.scalar
        def _(act):
            s = Signals(act_done)

            act.wait_ge(ld_const, 32)
            act.wait_ge(turned, 1)
            for h in range(HALVES):
                ins = nc.scalar.activation(nT0[:, h, :].rearrange("p (i t) -> p i t", t=LEN)[:, :, 0],
                                           bank[1][:, h:h + 1].broadcast_to([P, IMAGES]), ACT.Copy)
                ins.then_inc(turned_out, 1)
            act.wait_ge(logit_ready, 1)
            nc.scalar.activation(gl[:, 1], gl[:, 0], ACT.Exp).then_inc(exp_ready, 1)
            for c in range(CH):
                act.wait_ge(fold_done, c + 1)
                nc.scalar.activation(w_fold[:, c], bank[2 + c % 2][:, :], ACT.Copy).then_inc(fold_out, 1)
            for g in range(2):
                for n in range(4):
                    h, jj = n // 2, 4 * (n % 2)
                    act.wait_ge(turned, 1 + 4 * g + n + 1)
                    dst = nT0[:, h, :].rearrange("p (i t) -> p i t", t=LEN)[:, 4 * g:4 * g + 4, 1:LEN]
                    dst = dst.rearrange("p i (r j) -> p j i r", j=8)[:, jj:jj + 4]
                    nc.scalar.activation(dst, bank[4 + n % 4][:, :].rearrange("p (j i r) -> p j i r", j=4, i=4),
                                         ACT.Copy).then_inc(turned_out, 1)
            if phases == 1:
                return
            act.wait_ge(ld_mix, 7 * 16)
            act.wait_ge(rows_stored, 16 * 16)
            act.wait_ge(bc_ready, 1)

            def tap(n, c):
                act.wait_ge(x_ready, 4 * n + (c + 1))
                nc.scalar.activation(conv[:, c], bank[c][:, 0:LEN], ACT.Identity, bias=chan[:, c, 4:5],
                                     scale=chan[:, c, 3:4]).then_inc(tap_done, 1)

            def gate_silus(n, par, tiles):
                after(act, y_ready, n - 1)
                for c in tiles:
                    act.wait_ge(z_ready, 4 * n + (c + 1))
                    ins = nc.scalar.activation(zs[par][:, c], bank[4 + c][:, 0:LEN], ACT.Silu)
                    s.on(ins) if c < CH - 1 else ins.then_inc(zs_done, 1)

            def conv_silu(n, par):
                act.wait_ge(conv_done, 2 * n + 2)
                nc.scalar.activation(xconv[par], conv, ACT.Silu).then_inc(xconv_ready, 1)

            def out_rows(i):
                for h in range(HALVES):
                    act.wait_ge(out_ready, 2 * i + (h + 1))
                    if h == 0:
                        after(act, tok_ready, i)
                    ins = nc.scalar.activation(outT[:, h], bank[h][:, 0:LEN], ACT.Copy)
                    s.on(ins) if h == 0 else ins.then_inc(outT_done, 1)

            def steps(n, par):
                act.wait_ge(bcsum_ready, n + 1)
                for b in range(2):
                    ins = nc.scalar.activation(bct[par][:, b], bank[4 + b][:, 0:LEN], ACT.Tanh, scale=0.5 / STATE)
                    s.on(ins) if b == 0 else ins.then_inc(bct_done, 1)
                after(act, dt_done, n)
                for k, c in enumerate(DT_ORDER):
                    act.wait_ge(dt_ready, 4 * n + (k + 1))
                    nc.scalar.activation(xb[:, c], bank[(6 + c) % 8][:, 0:LEN], ACT.Identity,
                                         bias=chan[:, c, 5:6]).then_inc(xb_done, 1)

            def log_sigmoid(i, part):
                if part == 0:
                    act.wait_ge(xb_done, 4 * i + 4)
                    s.on(nc.scalar.activation(soft, xb, ACT.Tanh, scale=0.5))
                    return
                act.wait_ge(act_done, s.now())
                if part == 1:
                    s.on(nc.scalar.activation(soft, soft, ACT.Abs))
                else:
                    nc.scalar.activation(soft, soft, ACT.Ln, bias=misc[:, M_HALF:M_HALF + 1], scale=0.5).then_inc(soft_ready, 1)

            def decay(i, par):
                act.wait_ge(dt_done, i + 1)
                after(act, y_ready, i - 1)
                nc.scalar.activation(es[par], dts, ACT.Tanh, scale=0.05).then_inc(e_done, 1)

            def norm_out(i, turned_sem, done, dst):
                act.wait_ge(turned_sem, i + 1)
                s.on(nc.scalar.activation(dst[:, :, 0:2 * P].rearrange("p h (q t) -> p q h t", q=2),
                                          bank[2][:, :].rearrange("p (q h t) -> p q h t", q=2, h=2), ACT.Copy))
                nc.scalar.activation(dst[:, :, 2 * P:LEN], bank[3][:, 256:258].unsqueeze(2), ACT.Copy).then_inc(done, 1)

            def stage(n, par, a=True, b=True, c=True, d=True):
                if a:
                    tap(n, 0)
                    tap(n, 1)
                if d:
                    norm_out(n - 3, n2_turned, n2T_done, n2T)
                if b:
                    log_sigmoid(n - 1, 0)
                if a:
                    tap(n, 2)
                if b:
                    log_sigmoid(n - 1, 1)
                if a:
                    tap(n, 3)
                if b:
                    log_sigmoid(n - 1, 2)
                if a:
                    gate_silus(n, par, (0,))
                if b:
                    decay(n - 1, 1 - par)
                if a:
                    gate_silus(n, par, (1, 2, 3))
                    conv_silu(n, par)
                if c:
                    out_rows(n - 2)
                if a:
                    steps(n, par)

            stage(0, 0, b=False, c=False, d=False)
            stage(1, 1, c=False, d=False)
            stage(2, 0, d=False)
            staged(act, 3, 6, stage, ((s, PER_MIX_ACT),))
            stage(7, 1)
            stage(IMAGES, 0, a=False)
            stage(IMAGES + 1, 1, a=False, b=False)
            stage(IMAGES + 2, 0, a=False, b=False, c=False)

            act.wait_ge(shift_ready, 1)
            nc.scalar.activation(r_exp, r_exp, ACT.Exp).then_inc(exps_ready, 1)
            act.wait_ge(ld_b, 32)

            def expert(e, par):
                for m in range(DFF // P):
                    act.wait_ge(hid_ready, 8 * e + (m + 1))
                    nc.scalar.activation(hidden[par][:, m], bank[2 + m % 4][:, 0:CAP], ACT.Relu,
                                         bias=b1_cols[:, ds(e, 1), m]).then_inc(hid_done, 1)

            staged(act, 0, EXP0 - 1, expert)

            def turned_rows(i, ready, done, dst, b):
                act.wait_ge(ready, i + 1)
                s.on(nc.scalar.activation(dst[:, :, 0:2 * P].rearrange("p h (q t) -> p q h t", q=2),
                                          bank[b][:, :].rearrange("p (q h t) -> p q h t", q=2, h=2), ACT.Copy))
                nc.scalar.activation(dst[:, :, 2 * P:LEN], bank[b + 1][:, 256:258].unsqueeze(2), ACT.Copy).then_inc(done, 1)

            def exponents(i, par):
                after(act, pt_ready, 3 * i)
                after(act, h3_done, i)
                for q in range(TILES):
                    k = ROWS[q]
                    act.wait_ge(m_ready, 3 * i + (q + 1))
                    nc.scalar.activation(probs[0:k, q], bank[2 + q][0:k, 0:LEN], ACT.Exp, bias=soft_c[0:k, 3 + q:4 + q],
                                         scale=float(HEAD) ** -0.5, accum_out=soft_c[0:k, 6 + q:7 + q]).then_inc(p_ready, 1)

            def probs_out(i, par):
                after(act, o_ready, 2 * i)
                for q in range(TILES):
                    k = ROWS[q]
                    act.wait_ge(pt_ready, 3 * i + (q + 1))
                    nc.scalar.activation(probsT[0:k, q], bank[(5, 2, 3)[q]][0:k, 0:LEN], ACT.Copy).then_inc(pt_done, 1)

            def shared_silu(j, par):
                after(act, hs_done, 3 * j)
                for q in range(TILES):
                    k = ROWS[q]
                    act.wait_ge(gu_ready, 3 * j + (q + 1))
                    nc.scalar.activation(silu_g[0:k, q], bank[6 + q % 2][0:k, 0:DFE], ACT.Silu).then_inc(sg_done, 1)

            def gated_out(j, par):
                after(act, mm2_ready, j)
                for k in range(2):
                    act.wait_ge(ht_ready, 2 * j + (k + 1))
                    nc.scalar.activation(gatedT[0:DK, k], bank[7 - k][0:DK, 0:LEN], ACT.Copy).then_inc(ht_done, 1)

            def attended(i, par):
                after(act, tokens_ready, i)
                for h in range(HALVES):
                    act.wait_ge(o_ready, 2 * i + (h + 1))
                    ins = nc.scalar.activation(outT[:, h], bank[4 + h][:, 0:LEN], ACT.Copy)
                    s.on(ins) if h == 0 else ins.then_inc(oT_done, 1)

            def norm_rows(j):
                after(act, gu_ready, 3 * j)
                turned_rows(j, n4_turned, n4T_done, n4T, 6)
                act.wait_ge(n4T_done, j + 1)
                s.on(nc.scalar.activation(n4T_last[:, :, ds(j, 1)], n4T[:, :, 2 * P:LEN], ACT.Copy))

            def stage(n, par, a=True, b=True, c=True, ahead=True):
                if a:
                    after(act, qk_ready, 4 * n)
                    after(act, v_ready, n)
                    turned_rows(n, n3_turned, n3T_done, n3T, 0)
                if b:
                    exponents(n - 1, 1 - par)
                if c:
                    norm_rows(n - 2)
                if c:
                    shared_silu(n - 2, par)
                if b:
                    probs_out(n - 1, 1 - par)
                if c:
                    gated_out(n - 2, par)
                if b:
                    attended(n - 1, 1 - par)

            stage(0, 0, b=False, c=False)
            stage(1, 1, c=False)
            stage(2, 0)
            staged(act, 3, 6, stage, ((s, PER_ATT_ACT),))
            stage(7, 1, ahead=False)
            stage(8, 0, a=False, ahead=False)
            norm_rows(IMAGES - 1)
            nc.scalar.activation(gl8[:], n4T_last[:, 0, 0:1], ACT.Copy).then_inc(last_cols, 1)
            act.wait_ge(sg_shift, 1)
            nc.scalar.activation(score, score, ACT.Exp).then_inc(sg_exp, 1)
            shared_silu(IMAGES - 1, 1)
            gated_out(IMAGES - 1, 1)

            def x_out(j, par):
                act.wait_ge(x_turned, j + 1)
                nc.scalar.activation(xT1[par], bank[par][:, 0:2 * P].rearrange("p (h t) -> p h t", h=HALVES),
                                     ACT.Copy).then_inc(xT_done, 1)

            def silu(j, par):
                act.wait_ge(gu1_ready, j + 1)
                after(act, g1_done, j - 1)
                nc.scalar.activation(sg1[par], bank[2 + par][:, 0:DFE], ACT.Silu).then_inc(sg1_done, 1)

            def gated1_out(j, par):
                act.wait_ge(g1_turned, j + 1)
                nc.scalar.activation(gT1[par][0:DK], bank[4 + par][0:DK, 0:2 * P].rearrange("p (k t) -> p k t", k=2),
                                     ACT.Copy).then_inc(gT_done, 1)

            def tile(j, par, ahead=True, now=True, late=True):
                if ahead:
                    x_out(j + 1, 1 - par)
                if now:
                    silu(j, par)
                if late:
                    gated1_out(j - 1, 1 - par)

            x_out(0, 0)
            tile(0, 0, late=False)
            tile(1, 1)
            tile(2, 0)
            staged(act, 3, NT1 - 2, tile)
            tile(NT1 - 1, 1, ahead=False)
            tile(NT1, 0, ahead=False, now=False)

            def weigh_last(i, r):
                act.wait_ge(ys_in[r], 12 * (i + (4 - r)))
                for k in range(TOPK):
                    row = ysum[r][0:1, k, 2]
                    ins = nc.scalar.activation(row, row, ACT.Identity, scale=last_w[0:1, ds(TOPK * i + k, 1)])
                    s.on(ins) if k < TOPK - 1 else ins.then_inc(last_scaled, 1)

            act.wait_ge(last_w_in, 16)
            with act.Fori(0, IMAGES // 4) as p:
                with s.loop(p, IMAGES // 4, 12):
                    for r in range(4):
                        weigh_last(4 * p + r, r)

        @block.tensor
        def _(pe):
            pe.wait_ge(ld_const, 32)
            pe.wait_ge(normed_ready, 1)
            for h in range(HALVES):
                mm = nc.tensor.transpose(bank[1][:, h:h + 1], cls[0:1, HID + h * P:HID + (h + 1) * P], ident[0:1, 0:1])
            mm.then_inc(turned, 1)
            pe.wait_ge(dots_ready, 1)
            nc.tensor.matmul(bank[0][:, 0:20], same_image, partial.rearrange("p g n -> p (g n)"),
                             start=True, stop=True).then_inc(sums_ready, 1)
            pe.wait_ge(ld_mix, 7 * 16)
            for c in range(CH):
                if c >= 2:
                    pe.wait_ge(fold_out, c - 1)
                for k in range(CH):
                    mm = nc.tensor.matmul(bank[2 + c % 2][:, :], w_xdt[:, k, c * P:(c + 1) * P], w_dt[:, k],
                                          start=(k == 0), stop=(k == CH - 1))
                mm.then_inc(fold_done, 1)
            for g in range(2):
                pe.wait_ge(normed_ready, 1 + g + 1)
                for n in range(4):
                    h, jj = n // 2, 4 * (n % 2)
                    if g:
                        pe.wait_ge(turned_out, 2 + n + 1)
                    for j in range(4):
                        mm = nc.tensor.transpose(bank[4 + n][:, j * P:(j + 1) * P], normed[:, jj + j, h * P:(h + 1) * P], ident)
                    mm.then_inc(turned, 1)
            if phases == 1:
                return
            pe.wait_ge(fold_out, CH)
            pe.wait_ge(turned_out, 10)
            pe.wait_ge(bc_ready, 1)

            def dense(out, weights, moving, last=None):
                for k in range(len(weights)):
                    mm = nc.tensor.matmul(out, weights[k], moving[k], start=(k == 0), stop=(k == len(weights) - 1))
                return mm

            def project(n, b):
                x = [nT0[:, h, ds(n * LEN, LEN)] for h in range(HALVES)]
                dense(bank[b][:, 0:LEN], [w_in[:, h, b * P:(b + 1) * P] for h in range(HALVES)], x)\
                    .then_inc(x_ready if b < CH else z_ready, 1)

            def out_rows(i, par, conv_count):
                pe.wait_ge(conv_done, conv_count)
                pe.wait_ge(y_ready, i + 1)
                for h in range(HALVES):
                    dense(bank[h][:, 0:LEN], [w_out[:, c, h * P:(h + 1) * P] for c in range(CH)],
                          [ys[par][:, c] for c in range(CH)]).then_inc(out_ready, 1)

            def turn_rows(src, done):
                for q in range(TILES):
                    for h in range(HALVES):
                        o = bank[2][:, q * HID + h * P:q * HID + (h + 1) * P] if q < 2 else bank[3][0:1, h * P:(h + 1) * P]
                        mm = nc.tensor.transpose(o, src[:, h, q * P:q * P + ROWS[q]], ident)
                mm.then_inc(done, 1)

            def turn_norm(i, ready, done):
                pe.wait_ge(ready, i + 1)
                for q in range(TILES):
                    for h in range(HALVES):
                        k = ROWS[q]
                        o = bank[2][:, (q * 2 + h) * P:(q * 2 + h + 1) * P] if q < 2 else bank[3][:, 256 + h:257 + h]
                        src = turn_src[0:k, q, h * P:(h + 1) * P]
                        mm = nc.tensor.transpose(o, src, ident[0:k, 0:k])
                mm.then_inc(done, 1)

            def gate_sums(n, par):
                pe.wait_ge(xconv_ready, n + 1)
                pe.wait_ge(zs_done, n + 1)
                for b in range(2):
                    mm = dense(bank[4 + b][:, 0:LEN], [w_bcr[:, b, c] for c in range(CH)],
                               [xconv[par][:, c] for c in range(CH)])
                mm.then_inc(bcsum_ready, 1)

            def steps(n, par):
                after(pe, outT_done, n - 1)
                for c in DT_ORDER:
                    dense(bank[(6 + c) % 8][:, 0:LEN], [w_fold[:, k, c * P:(c + 1) * P] for k in range(CH)],
                          [xconv[par][:, k] for k in range(CH)]).then_inc(dt_ready, 1)

            def logits(i, done, wg, nT, n_exp, out):
                pe.wait_ge(done, i + 1)
                for q in range(TILES):
                    k = ROWS[q]
                    mm = dense(bank[3][0:k, 300 + q * n_exp:300 + (q + 1) * n_exp],
                               [nT[:, h, q * P:q * P + k] for h in range(HALVES)], [wg[:, h] for h in range(HALVES)])
                mm.then_inc(out, 1)

            def stage(n, par, a=True, b=True, c=True, d=True):
                if a:
                    for b_ in range(2):
                        after(pe, xb_done, 4 * n + (b_ - 3))
                        project(n, b_)
                if d:
                    turn_norm(n - 3, n2_ready, n2_turned)
                if a:
                    after(pe, bct_done, n)
                    project(n, 4)
                if d:
                    logits(n - 3, n2T_done, wg0, n2T, EXP0, log_ready)
                if a:
                    project(n, 2)
                    after(pe, log_saved, n - 2)
                    project(n, 3)
                    project(n, 5)
                    after(pe, xb_done, 4 * n)
                    project(n, 6)
                    project(n, 7)
                if c:
                    out_rows(n - 2, par, 2 * n + 1 if a else 2 * IMAGES)
                if a:
                    gate_sums(n, par)
                if c:
                    pe.wait_ge(outT_done, n - 1)
                    after(pe, log_saved, n - 2)
                    turn_rows(outT, tok_ready)
                if a:
                    steps(n, par)

            stage(0, 0, b=False, c=False, d=False)
            stage(1, 1, c=False, d=False)
            stage(2, 0, d=False)
            staged(pe, 3, 6, stage)
            stage(7, 1)
            stage(IMAGES, 0, a=False)
            stage(IMAGES + 1, 1, a=False, b=False)
            stage(IMAGES + 2, 0, a=False, b=False, c=False)

            pe.wait_ge(hot_ready, 1)
            flat = lambda a: a.rearrange("p t e -> p (t e)")
            dense(bank[0][:, 0:IMAGES * TILES * EXP0], [before, ones], [flat(r_hot), flat(r_tmp)]).then_inc(pos_ready, 1)

            pe.wait_ge(hots0_ready, 1)
            dense(bank[1][0:CAPP, 0:SLOT_TILES], [lane_hot0[:, t] for t in range(IMAGES * TILES)],
                  [tile_hot0[:, t] for t in range(IMAGES * TILES)]).then_inc(table0_ready, 1)

            def turn_slots(e, par):
                pe.wait_ge(xs_loaded[par], 24 * (e + (2 - par)))
                after(pe, xt_done, e)
                for h in range(HALVES):
                    for q in range(3):
                        mm = nc.tensor.transpose(bank[h][:, q * CAPP:(q + 1) * CAPP],
                                                 slot_rows[par][0:CAPP, q, h * P:(h + 1) * P], ident[0:CAPP, 0:CAPP])
                mm.then_inc(xt_ready, 1)

            def expert(e, par, more=True):
                pe.wait_ge(w_loaded[par], 16 * (e + (2 - par)))
                pe.wait_ge(xt_done, e + 1)
                x = [slotT[par][:, h] for h in range(HALVES)]
                for m in range(DFF // P):
                    after(pe, hid_done, 8 * e + (m - 3))
                    dense(bank[2 + m % 4][:, 0:CAP], [w1e[par][:, h, m * P:(m + 1) * P] for h in range(HALVES)],
                          x).then_inc(hid_ready, 1)
                if more:
                    turn_slots(e + 1, 1 - par)
                pe.wait_ge(hid_done, 8 * e + 8)
                after(pe, eo_done, e)
                for q in range(3):
                    o = bank[6][0:CAPP, q * HID:(q + 1) * HID] if q < 2 else bank[7][0:CAPP, 0:HID]
                    mm = dense(o, [hidden[par][:, m, q * CAPP:(q + 1) * CAPP] for m in range(DFF // P)],
                               [w2e[par][:, m] for m in range(DFF // P)])
                mm.then_inc(eo_ready, 1)

            pe.wait_ge(slots_ready, 1)
            turn_slots(0, 0)
            expert(0, 0)
            staged(pe, 1, 6, expert)
            expert(7, 1, more=False)

            def turn_rows_in(i, src, ready, done, b):
                pe.wait_ge(ready, i + 1)
                for q in range(TILES):
                    for h in range(HALVES):
                        k = ROWS[q]
                        o = bank[b][:, (q * 2 + h) * P:(q * 2 + h + 1) * P] if q < 2 else bank[b + 1][:, 256 + h:257 + h]
                        mm = nc.tensor.transpose(o, src[0:k, q, h * P:(h + 1) * P], ident[0:k, 0:k])
                mm.then_inc(done, 1)

            def tile_of(x, q):
                return x[:, q * P:q * P + ROWS[q]]

            def query_keys(n, quarters):
                for g in quarters:
                    if g >= 2:
                        pe.wait_ge(qk_done, 4 * n + (g - 1))
                    dense(bank[g % 2][:, 0:LEN], [w_qk[:, h, g * P:(g + 1) * P] for h in range(HALVES)],
                          [n3T[:, h] for h in range(HALVES)]).then_inc(qk_ready, 1)

            def router(j):
                pe.wait_ge(n4T_done, j + 1)
                for q in range(2):
                    k = ROWS[q]
                    mm = dense(bank[7][0:k, 300 + q * EXP1:300 + (q + 1) * EXP1],
                               [tile_of(n4T[:, h], q) for h in range(HALVES)], [wg1[:, h] for h in range(HALVES)])
                mm.then_inc(lg1_ready, 1)

            def shared_up(j):
                for q in range(TILES):
                    k = ROWS[q]
                    if q == 1:
                        pe.wait_ge(lg1_saved, j + 1)
                    if q == 2:
                        pe.wait_ge(hs_done, 3 * j + 1)
                    dense(bank[6 + q % 2][0:k, 0:2 * DFE], [tile_of(n4T[:, h], q) for h in range(HALVES)],
                          [ws13[:, h] for h in range(HALVES)]).then_inc(gu_ready, 1)

            def shared_turn(j):
                pe.wait_ge(hs_done, 3 * j + 3)
                for k in range(2):
                    for q in range(TILES):
                        mm = nc.tensor.transpose(bank[7 - k][0:DK, q * P:q * P + ROWS[q]],
                                                 gated[0:ROWS[q], q, k * DK:(k + 1) * DK], ident[0:ROWS[q], 0:ROWS[q]])
                    mm.then_inc(ht_ready, 1)

            def shared_down(j):
                pe.wait_ge(ht_done, 2 * j + 2)
                for q in range(TILES):
                    mm = dense(bank[6][:, q * HID:(q + 1) * HID] if q < 2 else bank[7][0:1, 0:HID],
                               [tile_of(gatedT[0:DK, k], q) for k in range(2)], [ws2[0:DK, k] for k in range(2)])
                mm.then_inc(mm2_ready, 1)

            def stage(n, par, a=True, b=True, c=True, ahead=True):
                i, j = n - 1, n - 2
                if a:
                    after(pe, v_done, n)
                    turn_rows_in(n, turn_src, n3_ready, n3_turned, 0)
                if b:
                    pe.wait_ge(qk_done, 4 * i + 4)
                    after(pe, h3_done, i)
                    after(pe, oT_done, i)
                    for q in range(TILES):
                        dense(bank[2 + q][0:ROWS[q], 0:LEN], [tile_of(qkT[:, h], q) for h in range(HALVES)],
                              [qkT[:, HALVES + h] for h in range(HALVES)]).then_inc(s_ready, 1)
                if a:
                    pe.wait_ge(n3T_done, n + 1)
                    query_keys(n, (0, 1))
                if c:
                    after(pe, acc_done, j)
                    turn_rows_in(j, turn_src4, n4_ready, n4_turned, 6)
                if a:
                    query_keys(n, (2, 3))
                if c:
                    router(j)
                    shared_up(j)
                if b:
                    pe.wait_ge(p_ready, 3 * i + 3)
                    for kt in range(TILES):
                        for q in range(TILES):
                            mm = nc.tensor.transpose(bank[(5, 2, 3)[kt]][0:ROWS[kt], q * P:q * P + ROWS[q]],
                                                     tile_of(probs[0:ROWS[q], q], kt), ident[0:ROWS[q], 0:ROWS[q]])
                        mm.then_inc(pt_ready, 1)
                if a:
                    pe.wait_ge(qk_done, 4 * n + 4)
                    for q in range(TILES):
                        k = ROWS[q]
                        mm = dense(bank[0][:, q * HID:(q + 1) * HID] if q < 2 else bank[1][0:1, 0:HID],
                                   [tile_of(n3T[:, h], q) for h in range(HALVES)], [w_v[:, h] for h in range(HALVES)])
                    mm.then_inc(v_ready, 1)
                if c:
                    shared_turn(j)
                if b:
                    pe.wait_ge(pt_done, 3 * i + 3)
                    pe.wait_ge(v_done, i + 1)
                    for h in range(HALVES):
                        dense(bank[4 + h][:, 0:LEN],
                              [vals[1 - par][0:ROWS[kt], kt, h * P:(h + 1) * P] for kt in range(TILES)],
                              [probsT[0:ROWS[kt], kt] for kt in range(TILES)]).then_inc(o_ready, 1)
                if c:
                    shared_down(j)
                if b:
                    pe.wait_ge(oT_done, i + 1)
                    turn_rows(outT, tokens_ready)

            pe.wait_ge(w_qk_ready, 1)
            stage(0, 0, b=False, c=False)
            stage(1, 1, c=False)
            pe.wait_ge(ld_shared, 48)
            stage(2, 0)
            staged(pe, 3, 6, stage)
            stage(7, 1)
            stage(8, 0, a=False)
            pe.wait_ge(acc_done, IMAGES - 1)
            turn_rows_in(IMAGES - 1, turn_src4, n4_ready, n4_turned, 6)
            router(IMAGES - 1)

            pe.wait_ge(last_cols, 1)
            dense(bank[0][0:IMAGES, 0:EXP1], [n4T_last[:, h] for h in range(HALVES)],
                  [wg1[:, h] for h in range(HALVES)]).then_inc(last_lg, 1)
            shared_up(IMAGES - 1)
            shared_turn(IMAGES - 1)
            shared_down(IMAGES - 1)
            pe.wait_ge(ranks_in, 1)
            dense(bank[1][:, 0:EXP1], [ones], [per_exp[:, 0]]).then_inc(cnt_ready, 1)
            dense(bank[0][:, 0:T1 * EXP1], [before, ones], [flat(sel), flat(cumB)]).then_inc(rank_ready, 1)

            def slot_table(t, par, first=False, last=False):
                rows_ = IMAGES if last else P
                pe.wait_ge(numbered, t + 1)
                for k in range(TOPK):
                    mm = nc.tensor.matmul(bank[2][:, 0:NT1], lane_hot[par][0:rows_, k], tile_hot[par][0:rows_, k],
                                          start=first and k == 0, stop=last and k == TOPK - 1)
                mm.then_inc(hots_used, 1)

            for r in range(4):
                slot_table(r, r, first=r == 0)
            fours(pe, slot_table)
            slot_table(T1 - 1, 0, last=True)

            def turn_x(j, par, r):
                pe.wait_ge(xg_in[r], 16 // XR * (j + (XR - r)))
                after(pe, xT_done, j - 1)
                for h in range(HALVES):
                    mm = nc.tensor.transpose(bank[par][:, h * P:(h + 1) * P], xg[r][:, h * P:(h + 1) * P], ident)
                mm.then_inc(x_turned, 1)

            def expert_of(j):
                return pe.value_load(tile_exp[0:1, ds(j, 1)], min_val=0, max_val=EXP1 - 1)

            def gate_up(j, par):
                e = expert_of(j)
                pe.wait_ge(xT_done, j + 1)
                after(pe, g1_done, j - 1)
                dense(bank[2 + par][:, 0:2 * DFE], [xT1[par][:, h] for h in range(HALVES)],
                      [w13[:, ds(e, 1), h].rearrange("p e n -> p (e n)") for h in range(HALVES)]).then_inc(gu1_ready, 1)

            def turn_gated(j, par):
                pe.wait_ge(g1_done, j + 1)
                after(pe, gT_done, j - 1)
                for k in range(2):
                    mm = nc.tensor.transpose(bank[4 + par][0:DK, k * P:(k + 1) * P], gu1[par][:, k * DK:(k + 1) * DK], ident)
                mm.then_inc(g1_turned, 1)

            def down(j, par):
                e = expert_of(j)
                pe.wait_ge(gT_done, j + 1)
                after(pe, y_done, j - 1)
                dense(bank[6 + par][:, 0:HID], [gT1[par][0:DK, k] for k in range(2)],
                      [w2s[0:DK, ds(e, 1), k].rearrange("p e n -> p (e n)") for k in range(2)]).then_inc(y_ready2, 1)

            def tile(j, r, ahead=True, now=True, late=True, last=True):
                par = r % 2
                if ahead:
                    turn_x(j + 1, 1 - par, (r + 1) % XR)
                if now:
                    gate_up(j, par)
                if late:
                    turn_gated(j - 1, 1 - par)
                if last:
                    down(j - 2, par)

            pe.wait_ge(idx_ready, 1)
            turn_x(0, 0, 0)
            tile(0, 0, late=False, last=False)
            tile(1, 1, last=False)
            for j in range(2, XR):
                tile(j, j)
            with pe.Fori(1, NT1 // XR - 1) as p:
                for r in range(XR):
                    tile(XR * p + r, r)
            for j in range(NT1 - XR, NT1 - 1):
                tile(j, j % XR)
            tile(NT1 - 1, XR - 1, ahead=False)
            tile(NT1, 0, ahead=False, now=False)
            tile(NT1 + 1, 1, ahead=False, now=False, late=False)
    return nc


def rows_on_partitions(w):
    k, n = w.shape
    return w.reshape(k // P, P, n).transpose(1, 0, 2)


def lay_out(a):
    o = dict(constants())
    o["x"] = a["x"].reshape(IMAGES, SIDE, SIDE)
    o["cls_tok"] = a["cls_tok"].reshape(1, HID)
    for n in ("Wa", "Wd1", "Wd2", "Wd3"):
        o[n] = a["L0_tok_" + n]
    o["gbias"] = np.concatenate([a["L0_tok_" + n] for n in ("ba", "bd1", "bd2", "bd3")])
    wx = a["L0_attn_W_x"]
    o["w_in"] = rows_on_partitions(a["L0_attn_W_in"].T)
    o["w_dt"] = rows_on_partitions(a["L0_attn_W_dt"].T)
    o["w_xdt"] = rows_on_partitions(wx[2 * STATE:])
    o["w_bc"] = rows_on_partitions(wx[:2 * STATE].T)
    o["w_out"] = rows_on_partitions(a["L0_attn_W_out"].T)
    chan = np.concatenate([a["L0_attn_conv_w"][:, 0, :], a["L0_attn_conv_b"][:, None], a["L0_attn_b_dt"][:, None],
                           a["L0_attn_D"][:, None], a["L0_attn_D"][:, None]], 1)
    o["chan"] = rows_on_partitions(chan)
    o["w1"] = a["L0_ffn_w1"].reshape(EXP0, HALVES, P, DFF).transpose(0, 2, 1, 3).reshape(EXP0, P, -1)
    o["w2"] = a["L0_ffn_w2"].reshape(EXP0, DFF // P, P, HID).transpose(0, 2, 1, 3).reshape(EXP0, P, -1)
    o["b1"] = a["L0_ffn_b1"].reshape(EXP0, DFF // P, P).transpose(2, 0, 1)
    o["b2"] = a["L0_ffn_b2"].reshape(-1)
    wq, wk, bq, bk = (a["L1_attn_" + n] for n in ("Wq", "Wk", "bq", "bk"))
    o["w_qk"] = rows_on_partitions(np.concatenate([wq.T, wk.T], 1))
    bias = np.concatenate([bq, bk]).reshape(4, P)
    pair = bias.reshape(4, P // 2, 2)[:, :, ::-1].reshape(4, P)
    sign = np.broadcast_to(np.tile(np.array([-1, 1], np.float32), P // 2), (4, P))
    o["qk_bias"] = np.concatenate([bias, pair, sign]).T
    o["w_v"] = rows_on_partitions(a["L1_attn_Wv"].T)
    o["bv"] = a["L1_attn_bv"]
    o["wg1"] = rows_on_partitions(a["L1_ffn_gate_w"].T)
    o["ws13"] = rows_on_partitions(np.concatenate([a["L1_ffn_ws1"].T, a["L1_ffn_ws3"].T], 1))
    o["ws2"] = a["L1_ffn_ws2"].T.reshape(2, DK, HID).transpose(1, 0, 2)
    o["gate_bias"] = a["L1_ffn_gate_bias"]
    w13 = np.concatenate([a["L1_ffn_w1"], a["L1_ffn_w3"]], 1)
    o["w13"] = w13.transpose(2, 0, 1).reshape(HALVES, P, EXP1, 2 * DFE).transpose(1, 2, 0, 3).reshape(P, -1)
    w2 = a["L1_ffn_w2"].transpose(2, 0, 1).reshape(2, DK, EXP1, HID)
    o["w2s"] = w2.transpose(1, 2, 0, 3).reshape(DK, -1)
    o["wg0"] = rows_on_partitions(a["L0_ffn_wg"])
    return {k: np.ascontiguousarray(v) for k, v in o.items()}


def kernel(**inputs):
    import concourse.bacc as bacc
    from concourse.bass_utils import run_bass_kernel_spmd

    nc = bacc.Bacc("TRN2", target_bir_lowering=False, num_devices=1)
    arrays = {f"in_{n}": v for n, v in lay_out({n: np.asarray(v) for n, v in inputs.items()}).items()}
    d = {n[3:]: nc.dram_tensor(n, v.shape, mybir.dt.from_np(v.dtype), kind="ExternalInput").ap()
         for n, v in arrays.items()}
    d["out"] = nc.dram_tensor("out", (TOKENS, HID), F32, kind="ExternalOutput").ap()
    build(nc, d)
    r = run_bass_kernel_spmd(nc, [arrays], core_ids=[0])
    return r.results[0]["out"].reshape(IMAGES, LEN, HID)
```
